# Optimizing a Trainium2 kernel written in Bass

```python
import numpy as np
import jax
import jax.numpy as jnp

def _softmax(x, axis=-1):
    return jax.nn.softmax(x, axis=axis)

def _gelu(x):
    return jax.nn.gelu(x, approximate=True)

def _silu(x):
    return jax.nn.silu(x)

def _sigmoid(x):
    return jax.nn.sigmoid(x)

def _layernorm(x, axis=-1, eps=1e-05):
    m = jnp.mean(x, axis=axis, keepdims=True)
    v = jnp.var(x, axis=axis, keepdims=True)
    return (x - m) / jnp.sqrt(v + eps)

def _scatter_add(tgt, idx, src, axis=0):
    return tgt.at[idx].add(src)

def _segment_sum(src, seg, n):
    return jax.ops.segment_sum(src, seg, n)
kernel_name = 'mk_gnn_preln_d2_gnn_r32_5e2086'

def setup_inputs(seed: int=0):
    np.random.seed(seed)
    _w = jnp.asarray

    def _rec_inputs():
        import jax
        import jax.numpy as jnp
        _gk = jax.random.key(seed)
        x = -0.000202 + 1 * jax.random.normal(jax.random.fold_in(_gk, 1), (3125, 128), jnp.float32)
        src = jax.random.randint(jax.random.fold_in(_gk, 2), (50000,), 0, 3125, jnp.int32)
        dst = jax.random.randint(jax.random.fold_in(_gk, 3), (50000,), 0, 3125, jnp.int32)
        _o = jnp.argsort(dst, stable=True)
        src = src[_o]
        dst = dst[_o]
        edge_attr_128 = 5.93493e-05 + 1.00006 * jax.random.normal(jax.random.fold_in(_gk, 13), (50000, 128), jnp.float32)
        return (x, src, dst, edge_attr_128)
    x, src, dst, edge_attr_128 = _rec_inputs()

    def _L0_gnn_setup():
        import jax, jax.numpy as jnp
        import numpy as np
        N_NODES = 50000
        N_EDGES = 25000
        ENC_DIM = 128

        def _sage_layer(h, edge_src, edge_dst, W, b):
            n = h.shape[0]
            msg_sum = jax.ops.segment_sum(h[edge_src], edge_dst, num_segments=n)
            deg = jax.ops.segment_sum(jnp.ones_like(edge_dst, dtype=h.dtype), edge_dst, num_segments=n)
            m = msg_sum / jnp.maximum(deg, 1.0)[:, None]
            hc = jnp.concatenate([h, m], axis=1)
            return jax.nn.relu(hc @ W + b)
        key = jax.random.key(seed)
        k_h, k_s, k_d, k_w1, k_w2 = jax.random.split(key, 5)
        h = jax.random.normal(k_h, (N_NODES, ENC_DIM), dtype=jnp.float32)
        edge_src = jax.random.randint(k_s, (N_EDGES,), 0, N_NODES, dtype=jnp.int32)
        edge_dst = jax.random.randint(k_d, (N_EDGES,), 0, N_NODES, dtype=jnp.int32)
        scale = 1.0 / np.sqrt(2 * ENC_DIM)
        W1 = jax.random.normal(k_w1, (2 * ENC_DIM, ENC_DIM), dtype=jnp.float32) * scale
        b1 = jnp.zeros((ENC_DIM,), dtype=jnp.float32)
        W2 = jax.random.normal(k_w2, (2 * ENC_DIM, ENC_DIM), dtype=jnp.float32) * scale
        b2 = jnp.zeros((ENC_DIM,), dtype=jnp.float32)
        return {'h': h, 'edge_src': edge_src, 'edge_dst': edge_dst, 'W1': W1, 'b1': b1, 'W2': W2, 'b2': b2}
    _L0_gnn_all = _L0_gnn_setup()
    _L0_gnn_in = {k: v for k, v in _L0_gnn_all.items() if k in ('W1', 'b1', 'W2', 'b2')}
    del _L0_gnn_all

    def _L1_gnn_setup():
        import jax, jax.numpy as jnp
        import numpy as np
        N_NODES = 3125
        N_EDGES = 18750
        D = 128
        HID = 512
        N_GRAPHS = 16
        MLP_IN = D + 3 * D + 1
        key = jax.random.key(seed)
        ks = jax.random.split(key, 9)
        x = jax.random.normal(ks[0], (N_NODES, D), dtype=jnp.float32)
        edge_index = jax.random.randint(ks[1], (2, N_EDGES), 0, N_NODES, dtype=jnp.int64)
        edge_attr = jax.random.normal(ks[2], (N_EDGES, D), dtype=jnp.float32)
        u = jax.random.normal(ks[3], (N_GRAPHS, 1), dtype=jnp.float32)
        batch = jnp.sort(jax.random.randint(ks[4], (N_NODES,), 0, N_GRAPHS, dtype=jnp.int64))
        s1 = 1.0 / np.sqrt(MLP_IN)
        s2 = 1.0 / np.sqrt(HID)
        W1 = jax.random.uniform(ks[5], (MLP_IN, HID), jnp.float32, -s1, s1)
        b1 = jax.random.uniform(ks[6], (HID,), jnp.float32, -s1, s1)
        W2 = jax.random.uniform(ks[7], (HID, D), jnp.float32, -s2, s2)
        b2 = jax.random.uniform(ks[8], (D,), jnp.float32, -s2, s2)
        return {'x': x, 'edge_index': edge_index, 'edge_attr': edge_attr, 'u': u, 'batch': batch, 'W1': W1, 'b1': b1, 'W2': W2, 'b2': b2}
    _L1_gnn_all = _L1_gnn_setup()
    _L1_gnn_in = {k: v for k, v in _L1_gnn_all.items() if k in ('u', 'W1', 'b1', 'W2', 'b2')}
    del _L1_gnn_all
    return {'x': x, 'src': src, 'dst': dst, 'edge_attr_128': edge_attr_128, 'L0_gnn_W1': _L0_gnn_in['W1'], 'L0_gnn_b1': _L0_gnn_in['b1'], 'L0_gnn_W2': _L0_gnn_in['W2'], 'L0_gnn_b2': _L0_gnn_in['b2'], 'L1_gnn_u': _L1_gnn_in['u'], 'L1_gnn_W1': _L1_gnn_in['W1'], 'L1_gnn_b1': _L1_gnn_in['b1'], 'L1_gnn_W2': _L1_gnn_in['W2'], 'L1_gnn_b2': _L1_gnn_in['b2']}

def reference(x, src, dst, edge_attr_128, L0_gnn_W1, L0_gnn_b1, L0_gnn_W2, L0_gnn_b2, L1_gnn_u, L1_gnn_W1, L1_gnn_b1, L1_gnn_W2, L1_gnn_b2):
    import jax
    import jax.numpy as jnp

    def _L0_gnn_ref(h, edge_src, edge_dst, W1, b1, W2, b2):
        import jax, jax.numpy as jnp
        import numpy as np
        N_NODES = 50000
        N_EDGES = 25000
        ENC_DIM = 128

        def _sage_layer(h, edge_src, edge_dst, W, b):
            n = h.shape[0]
            msg_sum = jax.ops.segment_sum(h[edge_src], edge_dst, num_segments=n)
            deg = jax.ops.segment_sum(jnp.ones_like(edge_dst, dtype=h.dtype), edge_dst, num_segments=n)
            m = msg_sum / jnp.maximum(deg, 1.0)[:, None]
            hc = jnp.concatenate([h, m], axis=1)
            return jax.nn.relu(hc @ W + b)
        h = _sage_layer(h, edge_src, edge_dst, W1, b1)
        h = _sage_layer(h, edge_src, edge_dst, W2, b2)
        return h

    def _L1_gnn_ref(x, edge_index, edge_attr, u, batch, W1, b1, W2, b2):
        import jax, jax.numpy as jnp
        import numpy as np
        N_NODES = 3125
        N_EDGES = 18750
        D = 128
        HID = 512
        N_GRAPHS = 16
        MLP_IN = D + 3 * D + 1
        N = x.shape[0]
        row = edge_index[0]
        ones = jnp.ones((edge_attr.shape[0], 1), dtype=edge_attr.dtype)
        cnt = jax.ops.segment_sum(ones, row, num_segments=N)
        agg_sum = jax.ops.segment_sum(edge_attr, row, num_segments=N)
        agg_max = jax.ops.segment_max(edge_attr, row, num_segments=N)
        agg_max = jnp.where(cnt > 0, agg_max, jnp.zeros((), edge_attr.dtype))
        agg_mean = agg_sum / jnp.maximum(cnt, 1.0)
        h = jnp.concatenate([x, agg_sum, agg_max, agg_mean, u[batch]], axis=1)
        h = jax.nn.relu(h @ W1 + b1) @ W2 + b2
        return h + x
    edge_index = jnp.stack([src, dst])
    batch0 = jnp.zeros((3125,), jnp.int32)
    h = jnp.maximum(_layernorm(x, axis=-1), 0.0)
    x = x + _L0_gnn_ref(h, src, dst, L0_gnn_W1, L0_gnn_b1, L0_gnn_W2, L0_gnn_b2)
    h = jnp.maximum(_layernorm(x, axis=-1), 0.0)
    x = x + _L1_gnn_ref(h, edge_index, edge_attr_128, L1_gnn_u, batch0, L1_gnn_W1, L1_gnn_b1, L1_gnn_W2, L1_gnn_b2)
    return x

_drawn_inputs = setup_inputs


def setup_inputs(seed=0):
    import zlib

    import numpy as np

    out = dict(_drawn_inputs(seed))
    spreads = {'L0_gnn_b1': (0.0, 0.1), 'L0_gnn_b2': (0.0, 0.1)}
    factors = {'L1_gnn_u': 8.0, 'L1_gnn_b1': 8.0, 'L1_gnn_b2': 3.746}
    for name, (base, spread) in spreads.items():
        noise = np.random.default_rng([zlib.crc32(name.encode()), seed]).standard_normal(out[name].shape)
        drawn = base * np.exp(spread * noise) if base else spread * noise
        out[name] = jnp.asarray(drawn.astype(out[name].dtype))
    for name, factor in factors.items():
        out[name] = (out[name] * factor).astype(out[name].dtype)
    return out
```

```python
import concourse.bass as bass
from concourse import mybir
from contextlib import ExitStack

P = 128
N_NODES = 3125
D = 128
HID = 512
N_EDGES = 50000
K = 8
GE = K * P
NG = -(-N_EDGES // GE)
TP = NG * K
E_PAD = TP * P
NJ = -(-N_NODES // P)
N_LAST = N_NODES - (NJ - 1) * P
NPAD = NJ * P
W = 128
EP = N_EDGES // P
E_TAIL = N_EDGES - EP * P
NH = 64
PAD_KEY = NH * NH - 1
PAD_DST = 1 << 20
FMAX = 3.4028234663852886e38
EPS = 1e-5
R_DUMP = E_PAD
R_ZERO = E_PAD + P
HALF = NG // 2
assert NG == 2 * HALF + 1 and EP * P + E_TAIL == N_EDGES and TP - EP == 2


def over_chunks(eng, step):
    step(0, 0, True, False)
    step(0, 1, True, False)
    with eng.Fori(1, HALF) as i:
        step(i, 0, False, False)
        step(i, 1, False, False)
    step(HALF, 0, False, True)


def over_tiles(eng, step):
    step(0, True)
    with eng.Fori(1, NJ) as j:
        step(j, False)


def gnn(nc, x, src, dst, attr, w0a, b0a, w0b, b0b, u, w1, b1, w2, b2, out, table, sorted_rows, flags, running, node_scr):
    fp32, bf16, i32 = mybir.dt.float32, mybir.dt.bfloat16, mybir.dt.int32
    ALU = mybir.AluOpType
    ACT = mybir.ActivationFunctionType
    AX = mybir.AxisListType
    ds = bass.ds

    ctx = ExitStack()
    with ctx:
        def sb(name, shape, dt):
            return ctx.enter_context(nc.sbuf_tensor(name, shape, dt))

        def pb(name, shape, dt):
            return ctx.enter_context(nc.psum_tensor(name, shape, dt))

        def sem(name):
            return ctx.enter_context(nc.semaphore(name))

        def sem2(name):
            return [sem(f"{name}{s}") for s in range(2)]

        x_sb = sb("x_sb", [P, NJ, D], fp32)
        h_sb = sb("h_sb", [P, NJ, D], fp32)
        tmp = sb("tmp", [P, NJ, D], fp32)
        accT = sb("accT", [P, NPAD + W], fp32)
        agg_mem = sb("agg_mem", [P, NJ * 2 * D], fp32)
        agg = agg_mem[:, :].rearrange("p (j f) -> p j f", j=NJ)
        parts = agg_mem[:, 0:NJ * 3 * D // 2].bitcast(bf16).rearrange("p (j c f) -> p j c f", j=NJ, c=3)
        stat = sb("stat", [P, 4, NJ], fp32)
        iota_w = sb("iota_w", [P, W], fp32)
        tri = sb("tri", [P, P], fp32)
        ident = sb("ident", [P, P], fp32)
        identb = sb("identb", [P, P], bf16)
        ones = sb("ones", [P, P], fp32)
        zeros = sb("zeros", [P, 448], fp32)
        zerob = sb("zerob", [P, NH], bf16)
        dump_f = sb("dump_f", [P, 32], fp32)
        pdump = sb("pdump", [P, 2], fp32)
        tcol = sb("tcol", [P, TP], fp32)
        run_sb0, run_sb1 = [sb(f"run_sb{s}", [P, K, 2 * D], fp32) for s in range(2)]
        attr_sb = [sb(f"attr_sb{s}", [P, K, D], fp32) for s in range(2)]
        sorted_sb = [sb(f"sorted_sb{s}", [P, K, D], fp32) for s in range(2)]
        src_g, dst_g = [attr_sb[s][0:NG, :, :].rearrange("g k f -> g (k f)").bitcast(i32) for s in range(2)]
        srcf_g, dl_g = [sorted_sb[s][0:NG, :, :].rearrange("g k f -> g (k f)") for s in range(2)]
        base_g = sb("base_g", [NG, 1], fp32)
        base_row = sb("base_row", [1, NG], i32)
        src_col = sb("src_col", [P, NG, K], i32)
        dl_col = sb("dl_col", [P, NG, K], fp32)
        far_col = sb("far_col", [P, NG, K], fp32)
        far_g = run_sb0[0:NG, 0:K // 2, :].rearrange("g k f -> g (k f)")
        any_g = sb("any_g", [NG, 1], fp32)
        any_row = sb("any_row", [1, NG], fp32)
        any_far = sb("any_far", [1, 1], i32)
        far_key = sb("far_key", [P, K], fp32)
        src_p = sb("src_p", [P, TP], i32)
        dst_p = sb("dst_p", [P, TP], i32)
        ki = sb("ki", [P, TP], i32)
        s_hi = sb("s_hi", [P, TP], fp32)
        s_lo = sb("s_lo", [P, TP], fp32)
        d_hi = sb("d_hi", [P, TP], fp32)
        d_lo = sb("d_lo", [P, TP], fp32)
        pos_f = sb("pos_f", [P, K], fp32)
        pos = sb("pos", [P, TP], i32)
        w0 = [sb(f"w0_{n}", [P, 2, D], fp32) for n in range(2)]
        b0 = [sb(f"b0_{n}", [1, D], fp32) for n in range(2)]
        w1_sb = sb("w1_sb", [P, 4, HID], fp32)
        w1u_b1 = sb("w1u_b1", [8, P], fp32)
        w1u_b1T = sb("w1u_b1T", [P, 8], fp32)
        u_sb = sb("u_sb", [1, 1], fp32)
        u_col = sb("u_col", [P, 1], fp32)
        bias1 = sb("bias1", [P, 4], fp32)
        w2_sb = sb("w2_sb", [P, 4, D], fp32)
        b2_sb = sb("b2_sb", [1, D], fp32)
        idx = [sb(f"idx{s}", [P, K], i32) for s in range(2)]
        rows = [sb(f"rows{s}", [P, K, 3 * D], bf16) for s in range(2)]
        onehot = [sb(f"onehot{s}", [P, K, W], bf16) for s in range(2)]
        oh_shi = [sb(f"oh_shi{s}", [P, K, NH], bf16) for s in range(2)]
        oh_slo = [sb(f"oh_slo{s}", [P, K, NH], bf16) for s in range(2)]
        oh_dhi = [run_sb0[:, 4 + s, :].bitcast(bf16).rearrange("p (k l) -> p k l", k=K) for s in range(2)]
        oh_dlo = [run_sb0[:, 6 + s, :].bitcast(bf16).rearrange("p (k l) -> p k l", k=K) for s in range(2)]
        hiT_f = sb("hiT_f", [NH, K * P], fp32)
        hiT_b = sb("hiT_b", [NH, K * P], bf16)
        same = sb("same", [P, K, P], bf16)
        before = [sb(f"before{s}", [NH, K + 1, NH], fp32) for s in range(2)]
        picked = sb("picked", [P, K, NH], fp32)
        run_sb = [run_sb0, run_sb1]
        gate = [sb(f"gate{s}", [P, 2, K], fp32) for s in range(2)]
        info = sb("info", [NH, 4, NH], fp32)
        incl = sb("incl", [NH, NH], fp32)
        off = sb("off", [NH, 1], fp32)
        info_r = sb("info_r", [32, 4, P], fp32)
        info_n = sb("info_n", [P, 4, 32], fp32)
        has = sb("has", [P, 32], fp32)
        nt1 = sb("nt1", [P, 32], fp32)
        start_idx = sb("start_idx", [P, 32], i32)
        last_idx = sb("last_idx", [P, 32], i32)
        rdeg = sb("rdeg", [P, 32], fp32)
        rcnt = sb("rcnt", [P, 32], fp32)
        is_start = sb("is_start", [P, TP], fp32)
        keep = sb("keep", [P, 2, TP], fp32)
        seg_t = sb("seg_t", [P, TP], fp32)
        first_t = sb("first_t", [P, 1], fp32)
        whole = sb("whole", [P, 1], fp32)
        fix_f = sb("fix_f", [P, 4], fp32)
        fix_idx = sb("fix_idx", [P, 1], i32)
        diag = sb("diag", [P, P], fp32)
        tail = sb("tail", [P, 2 * D], fp32)
        whole_row = sb("whole_row", [P, 2, P], fp32)
        carry = sb("carry", [P, 2, P + 1], fp32)
        fix_rows = sb("fix_rows", [P, 2 * D], fp32)
        fixed = sb("fixed", [P, 2 * D], fp32)
        t_h = sb("t_h", [P, D], fp32)
        t_hT = sb("t_hT", [P, D], fp32)
        t_acc = sb("t_acc", [P, D], fp32)
        t_z = sb("t_z", [P, D], fp32)
        feat = sb("feat", [P, 4, D], fp32)
        featT = sb("featT", [P, 4, P], fp32)
        hidT = sb("hidT", [P, 4, P], fp32)
        y_sb = tmp

        p_agg = [pb(f"p_agg{s}", [P, 512], fp32) for s in range(2)]
        p_pre = pb("p_pre", [P, 512], fp32)
        p_hiT = pb("p_hiT", [P, 1024], bf16)
        p_eq = pb("p_eq", [P, 1024], fp32)
        p_rank = pb("p_rank", [P, 512], fp32)
        p_misc = pb("p_misc", [P, 512], fp32)

        consts_a = sem("consts_a")
        consts = sem("consts")
        memsets = sem("memsets")
        x_in = sem("x_in")
        e_in = sem("e_in")
        w_in = sem("w_in")
        zero_out = sem("zero_out")
        dve = sem("dve_step")
        var_ready = sem("var_ready")
        std_ready = sem("std_ready")
        parts_ready = sem("parts_ready")
        table_out = [sem("table_out0"), sem("table_out1")]
        edges_f = sem("edges_f")
        edgesT = sem("edgesT")
        edge_cols = sem("edge_cols")
        acc_zero = sem("acc_zero")
        hist_oh = sem2("hist_oh")
        hist_used = sem2("hist_used")
        hist_done = sem("hist_done")
        totals = sem("totals")
        offsets = sem("offsets")
        info_ready = sem("info_ready")
        info_out = sem("info_out")
        info_in = sem("info_in")
        infoT = sem("infoT")
        u_done = sem("u_done")
        idx_ready = sem("idx_ready")
        idx_staged = [sem2(f"idx_staged{n}_") for n in range(3)]
        idx_first = [sem2(f"idx_first{n}_") for n in range(3)]
        rows_in = [sem2(f"rows_in{n}_") for n in range(2)]
        onehot_ready = [sem2(f"onehot_ready{n}_") for n in range(2)]
        summed = [sem2(f"summed{n}_") for n in range(2)]
        added = [sem2(f"added{n}_") for n in range(2)]
        sums_ready = [sem("sums_ready0"), sem("sums_ready1")]
        far_free = [sem("far_free0"), sem("far_free1")]
        far_staged = [sem("far_staged0"), sem("far_staged1")]
        far_rows = [sem("far_rows0"), sem("far_rows1")]
        far_key_ready = [sem("far_key_ready0"), sem("far_key_ready1")]
        far_onehot = [sem("far_onehot0"), sem("far_onehot1")]
        far_summed = [sem("far_summed0"), sem("far_summed1")]
        far_added = [sem("far_added0"), sem("far_added1")]
        oh_ready = sem("oh_ready")
        pre_done = sem("pre_done")
        hiT_done = sem("hiT_done")
        hiT_ready = sem("hiT_ready")
        before_ready = sem("before_ready")
        eq_done = sem("eq_done")
        same_ready = sem("same_ready")
        rank_done = sem("rank_done")
        picked_ready = sem("picked_ready")
        pos_f_ready = sem("pos_f_ready")
        pos_ready = sem("pos_ready")
        attr_in = sem2("attr_in")
        scattered = sem2("scattered")
        flags_out = sem("flags_out")
        flags_in = sem("flags_in")
        keep_ready = sem("keep_ready")
        sorted_in = sem2("sorted_in")
        run_step = sem("run_step")
        run_done = sem2("run_done")
        run_out = sem2("run_out")
        gate_ready = sem("gate_ready")
        tails_ready = sem("tails_ready")
        tailsT = sem("tailsT")
        carry_ready = sem("carry_ready")
        carry_back = sem("carry_back")
        fix_in = sem("fix_in")
        fixed_ready = sem("fixed_ready")
        fix_out = sem("fix_out")
        agg_in = sem("agg_in")
        z_h = [sem("z_h0"), sem("z_h1")]
        z_T = [sem("z_T0"), sem("z_T1")]
        z_Tc = [sem("z_Tc0"), sem("z_Tc1")]
        z_mm = [sem("z_mm0"), sem("z_mm1")]
        z_c = [sem("z_c0"), sem("z_c1")]
        z_done = [sem("z_done0"), sem("z_done1")]
        ln2_ready = sem("ln2_ready")
        f_ready = sem("f_ready")
        f_T = sem("f_T")
        f_Tc = sem("f_Tc")
        m_hid = sem("m_hid")
        m_relu = sem("m_relu")
        m_out = sem("m_out")
        m_y0 = sem("m_y0")
        y_ready = sem("y_ready")
        y_out = sem("y_out")

        block = ctx.enter_context(nc.Block())

        sorted_v = sorted_rows.rearrange("(p t) f -> p t f", p=P)
        running_v = running[0:E_PAD, :].rearrange("(p t) f -> p t f", p=P)
        attr_v = attr[0:EP * P, :].rearrange("(p t) f -> p t f", p=P)

        def node_view(a, j0, j1):
            return a[j0 * P:j1 * P, :].rearrange("(j p) f -> p j f", p=P)

        @block.sync
        def _(sp):
            sp.wait_ge(memsets, 5)
            sp.dma_start(x_sb[:, 0:NJ - 1, :], node_view(x, 0, NJ - 1)).then_inc(x_in, 16)
            sp.dma_start(x_sb[0:N_LAST, NJ - 1, :], x[(NJ - 1) * P:N_NODES, :]).then_inc(x_in, 16)
            full = (NG - 1) * GE
            for t, a in ((dst_g, dst), (src_g, src)):
                sp.dma_start(t[0:NG - 1, :], a[0:full].rearrange("(g e) -> g e", e=GE)).then_inc(e_in, 16)
                sp.dma_start(t[NG - 1:NG, 0:N_EDGES - full], a[full:N_EDGES].rearrange("(o e) -> o e", o=1)).then_inc(e_in, 16)
            for t, a in ((src_p, src), (dst_p, dst)):
                sp.dma_start(t[:, 0:EP], a[0:EP * P].rearrange("(p t) -> p t", p=P)).then_inc(e_in, 16)
                sp.dma_start(t[0:E_TAIL, EP:EP + 1], a[EP * P:N_EDGES].rearrange("(p o) -> p o", o=1)).then_inc(e_in, 16)
            sp.wait_ge(consts, 1)
            sp.dma_start(flags.rearrange("(p c) o -> p (c o)", p=P), zeros[:, 0:424]).then_inc(zero_out, 16)
            sp.dma_start(sorted_rows[N_EDGES:E_PAD, :].rearrange("r f -> (r f)").rearrange("(p c) -> p c", p=P),
                         zeros[:, 0:E_PAD - N_EDGES]).then_inc(zero_out, 16)
            sp.dma_start(running[R_DUMP:R_ZERO + 1, :].rearrange("r f -> (r f)").rearrange("(p c) -> p c", p=P),
                         zeros[:, 0:258]).then_inc(zero_out, 16)
            sp.wait_ge(info_ready, 1)
            sp.dma_start(node_scr.rearrange("k (h l) -> h k l", l=NH), info[:, :, :]).then_inc(info_out, 16)
            sp.wait_ge(info_out, 16)
            sp.dma_start(info_r[:, :, :], node_scr.rearrange("k (j p) -> j k p", p=P)).then_inc(info_in, 16)

            def load_attr(i, s, first, last):
                g = i * 2 + s
                if not first:
                    sp.wait_ge(scattered[s], i * (16 * K))
                if not last:
                    sp.dma_start(attr_sb[s][:, :, :], attr_v[:, ds(g * K, K), :]).then_inc(attr_in[s], 16)
                else:
                    sp.dma_start(attr_sb[s][:, 0:K - 2, :], attr_v[:, EP - K + 2:EP, :]).then_inc(attr_in[s], 16)
                    sp.dma_start(attr_sb[s][0:E_TAIL, K - 2, :], attr[EP * P:N_EDGES, :]).then_inc(attr_in[s], 16)

            over_chunks(sp, load_attr)
            sp.wait_ge(flags_out, 16 * NJ)
            sp.dma_start(is_start[:, :], flags[0:E_PAD, :].rearrange("(p t) o -> p (t o)", p=P)).then_inc(flags_in, 16)
            sp.wait_ge(scattered[0], 16 * K * (HALF + 1) - 16)
            sp.wait_ge(scattered[1], 16 * K * HALF)

            def store_run(i, s):
                g = i * 2 + s
                sp.wait_ge(run_done[s], i + 1)
                sp.dma_start(running_v[:, ds(g * K, K), :], run_sb[s][:, :, :]).then_inc(run_out[s], 16)

            def load_sorted(i, s, first, last):
                g = i * 2 + s
                if not first:
                    sp.wait_ge(run_done[s], i)
                sp.dma_start(sorted_sb[s][:, :, :], sorted_v[:, ds(g * K, K), :]).then_inc(sorted_in[s], 16)
                if s == 1:
                    store_run(i, 0)
                elif not first:
                    store_run(i - 1, 1)

            over_chunks(sp, load_sorted)
            store_run(HALF, 0)

            for j in range(NJ):
                n = P if j < NJ - 1 else N_LAST
                sp.wait_ge(y_ready, j + 1)
                sp.dma_start(out[j * P:j * P + n, :], y_sb[0:n, j, :]).then_inc(y_out, 16)
            sp.wait_ge(y_out, 16 * NJ)

        @block.gpsimd
        def _(pool):
            pool.memset(x_sb[:, NJ - 1, :], 0.0).then_inc(memsets, 1)
            pool.memset(src_g, 0).then_inc(memsets, 1)
            pool.memset(dst_g, PAD_DST).then_inc(memsets, 1)
            pool.memset(src_p[:, EP:TP], PAD_KEY).then_inc(memsets, 1)
            pool.memset(dst_p[:, EP:TP], PAD_KEY).then_inc(memsets, 1)
            pool.memset(zeros[:, :], 0.0).then_inc(consts, 1)
            pool.memset(ones[:, :], 1.0).then_inc(consts_a, 1)
            pool.memset(ident[:, :], 0.0).then_inc(consts_a, 1)
            pool.memset(identb[:, :], 0.0).then_inc(consts_a, 1)
            pool.wait_ge(consts_a, 3)
            for m in (ident, identb):
                pool.affine_select(out=m[:, :], in_=m[:, :], compare_op=ALU.not_equal, fill=1.0, base=0,
                                   pattern=[[-1, P]], channel_multiplier=1).then_inc(consts, 1)
            pool.affine_select(out=tri[:, :], in_=ones[:, :], compare_op=ALU.is_gt, fill=0.0, base=0,
                               pattern=[[1, P]], channel_multiplier=-1).then_inc(consts, 1)
            pool.iota(iota_w[:, :], pattern=[[1, W]], base=0, channel_multiplier=0,
                      allow_small_or_imprecise_dtypes=True).then_inc(consts, 1)
            pool.iota(dump_f[:, :], pattern=[[P, 32]], base=E_PAD, channel_multiplier=1,
                      allow_small_or_imprecise_dtypes=True).then_inc(consts, 1)
            pool.iota(pdump[:, 0:1], pattern=[[0, 1]], base=R_DUMP, channel_multiplier=1,
                      allow_small_or_imprecise_dtypes=True).then_inc(consts, 1)
            pool.iota(pdump[:, 1:2], pattern=[[0, 1]], base=-1, channel_multiplier=TP,
                      allow_small_or_imprecise_dtypes=True).then_inc(consts, 1)
            pool.iota(tcol[:, :], pattern=[[1, TP]], base=0, channel_multiplier=0,
                      allow_small_or_imprecise_dtypes=True).then_inc(consts, 1)
            pool.memset(zerob[:, :], 0.0).then_inc(consts, 1)
            pool.memset(accT[:, :], 0.0).then_inc(acc_zero, 1)
            pool.memset(run_sb[1][:, K - 1, 0:D], -FMAX).then_inc(consts, 1)
            pool.memset(run_sb[1][:, K - 1, D:2 * D], 0.0).then_inc(consts, 1)

            def stage(n, i, s, cols, first):
                g = i * 2 + s
                copied = pool.tensor_copy(idx[s][:, :], cols[:, ds(g * K, K)])
                if first:
                    copied.then_inc(idx_first[n][s], 1)
                    pool.wait_ge(idx_first[n][s], 1)
                else:
                    copied.then_inc(idx_staged[n][s], 1)
                    pool.wait_ge(consts, 11)
                    pool.wait_ge(idx_staged[n][s], i)

            src_cols = src_col[:, :, :].rearrange("p g k -> p (g k)")

            def gather(layer):
                def step(i, s, first, last):
                    if not first:
                        pool.wait_ge(acc_zero, 1)
                        pool.wait_ge(summed[layer][s], i)
                    stage(layer, i, s, src_cols, first)
                    for k in range(K):
                        pool.indirect_dma_start(rows[s][:, k, :], None, table[layer][:, :],
                                                bass.IndirectOffsetOnAxis(ap=idx[s][:, k:k + 1], axis=0)
                                                ).then_inc(rows_in[layer][s], 16)
                return step

            def gather_again(layer):
                pool.wait_ge(far_free[layer], 1)
                with pool.If(pool.value_load(any_far[0:1, 0:1]) > 0):
                    with pool.Fori(1, NG + 1) as g1:
                        pool.wait_ge(consts, 11)
                        pool.wait_ge(far_free[layer], g1)
                        pool.tensor_copy(idx[0][:, :], src_cols[:, ds((g1 - 1) * K, K)]).then_inc(far_staged[layer], 1)
                        pool.wait_ge(consts, 11)
                        pool.wait_ge(far_staged[layer], g1)
                        for k in range(K):
                            pool.indirect_dma_start(rows[0][:, k, :], None, table[layer][:, :],
                                                    bass.IndirectOffsetOnAxis(ap=idx[0][:, k:k + 1], axis=0)
                                                    ).then_inc(far_rows[layer], 16)
                    pool.wait_ge(far_rows[layer], NG * 16 * K)

            pool.wait_ge(edge_cols, 1)
            pool.wait_ge(table_out[0], 32)
            over_chunks(pool, gather(0))
            gather_again(0)
            pool.wait_ge(summed[0][0], HALF + 1)
            pool.wait_ge(summed[0][1], HALF)
            pool.wait_ge(zero_out, 48)
            pool.wait_ge(idx_ready, 2)
            for j in range(NJ):
                pool.indirect_dma_start(flags[:, :], bass.IndirectOffsetOnAxis(ap=start_idx[:, j:j + 1], axis=0),
                                        ones[:, 0:1], None).then_inc(flags_out, 16)

            def scatter(i, s, first, last):
                if not first:
                    pool.wait_ge(acc_zero, 1)
                    pool.wait_ge(scattered[s], i * (16 * K))
                pool.wait_ge(attr_in[s], (i + 2 if last else i + 1) * 16)
                stage(2, i, s, pos, first)
                for k in range(K if not last else K - 1):
                    n = E_TAIL if last and k == K - 2 else P
                    pool.indirect_dma_start(sorted_rows[:, :], bass.IndirectOffsetOnAxis(ap=idx[s][0:n, k:k + 1], axis=0),
                                            attr_sb[s][0:n, k, :], None).then_inc(scattered[s], 16)

            pool.wait_ge(pos_ready, NG)
            over_chunks(pool, scatter)
            pool.wait_ge(scattered[0], 16 * K * (HALF + 1) - 16)
            pool.wait_ge(scattered[1], 16 * K * HALF)
            pool.wait_ge(table_out[1], 32)
            over_chunks(pool, gather(1))
            gather_again(1)
            pool.wait_ge(run_out[0], 16 * (HALF + 1))
            pool.wait_ge(run_out[1], 16 * HALF)
            pool.wait_ge(zero_out, 48)
            pool.wait_ge(idx_ready, 3)
            pool.indirect_dma_start(fix_rows[:, :], None, running[:, :],
                                    bass.IndirectOffsetOnAxis(ap=fix_idx[:, 0:1], axis=0)).then_inc(fix_in, 16)
            pool.wait_ge(fixed_ready, 2)
            pool.indirect_dma_start(running[:, :], bass.IndirectOffsetOnAxis(ap=fix_idx[:, 0:1], axis=0),
                                    fixed[:, :], None).then_inc(fix_out, 16)
            pool.wait_ge(fix_out, 16)
            for j in range(NJ):
                pool.indirect_dma_start(agg[:, j, :], None, running[:, :],
                                        bass.IndirectOffsetOnAxis(ap=last_idx[:, j:j + 1], axis=0)).then_inc(agg_in, 16)

        @block.scalar
        def _(act):
            for n, (w, b) in enumerate(((w0a, b0a), (w0b, b0b))):
                act.dma_start(w0[n][:, :, :], w.rearrange("(k p) n -> p k n", p=P)).then_inc(w_in, 16)
                act.dma_start(b0[n][:, :], b.rearrange("(o n) -> o n", o=1)).then_inc(w_in, 16)
            act.dma_start(w1_sb[:, :, :], w1[0:HID, :].rearrange("(k p) n -> p k n", p=P)).then_inc(w_in, 16)
            act.dma_start(w2_sb[:, :, :], w2.rearrange("(k p) n -> p k n", p=P)).then_inc(w_in, 16)
            act.dma_start(b2_sb[:, :], b2.rearrange("(o n) -> o n", o=1)).then_inc(w_in, 16)
            act.dma_start(u_sb[:, :], u[0:1, :]).then_inc(w_in, 16)
            act.dma_start(w1u_b1[0:4, :], w1[HID, :].rearrange("(c p) -> c p", p=P)).then_inc(w_in, 16)
            act.dma_start(w1u_b1[4:8, :], b1.rearrange("(c p) -> c p", p=P)).then_inc(w_in, 16)

            def write_table(layer):
                act.wait_ge(parts_ready, layer + 1)
                v = parts.rearrange("p j c f -> p j (c f)")
                act.dma_start(node_view(table[layer], 0, NJ - 1), v[:, 0:NJ - 1, :]).then_inc(table_out[layer], 16)
                act.dma_start(table[layer][(NJ - 1) * P:N_NODES, :], v[0:N_LAST, NJ - 1, :]).then_inc(table_out[layer], 16)

            act.wait_ge(var_ready, 1)
            act.activation(stat[:, 2, :], stat[:, 1, :], ACT.Sqrt).then_inc(std_ready, 1)
            write_table(0)

            def rank_copies(i, s, first, last):
                c = i * 2 + s + 1
                act.wait_ge(hiT_done, c)
                if s or not first:
                    act.wait_ge(rank_done, i * 2 + s)
                act.activation(hiT_f[:, :], p_hiT[0:NH, :], ACT.Copy).then_inc(hiT_ready, 1)
                act.activation(hiT_b[:, :], p_hiT[0:NH, :], ACT.Copy).then_inc(hiT_ready, 1)

            over_chunks(act, rank_copies)

            def z_copies(layer):
                def step(j, first):
                    if not first:
                        act.wait_ge(z_done[layer], j)
                    act.activation(t_h[:, :], h_sb[:, ds(j, 1), :].rearrange("p o f -> p (o f)"), ACT.Copy).then_inc(z_h[layer], 1)
                    act.activation(t_acc[:, :], accT[:, ds(j * P, P)], ACT.Copy).then_inc(z_h[layer], 1)
                    act.wait_ge(z_T[layer], j + 1)
                    act.activation(t_hT[:, :], p_misc[:, 0:P], ACT.Copy).then_inc(z_Tc[layer], 1)
                    act.wait_ge(z_mm[layer], j + 1)
                    act.activation(t_z[:, :], p_pre[:, 0:D], ACT.Copy).then_inc(z_c[layer], 1)
                return step

            act.wait_ge(sums_ready[0], 1)
            over_tiles(act, z_copies(0))
            write_table(1)
            act.wait_ge(sums_ready[1], 1)
            over_tiles(act, z_copies(1))
            act.wait_ge(var_ready, 2)
            act.activation(stat[:, 2, :], stat[:, 1, :], ACT.Sqrt).then_inc(std_ready, 1)

            act.wait_ge(agg_in, 16 * NJ)
            act.wait_ge(ln2_ready, 1)
            act.wait_ge(idx_ready, 2)

            def mlp(j, first):
                one = ds(j, 1)
                if not first:
                    act.wait_ge(y_ready, j)
                act.activation(feat[:, 0, :], h_sb[:, one, :].rearrange("p o f -> p (o f)"), ACT.Copy).then_inc(f_ready, 1)
                act.activation(feat[:, 1, :], agg[:, one, D:2 * D].rearrange("p o f -> p (o f)"), ACT.Copy).then_inc(f_ready, 1)
                act.activation(feat[:, 2, :], agg[:, one, 0:D].rearrange("p o f -> p (o f)"), ACT.Copy).then_inc(f_ready, 1)
                act.activation(feat[:, 3, :], agg[:, one, D:2 * D].rearrange("p o f -> p (o f)"), ACT.Copy,
                               scale=rcnt[:, one]).then_inc(f_ready, 1)
                act.wait_ge(f_T, j + 1)
                act.activation(featT[:, :, :].rearrange("p k n -> p (k n)"), p_misc[:, :], ACT.Copy).then_inc(f_Tc, 1)
                act.wait_ge(m_hid, j + 1)
                for c in range(4):
                    act.activation(hidT[:, c, :], p_rank[:, c * P:(c + 1) * P], ACT.Relu,
                                   bias=bias1[:, c:c + 1]).then_inc(m_relu, 1)

            over_tiles(act, mlp)

        @block.tensor
        def _(pe):
            mm = nc.tensor.matmul
            pe.wait_ge(consts, 11)
            pe.wait_ge(edges_f, 3)
            for k in range(K):
                nc.tensor.transpose(p_misc[:, k * NG:(k + 1) * NG], dl_g[:, k * P:(k + 1) * P], ident[0:NG, 0:NG]).then_inc(edgesT, 1)
            for k in range(K):
                nc.tensor.transpose(p_rank[:, k * NG:(k + 1) * NG], srcf_g[:, k * P:(k + 1) * P], ident[0:NG, 0:NG]).then_inc(edgesT, 1)
            for k in range(K):
                nc.tensor.transpose(p_agg[0][:, k * NG:(k + 1) * NG], far_g[:, k * P:(k + 1) * P], ident[0:NG, 0:NG]).then_inc(edgesT, 1)
            nc.tensor.transpose(p_pre[0:1, 64:64 + NG], any_g[:, :], ident[0:NG, 0:NG]).then_inc(edgesT, 1)
            nc.tensor.transpose(p_pre[0:1, 0:NG], base_g[:, :], ident[0:NG, 0:NG]).then_inc(edgesT, 1)
            pe.wait_ge(edge_cols, 1)

            mm(p_rank[0:NH, 0:NH], zerob[:, :], zerob[:, :], start=True, stop=False)
            mm(p_misc[0:NH, 0:NH], zerob[:, :], zerob[:, :], start=True, stop=False)

            def count(i, s, first, last):
                pe.wait_ge(hist_oh[s], (i + 1) * 4)
                for k in range(K):
                    mm(p_rank[0:NH, 0:NH], oh_shi[s][:, k, :], oh_slo[s][:, k, :], start=False, stop=False)
                    n = mm(p_misc[0:NH, 0:NH], oh_dhi[s][:, k, :], oh_dlo[s][:, k, :], start=False, stop=False)
                n.then_inc(hist_used[s], 1)

            over_chunks(pe, count)
            mm(p_rank[0:NH, 0:NH], zerob[:, :], zerob[:, :], start=False, stop=True)
            mm(p_misc[0:NH, 0:NH], zerob[:, :], zerob[:, :], start=False, stop=True).then_inc(hist_done, 1)
            pe.wait_ge(totals, 1)
            mm(p_pre[0:NH, 0:1], tri[0:NH, 0:NH], incl[:, NH - 1:NH], start=True, stop=True).then_inc(offsets, 1)
            pe.wait_ge(w_in, 16 * 10)
            pe.wait_ge(info_in, 16)
            for k in range(4):
                nc.tensor.transpose(p_misc[:, 32 * k:32 * k + 32], info_r[:, k, :], ident[0:32, 0:32]).then_inc(infoT, 1)
            nc.tensor.transpose(p_misc[:, 260:268], w1u_b1[:, :], ident[0:8, 0:8])
            mm(p_misc[:, 256:257], ones[0:1, :], u_sb[:, :], start=True, stop=True).then_inc(u_done, 1)
            pe.wait_ge(idx_ready, 2)

            def sum_rows(layer):
                def step(i, s, first, last):
                    pe.wait_ge(rows_in[layer][s], (i + 1) * (16 * K))
                    pe.wait_ge(onehot_ready[layer][s], i + 1)
                    if not first:
                        pe.wait_ge(added[layer][s], i)
                    for k in range(K):
                        for c in range(3):
                            n = mm(p_agg[s][:, 0:W], rows[s][:, k, c * D:(c + 1) * D], onehot[s][:, k, :],
                                   start=(k == 0 and c == 0), stop=(k == K - 1 and c == 2))
                    n.then_inc(summed[layer][s], 1)
                return step

            def rank(i, s, first, last):
                g1 = i * 2 + s + 1
                pe.wait_ge(oh_ready, g1)
                if s or not first:
                    pe.wait_ge(before_ready, i * 4 + 2 * s)
                for k in range(K):
                    n = mm(p_pre[0:NH, k * NH:K * NH].rearrange("p (t l) -> p t l", l=NH), oh_shi[s][:, k, :],
                           oh_slo[s][:, k:k + 1, :].to_broadcast([P, K - k, NH]), start=(k == 0), stop=(k == K - 1))
                n.then_inc(pre_done, 1)
                if s or not first:
                    pe.wait_ge(consts, 11)
                    pe.wait_ge(hiT_ready, i * 4 + 2 * s)
                for k in range(K):
                    n = nc.tensor.transpose(p_hiT[0:NH, k * P:(k + 1) * P], oh_shi[s][:, k, :], identb[:, :])
                n.then_inc(hiT_done, 1)
                pe.wait_ge(hiT_ready, i * 4 + 2 * s + 2)
                for k in range(K):
                    n = mm(p_eq[:, k * P:(k + 1) * P], hiT_b[:, k * P:(k + 1) * P], hiT_b[:, k * P:(k + 1) * P], start=True, stop=True)
                n.then_inc(eq_done, 1)
                pe.wait_ge(same_ready, g1)
                pe.wait_ge(before_ready, i * 4 + 2 * s + 2)
                for k in range(K):
                    mm(p_rank[:, k * NH:(k + 1) * NH], hiT_f[:, k * P:(k + 1) * P], before[s][:, k, :], start=True, stop=False)
                    n = mm(p_rank[:, k * NH:(k + 1) * NH], same[:, k, :], oh_slo[s][:, k, :], start=False, stop=True)
                n.then_inc(rank_done, 1)

            def sum_far(layer):
                pe.wait_ge(far_free[layer], 1)
                with pe.If(pe.value_load(any_far[0:1, 0:1]) > 0):
                    with pe.Fori(1, NG + 1) as g1:
                        with pe.Fori(1, NJ + 1) as c1:
                            pe.wait_ge(consts, 11)
                            pe.wait_ge(far_rows[layer], g1 * (16 * K))
                            pe.wait_ge(far_onehot[layer], (g1 - 1) * NJ + c1)
                            for k in range(K):
                                for c in range(3):
                                    n = mm(p_agg[0][:, 0:W], rows[0][:, k, c * D:(c + 1) * D], onehot[0][:, k, :],
                                           start=(k == 0 and c == 0), stop=(k == K - 1 and c == 2))
                            n.then_inc(far_summed[layer], 1)

            agg0 = sum_rows(0)

            def both(i, s, first, last):
                rank(i, s, first, last)
                agg0(i, s, first, last)

            over_chunks(pe, both)

            def z_mms(layer):
                def step(j, first):
                    pe.wait_ge(z_h[layer], j * 2 + 2)
                    nc.tensor.transpose(p_misc[:, 0:P], t_h[:, :], ident[:, :]).then_inc(z_T[layer], 1)
                    pe.wait_ge(z_Tc[layer], j + 1)
                    mm(p_pre[:, 0:D], t_hT[:, :], w0[layer][:, 0, :], start=True, stop=False)
                    mm(p_pre[:, 0:D], ones[0:1, :], b0[layer][:, :], start=False, stop=True)
                    mm(p_rank[:, 0:D], t_acc[:, :], w0[layer][:, 1, :], start=True, stop=True).then_inc(z_mm[layer], 1)
                return step

            sum_far(0)
            pe.wait_ge(pos_ready, NG)
            over_tiles(pe, z_mms(0))
            over_chunks(pe, sum_rows(1))
            sum_far(1)
            pe.wait_ge(tails_ready, 2)
            mm(p_misc[:, 0:P], ones[:, :], diag[:, :], start=True, stop=True)
            for c in range(2):
                n = nc.tensor.transpose(p_misc[:, (c + 1) * P:(c + 2) * P], tail[:, c * D:(c + 1) * D], ident[:, :])
            n.then_inc(tailsT, 1)
            pe.wait_ge(carry_ready, 4)
            for c in range(2):
                n = nc.tensor.transpose(p_eq[:, c * P:(c + 1) * P], carry[:, c, 0:P], ident[:, :])
            n.then_inc(carry_back, 1)
            over_tiles(pe, z_mms(1))

            def mlp(j, first):
                pe.wait_ge(f_ready, j * 4 + 4)
                for c in range(4):
                    n = nc.tensor.transpose(p_misc[:, c * P:(c + 1) * P], feat[:, c, :], ident[:, :])
                n.then_inc(f_T, 1)
                pe.wait_ge(f_Tc, j + 1)
                for c in range(4):
                    for k in range(4):
                        n = mm(p_rank[:, c * P:(c + 1) * P], w1_sb[:, k, c * P:(c + 1) * P], featT[:, k, :],
                               start=(k == 0), stop=(k == 3))
                n.then_inc(m_hid, 1)
                pe.wait_ge(m_relu, j * 4 + 4)
                for c in range(4):
                    mm(p_pre[:, 0:D], hidT[:, c, :], w2_sb[:, c, :], start=(c == 0), stop=False)
                mm(p_pre[:, 0:D], ones[0:1, :], b2_sb[:, :], start=False, stop=True).then_inc(m_out, 1)

            over_tiles(pe, mlp)

        @block.vector
        def _(v):
            tt, tsc, stt, copy = nc.vector.tensor_tensor, nc.vector.tensor_scalar, nc.vector.scalar_tensor_tensor, nc.vector.tensor_copy
            steps = [0]

            def link(ins):
                steps[0] += 1
                ins.then_inc(dve, 1)
                v.wait_ge(dve, steps[0])

            def bc(a, n):
                return a.unsqueeze(2).to_broadcast([a.shape[0], a.shape[1], n])

            def layernorm_relu(nth):
                link(nc.vector.tensor_reduce(stat[:, 0, :], x_sb[:, :, :], axis=AX.X, op=ALU.add))
                link(tsc(stat[:, 0, :], stat[:, 0, :], 1.0 / D, None, ALU.mult))
                link(tt(h_sb[:, :, :], x_sb[:, :, :], bc(stat[:, 0, :], D), ALU.subtract))
                link(tt(tmp[:, :, :], h_sb[:, :, :], h_sb[:, :, :], ALU.mult))
                link(nc.vector.tensor_reduce(stat[:, 1, :], tmp[:, :, :], axis=AX.X, op=ALU.add))
                tsc(stat[:, 1, :], stat[:, 1, :], 1.0 / D, EPS, ALU.mult, ALU.add).then_inc(var_ready, 1)
                v.wait_ge(std_ready, nth)
                link(nc.vector.reciprocal(stat[:, 3, :], stat[:, 2, :]))
                link(tt(h_sb[:, :, :], h_sb[:, :, :], bc(stat[:, 3, :], D), ALU.mult))
                link(tsc(h_sb[:, :, :], h_sb[:, :, :], 0.0, None, ALU.max))

            def split_parts():
                link(copy(parts[:, :, 0, :], h_sb[:, :, :]))
                link(tt(tmp[:, :, :], h_sb[:, :, :], parts[:, :, 0, :], ALU.subtract))
                link(copy(parts[:, :, 1, :], tmp[:, :, :]))
                link(tt(tmp[:, :, :], tmp[:, :, :], parts[:, :, 1, :], ALU.subtract))
                copy(parts[:, :, 2, :], tmp[:, :, :]).then_inc(parts_ready, 1)

            v.wait_ge(x_in, 32)
            layernorm_relu(1)
            split_parts()
            v.wait_ge(e_in, 16 * 8)
            link(copy(dl_g, dst_g))
            link(nc.vector.tensor_reduce(base_g[:, :], dl_g, axis=AX.X, op=ALU.min))
            copy(srcf_g, src_g).then_inc(edges_f, 1)
            link(tsc(far_g, dl_g, base_g[:, 0:1], float(W), ALU.subtract, ALU.is_lt))
            link(stt(far_g, far_g, float(PAD_DST), dl_g, ALU.mult, ALU.add))
            link(nc.vector.tensor_reduce(any_g[:, :], far_g, axis=AX.X, op=ALU.min))
            link(tsc(any_g[:, :], any_g[:, :], float(NPAD), None, ALU.is_lt))
            tsc(dl_g, dl_g, base_g[:, 0:1], None, ALU.subtract).then_inc(edges_f, 2)
            for key, hi, lo in ((src_p, s_hi, s_lo), (dst_p, d_hi, d_lo)):
                link(tsc(ki[:, :], key[:, :], 6, None, ALU.arith_shift_right))
                link(copy(hi[:, :], ki[:, :]))
                link(tsc(ki[:, :], key[:, :], NH - 1, None, ALU.bitwise_and))
                link(copy(lo[:, :], ki[:, :]))
            v.wait_ge(edgesT, 3 * K + 2)
            link(copy(far_col[:, :, :], p_agg[0][:, 0:TP].rearrange("p (k g) -> p g k", g=NG)))
            link(nc.vector.tensor_reduce(any_row[:, 0:1], p_pre[0:1, 64:64 + NG], axis=AX.X, op=ALU.max))
            link(copy(any_far[:, :], any_row[:, 0:1]))
            link(copy(dl_col[:, :, :], p_misc[:, 0:TP].rearrange("p (k g) -> p g k", g=NG)))
            link(copy(base_row[:, :], p_pre[0:1, 0:NG]))
            copy(src_col[:, :, :], p_rank[:, 0:TP].rearrange("p (k g) -> p g k", g=NG)).then_inc(edge_cols, 1)

            v.wait_ge(consts, 11)

            def which(dst_t, keys, g, n):
                return tt(dst_t[:, :, :], bc(keys[:, ds(g * K, K)], n),
                          iota_w[:, 0:n].unsqueeze(1).to_broadcast([P, K, n]), ALU.is_equal)

            def count(i, s, first, last):
                g = i * 2 + s
                if not first:
                    v.wait_ge(hist_used[s], i)
                which(oh_shi[s], s_hi, g, NH).then_inc(hist_oh[s], 1)
                which(oh_slo[s], s_lo, g, NH).then_inc(hist_oh[s], 1)
                which(oh_dhi[s], d_hi, g, NH).then_inc(hist_oh[s], 1)
                which(oh_dlo[s], d_lo, g, NH).then_inc(hist_oh[s], 1)

            over_chunks(v, count)
            v.wait_ge(hist_done, 1)
            link(copy(info[:, 1, :], p_rank[0:NH, 0:NH]))
            link(copy(info[:, 3, :], p_misc[0:NH, 0:NH]))
            nc.vector.tensor_tensor_scan(incl[:, :], ones[0:NH, 0:NH], info[:, 1, :], 0.0, ALU.mult, ALU.add).then_inc(totals, 1)
            v.wait_ge(offsets, 1)
            link(copy(off[:, :], p_pre[0:NH, 0:1]))
            link(tsc(incl[:, :], incl[:, :], off[:, 0:1], None, ALU.add))
            link(tt(info[:, 0, :], incl[:, :], info[:, 1, :], ALU.subtract))
            link(tsc(info[:, 2, :], incl[:, :], -1.0, None, ALU.add))
            copy(before[1][:, K, :], info[:, 0, :]).then_inc(info_ready, 1)
            v.wait_ge(infoT, 4)
            v.wait_ge(u_done, 1)
            link(copy(info_n[:, :, :], p_misc[:, 0:P].rearrange("p (k j) -> p k j", j=32)))
            link(copy(u_col[:, :], p_misc[:, 256:257]))
            v.wait_ge(w_in, 16 * 10)
            link(copy(w1u_b1T[:, :], p_misc[:, 260:268]))
            link(stt(bias1[:, :], w1u_b1T[:, 0:4], u_col[:, 0:1], w1u_b1T[:, 4:8], ALU.mult, ALU.add))
            link(tsc(has[:, :], info_n[:, 1, :], 0.0, None, ALU.is_gt))
            link(tt(nt1[:, :], info_n[:, 0, :], dump_f[:, :], ALU.subtract))
            link(tt(nt1[:, :], nt1[:, :], has[:, :], ALU.mult))
            tt(start_idx[:, :], nt1[:, :], dump_f[:, :], ALU.add).then_inc(idx_ready, 1)
            v.wait_ge(idx_ready, 1)
            link(stt(nt1[:, :], info_n[:, 2, :], -float(R_ZERO), has[:, :], ALU.add, ALU.mult))
            link(tsc(last_idx[:, :], nt1[:, :], float(R_ZERO), None, ALU.add))
            link(tsc(nt1[:, :], info_n[:, 3, :], 1.0, None, ALU.max))
            link(nc.vector.reciprocal(rdeg[:, :], nt1[:, :]))
            link(tsc(nt1[:, :], info_n[:, 1, :], 1.0, None, ALU.max))
            nc.vector.reciprocal(rcnt[:, :], nt1[:, :]).then_inc(idx_ready, 1)

            dl_cols = dl_col[:, :, :].rearrange("p g k -> p (g k)")

            def make_onehot(layer, i, s, first):
                if not first:
                    v.wait_ge(summed[layer][s], i)
                which(onehot[s], dl_cols, i * 2 + s, W).then_inc(onehot_ready[layer][s], 1)

            def add_sum(layer, i, s, very_first=False):
                v.wait_ge(summed[layer][s], i + 1)
                if s == 1:
                    v.wait_ge(added[layer][0], i + 1)
                elif not very_first:
                    v.wait_ge(added[layer][1], i)
                w = v.value_load(base_row[0:1, ds(i * 2 + s, 1)], min_val=0, max_val=NPAD)
                tt(accT[:, ds(w, W)], accT[:, ds(w, W)], p_agg[s][:, 0:W], ALU.add).then_inc(added[layer][s], 1)

            def add_before(layer, i, s, first):
                if s == 1:
                    add_sum(layer, i, 0, first)
                elif not first:
                    add_sum(layer, i - 1, 1)

            def rank(i, s, first, last):
                g = i * 2 + s
                if not first:
                    v.wait_ge(rank_done, i * 2 + s - 1)
                link2 = which(oh_shi[s], s_hi, g, NH)
                which(oh_slo[s], s_lo, g, NH).then_inc(oh_ready, 1)
                v.wait_ge(pre_done, i * 2 + s + 1)
                if s or not first:
                    v.wait_ge(before_ready, i * 4 + 2 * s)
                carried = before[1 - s][:, K:K + 1, :]
                copy(before[s][:, 0:1, :], carried).then_inc(before_ready, 1)
                tt(before[s][:, 1:K + 1, :], p_pre[0:NH, :].rearrange("p (t l) -> p t l", l=NH),
                   carried.to_broadcast([NH, K, NH]), ALU.add).then_inc(before_ready, 1)
                v.wait_ge(eq_done, i * 2 + s + 1)
                tt(same[:, :, :], p_eq[:, :].rearrange("p (k e) -> p k e", e=P),
                   tri[:, :].unsqueeze(1).to_broadcast([P, K, P]), ALU.mult).then_inc(same_ready, 1)
                v.wait_ge(rank_done, i * 2 + s + 1)
                tt(picked[:, :, :], p_rank[:, :].rearrange("p (k l) -> p k l", l=NH), oh_slo[s][:, :, :],
                   ALU.mult).then_inc(picked_ready, 1)
                v.wait_ge(picked_ready, i * 2 + s + 1)
                nc.vector.tensor_reduce(pos_f[:, :], picked[:, :, :], axis=AX.X, op=ALU.add).then_inc(pos_f_ready, 1)
                v.wait_ge(acc_zero, 1)
                v.wait_ge(pos_f_ready, i * 2 + s + 1)
                copy(pos[:, ds(g * K, K)], pos_f[:, :]).then_inc(pos_ready, 1)

            v.wait_ge(acc_zero, 1)

            def both(i, s, first, last):
                make_onehot(0, i, s, first)
                rank(i, s, first, last)
                add_before(0, i, s, first)

            def add_far(layer):
                v.wait_ge(added[layer][0], HALF + 1)
                nc.vector.memset(far_key[:, :], 0.0).then_inc(far_free[layer], 1)
                v.wait_ge(far_free[layer], 1)
                with v.If(v.value_load(any_far[0:1, 0:1]) > 0):
                    with v.Fori(1, NG + 1) as g1:
                        v.wait_ge(far_free[layer], g1)
                        copy(far_key[:, :], far_col[:, :, :].rearrange("p g k -> p (g k)")[:, ds((g1 - 1) * K, K)]
                             ).then_inc(far_key_ready[layer], 1)
                        with v.Fori(1, NJ + 1) as c1:
                            n = (g1 - 1) * NJ + c1
                            v.wait_ge(far_key_ready[layer], n + g1 - 1)
                            tt(onehot[0][:, :, :], bc(far_key[:, :], W), iota_w[:, :].unsqueeze(1).to_broadcast([P, K, W]),
                               ALU.is_equal).then_inc(far_onehot[layer], 1)
                            v.wait_ge(far_onehot[layer], n)
                            tsc(far_key[:, :], far_key[:, :], -float(W), None, ALU.add).then_inc(far_key_ready[layer], 1)
                            v.wait_ge(far_summed[layer], n)
                            acc = accT[:, ds((c1 - 1) * W, W)]
                            tt(acc, acc, p_agg[0][:, 0:W], ALU.add).then_inc(far_added[layer], 1)
                            v.wait_ge(far_added[layer], n)
                        v.wait_ge(far_key_ready[layer], g1 * (NJ + 1))
                        nc.vector.memset(any_row[:, 1:2], 0.0).then_inc(far_free[layer], 1)
                nc.vector.memset(any_row[:, 2:3], 0.0).then_inc(sums_ready[layer], 1)

            over_chunks(v, both)
            add_sum(0, HALF, 0)
            add_far(0)

            def z_finish(layer):
                def step(j, first):
                    v.wait_ge(z_c[layer], j + 1)
                    stt(h_sb[:, ds(j, 1), :].rearrange("p o f -> p (o f)"), p_rank[:, 0:D], rdeg[:, ds(j, 1)], t_z[:, :],
                        ALU.mult, ALU.add).then_inc(z_done[layer], 1)
                return step

            over_tiles(v, z_finish(0))
            v.wait_ge(z_done[0], NJ)
            link(nc.vector.memset(accT[:, :], 0.0))
            link(tsc(h_sb[:, :, :], h_sb[:, :, :], 0.0, None, ALU.max))
            v.wait_ge(table_out[0], 32)
            split_parts()

            v.wait_ge(flags_in, 16)
            link(tsc(keep[:, 0, :], is_start[:, :], -2.0, 1.0, ALU.mult, ALU.add))
            link(tsc(keep[:, 0, :], keep[:, 0, :], FMAX, None, ALU.mult))
            link(tsc(keep[:, 1, :], is_start[:, :], -1.0, 1.0, ALU.mult, ALU.add))
            link(tsc(seg_t[:, :], tcol[:, :], -float(TP), None, ALU.add))
            link(tt(seg_t[:, :], seg_t[:, :], is_start[:, :], ALU.mult))
            link(nc.vector.tensor_reduce(first_t[:, :], seg_t[:, :], axis=AX.X, op=ALU.min))
            link(tsc(first_t[:, :], first_t[:, :], float(TP), None, ALU.add))
            link(tsc(whole[:, :], first_t[:, :], float(TP), None, ALU.is_equal))
            link(tsc(diag[:, :], ident[:, :], whole[:, 0:1], None, ALU.mult))
            link(tsc(fix_f[:, 0:1], first_t[:, :], 0.0, None, ALU.is_gt))
            link(tt(fix_f[:, 1:2], first_t[:, :], pdump[:, 1:2], ALU.add))
            link(tt(fix_f[:, 2:3], fix_f[:, 1:2], pdump[:, 0:1], ALU.subtract))
            link(tt(fix_f[:, 3:4], fix_f[:, 2:3], fix_f[:, 0:1], ALU.mult))
            link(tt(fix_idx[:, :], fix_f[:, 3:4], pdump[:, 0:1], ALU.add))
            nc.vector.memset(fix_f[:, 0:1], 0.0).then_inc(idx_ready, 1)

            per = 2 * K

            def run(i, s, first, last):
                g = i * 2 + s
                for c in range(2):
                    copy(gate[s][:, c, :], keep[:, c, ds(g * K, K)]).then_inc(gate_ready, 1)
                v.wait_ge(sorted_in[s], (i + 1) * 16)
                if not first:
                    v.wait_ge(run_out[s], i * 16)
                v.wait_ge(gate_ready, i * 4 + 2 * s + 2)
                for k in range(K):
                    old = run_sb[s][:, k - 1, :] if k else run_sb[1 - s][:, K - 1, :]
                    for c, (o0, o1) in enumerate(((ALU.min, ALU.max), (ALU.mult, ALU.add))):
                        if k or s or not first:
                            v.wait_ge(run_step, i * (2 * per) + s * per + 2 * k + c - 1)
                        n = stt(run_sb[s][:, k, c * D:(c + 1) * D], old[:, c * D:(c + 1) * D],
                                gate[s][:, c, k:k + 1], sorted_sb[s][:, k, :], o0, o1).then_inc(run_step, 1)
                v.wait_ge(run_step, i * (2 * per) + s * per + per)
                copy(gate[s][:, 0, 0:1], gate[s][:, 0, 1:2]).then_inc(run_done[s], 1)

            def both2(i, s, first, last):
                make_onehot(1, i, s, first)
                run(i, s, first, last)
                add_before(1, i, s, first)

            over_chunks(v, both2)
            add_sum(1, HALF, 0)
            add_far(1)
            copy(tail[:, :], run_sb[0][:, K - 1, :]).then_inc(tails_ready, 2)
            v.wait_ge(tailsT, 1)
            link(tsc(whole_row[:, 0, :], p_misc[:, 0:P], 2.0, -1.0, ALU.mult, ALU.add))
            link(tsc(whole_row[:, 0, :], whole_row[:, 0, :], FMAX, None, ALU.mult))
            link(copy(whole_row[:, 1, :], p_misc[:, 0:P]))
            nc.vector.memset(carry[:, 0, 0:1], -FMAX).then_inc(carry_ready, 1)
            nc.vector.memset(carry[:, 1, 0:1], 0.0).then_inc(carry_ready, 1)
            nc.vector.tensor_tensor_scan(carry[:, 0, 1:P + 1], whole_row[:, 0, :], p_misc[:, P:2 * P], -FMAX, ALU.min, ALU.max).then_inc(carry_ready, 1)
            nc.vector.tensor_tensor_scan(carry[:, 1, 1:P + 1], whole_row[:, 1, :], p_misc[:, 2 * P:3 * P], 0.0, ALU.mult, ALU.add).then_inc(carry_ready, 1)
            v.wait_ge(fix_in, 16)
            v.wait_ge(carry_back, 1)
            tt(fixed[:, 0:D], fix_rows[:, 0:D], p_eq[:, 0:D], ALU.max).then_inc(fixed_ready, 1)
            tt(fixed[:, D:2 * D], fix_rows[:, D:2 * D], p_eq[:, D:2 * D], ALU.add).then_inc(fixed_ready, 1)
            over_tiles(v, z_finish(1))
            v.wait_ge(z_done[1], NJ)
            link(tsc(h_sb[:, :, :], h_sb[:, :, :], 0.0, None, ALU.max))
            link(tt(x_sb[:, :, :], x_sb[:, :, :], h_sb[:, :, :], ALU.add))
            layernorm_relu(2)
            tt(x_sb[:, :, :], x_sb[:, :, :], h_sb[:, :, :], ALU.add).then_inc(ln2_ready, 1)
            v.wait_ge(ln2_ready, 1)

            def finish(j, first):
                v.wait_ge(m_out, j + 1)
                tt(y_sb[:, ds(j, 1), :].rearrange("p o f -> p (o f)"), p_pre[:, 0:D],
                   x_sb[:, ds(j, 1), :].rearrange("p o f -> p (o f)"), ALU.add).then_inc(y_ready, 1)

            over_tiles(v, finish)


_INS = ["x", "src", "dst", "edge_attr_128", "L0_gnn_W1", "L0_gnn_b1", "L0_gnn_W2", "L0_gnn_b2",
        "L1_gnn_u", "L1_gnn_W1", "L1_gnn_b1", "L1_gnn_W2", "L1_gnn_b2"]


def kernel(**inputs):
    import numpy as np
    import concourse.bacc as bacc
    from concourse import mybir as mb
    from concourse.bass_utils import run_bass_kernel_spmd

    nc = bacc.Bacc("TRN2", target_bir_lowering=False, num_devices=1)
    arrays, args = {}, []
    for name in _INS:
        a = np.ascontiguousarray(inputs[name])
        arrays[f"in_{name}"] = a
        args.append(nc.dram_tensor(f"in_{name}", a.shape, mb.dt.from_np(a.dtype), kind="ExternalInput").ap())
    args.append(nc.dram_tensor("out_x", (N_NODES, D), mb.dt.float32, kind="ExternalOutput").ap())
    f32, b16 = mb.dt.float32, mb.dt.bfloat16
    table = [nc.dram_tensor(f"table{n}", (N_NODES, 3 * D), b16).ap() for n in range(2)]
    sorted_rows = nc.dram_tensor("sorted_rows", (E_PAD, D), f32).ap()
    flags = nc.dram_tensor("flags", (E_PAD + 4096, 1), f32).ap()
    running = nc.dram_tensor("running", (R_ZERO + 1, 2 * D), f32).ap()
    node_scr = nc.dram_tensor("node_scr", (4, NH * NH), f32).ap()
    gnn(nc, *args, table, sorted_rows, flags, running, node_scr)
    r = run_bass_kernel_spmd(nc, [arrays], core_ids=[0])
    return r.results[0]["out_x"]
```

```python
import concourse.bass as bass
from concourse import mybir
from contextlib import ExitStack

P = 128
N_NODES = 3125
D = 128
HID = 512
N_EDGES = 50000
K = 8
GE = K * P
NG = -(-N_EDGES // GE)
TP = NG * K
E_PAD = TP * P
NJ = -(-N_NODES // P)
N_LAST = N_NODES - (NJ - 1) * P
NPAD = NJ * P
W = 128
EP = N_EDGES // P
E_TAIL = N_EDGES - EP * P
NH = 64
PAD_KEY = NH * NH - 1
PAD_DST = 1 << 20
FMAX = 3.4028234663852886e38
EPS = 1e-5
R_DUMP = E_PAD
R_ZERO = E_PAD + P
assert NG % 2 == 1 and EP * P + E_TAIL == N_EDGES and TP - EP == 2
HALF = NG // 2
SCANNED = HALF // 2
FIXED = SCANNED + 2
NQ = 5
Q = NJ // NQ


def over_chunks(eng, step, i0=0, i1=HALF, last=True):
    if i0 == 0:
        step(0, 0, True, False)
        step(0, 1, True, False)
    i0 = max(i0, 1)
    if i0 + 1 == i1:
        step(i0, 0, False, False)
        step(i0, 1, False, False)
    elif i0 < i1:
        with eng.Fori(i0, i1) as i:
            step(i, 0, False, False)
            step(i, 1, False, False)
    if last:
        step(HALF, 0, False, True)


def over_groups(eng, step, n=NQ):
    step(0, True)
    with eng.Fori(1, n) as q:
        step(q, False)


def counted_links(eng, done):
    count = [0]

    def link(ins):
        count[0] += 1
        ins.then_inc(done, 1)
        eng.wait_ge(done, count[0])

    return link


def gnn(nc, x, src, dst, attr, w0a, b0a, w0b, b0b, u, w1, b1, w2, b2, out, table, sorted_rows, flags, running, node_scr, hid_scr):
    fp32, bf16, i32 = mybir.dt.float32, mybir.dt.bfloat16, mybir.dt.int32
    ALU = mybir.AluOpType
    ACT = mybir.ActivationFunctionType
    AX = mybir.AxisListType
    ds = bass.ds

    ctx = ExitStack()
    with ctx:
        def sb(name, shape, dt):
            return ctx.enter_context(nc.sbuf_tensor(name, shape, dt))

        def pb(name, shape, dt):
            return ctx.enter_context(nc.psum_tensor(name, shape, dt))

        def sem(name):
            return ctx.enter_context(nc.semaphore(name))

        def sem2(name):
            return [sem(f"{name}{s}") for s in range(2)]

        x_sb = sb("x_sb", [P, NJ, D], fp32)
        h_sb = sb("h_sb", [P, NJ, D], fp32)
        tmp = sb("tmp", [P, NJ, D], fp32)
        acc = sb("acc", [P, 2, NPAD + W], fp32)
        agg_mem = sb("agg_mem", [P, NJ * 2 * D], fp32)
        agg = agg_mem[:, :].rearrange("p (j f) -> p j f", j=NJ)
        parts = agg_mem[:, 0:NJ * 3 * D // 2].bitcast(bf16).rearrange("p (j c f) -> p j c f", j=NJ, c=3)
        stat = sb("stat", [P, 4, NJ], fp32)
        iota_w = sb("iota_w", [P, W], fp32)
        tri = sb("tri", [P, P], fp32)
        ident = sb("ident", [P, P], fp32)
        identb = sb("identb", [P, P], bf16)
        ones = sb("ones", [P, P], fp32)
        onesb = sb("onesb", [P, P], bf16)
        zeros = sb("zeros", [P, 424], fp32)
        dump_f = sb("dump_f", [P, 32], fp32)
        pdump = sb("pdump", [P, 2], fp32)
        tcol = sb("tcol", [P, TP], fp32)
        ring = sb("ring", [P, 8 * K * D], fp32)

        def ring_at(n, m, dt=fp32, parts_=P):
            v = ring[0:parts_, n * K * D // 2:(n + m) * K * D // 2]
            return v if dt == fp32 else v.bitcast(dt)

        attr_sb = [ring_at(2 * s, 2).rearrange("p (k f) -> p k f", k=K) for s in range(2)]
        sorted_sb = [ring_at(4 + 2 * s, 2).rearrange("p (k f) -> p k f", k=K) for s in range(2)]
        run_sb = [ring_at(8 + 4 * s, 4).rearrange("p (k f) -> p k f", k=K) for s in range(2)]
        hid_in = [ring_at(8 * s, 5).rearrange("p (j f) -> p j f", j=Q) for s in range(2)]
        src_g, dst_g = [ring_at(2 * s, 2, i32, NG) for s in range(2)]
        srcf_g, dl_g, far_g = [ring_at(4 + 2 * s, 2, fp32, NG) for s in range(3)]
        base_g = sb("base_g", [NG, 1], fp32)
        any_g = sb("any_g", [NG, 1], fp32)
        base_row = sb("base_row", [1, NG], i32)
        any_row = sb("any_row", [1, 4], fp32)
        any_far = sb("any_far", [1, 1], i32)
        far_key = sb("far_key", [P, K], fp32)
        src_col = sb("src_col", [P, NG, K], i32)
        dl_col = sb("dl_col", [P, NG, K], fp32)
        far_col = sb("far_col", [P, NG, K], fp32)
        src_p = sb("src_p", [P, TP], i32)
        ki = sb("ki", [P, TP], i32)
        s_hi = sb("s_hi", [P, TP], fp32)
        s_lo = sb("s_lo", [P, TP], fp32)
        rank_f = sb("rank_f", [P, TP], fp32)
        pos = sb("pos", [P, TP], i32)
        w0 = [sb(f"w0_{n}", [P, 2, D], fp32) for n in range(2)]
        w1_sb = sb("w1_sb", [P, 4, HID], fp32)
        w2_sb = sb("w2_sb", [P, 4, D], fp32)
        b_all = sb("b_all", [P, 3, D], fp32)
        w1u_b1 = sb("w1u_b1", [8, P], fp32)
        w1u_b1T = sb("w1u_b1T", [P, 8], fp32)
        u_sb = sb("u_sb", [1, 1], fp32)
        u_col = sb("u_col", [P, 1], fp32)
        bias1 = sb("bias1", [P, 4], fp32)
        idx = [sb(f"idx{s}", [P, K], i32) for s in range(2)]
        rows = [sb(f"rows{s}", [P, K, 3 * D], bf16) for s in range(2)]
        onehot = [sb(f"onehot{s}", [P, K, W], bf16) for s in range(2)]
        oh_hi = [sb(f"oh_hi{s}", [P, K, NH], bf16) for s in range(2)]
        oh_lo = [sb(f"oh_lo{s}", [P, K, NH], bf16) for s in range(2)]
        hiT_f = [ring_at(10 + 2 * s, 2, fp32, NH) for s in range(2)]
        hiT_b = [ring_at(14 + s, 1, bf16, NH) for s in range(2)]
        same = sb("same", [P, K, P], bf16)
        before = [sb(f"before{s}", [NH, K + 1, NH], fp32) for s in range(2)]
        picked = sb("picked", [P, K, NH], fp32)
        pos_f = sb("pos_f", [P, K], fp32)
        gate = [sb(f"gate{s}", [P, 2, K], fp32) for s in range(2)]
        info = sb("info", [NH, 3, NH], fp32)
        incl = sb("incl", [NH, NH], fp32)
        off = sb("off", [NH, 1], fp32)
        info_r = sb("info_r", [32, 3, P], fp32)
        info_n = sb("info_n", [P, 3, 32], fp32)
        has = sb("has", [P, 32], fp32)
        nt1 = sb("nt1", [P, 32], fp32)
        start_idx = sb("start_idx", [P, 32], i32)
        last_idx = sb("last_idx", [P, 32], i32)
        rcnt = sb("rcnt", [P, 32], fp32)
        is_start = sb("is_start", [P, TP], fp32)
        keep = sb("keep", [P, 2, TP], fp32)
        seg_t = sb("seg_t", [P, TP], fp32)
        first_t = sb("first_t", [P, 1], fp32)
        whole = sb("whole", [P, 1], fp32)
        fix_f = sb("fix_f", [P, 4], fp32)
        fix_idx = sb("fix_idx", [P, 1], i32)
        diag = sb("diag", [P, P], fp32)
        tail = sb("tail", [P, 2 * D], fp32)
        whole_row = sb("whole_row", [P, 2, P], fp32)
        carry = sb("carry", [P, 2, P + 1], fp32)
        fix_rows = sb("fix_rows", [P, 2 * D], fp32)
        fixed = sb("fixed", [P, 2 * D], fp32)
        g_h = sb("g_h", [P, Q, D], fp32)
        g_hT = sb("g_hT", [P, Q, P], fp32)
        g_m = sb("g_m", [P, Q, P], fp32)
        feat = g_h[:, 0:3, :]
        featT = g_hT[:, 0:3, :]
        hid_part = [picked[:, :, :].rearrange("p k l -> p (k l)"),
                    same[:, :, :].rearrange("p k e -> p (k e)").bitcast(fp32)]
        hidT = hid_part

        p_aggs = pb("p_aggs", [P, 1024], fp32)
        p_agg = [p_aggs[:, 512 * s:512 * s + 512] for s in range(2)]
        p_pre = pb("p_pre", [P, 512], fp32)
        p_hT = pb("p_hT", [P, 512], fp32)
        p_hiT = p_hT[:, :].bitcast(bf16)
        p_eq = pb("p_eq", [P, 1024], fp32)
        p_rank = pb("p_rank", [P, 512], fp32)
        p_misc = pb("p_misc", [P, 512], fp32)

        consts_a = sem("consts_a")
        consts = sem("consts")
        memsets = sem("memsets")
        x_in = sem2("x_in")
        e_in = sem("e_in")
        w_in = sem("w_in")
        zero_out = sem("zero_out")
        dve = sem("dve_step")
        centered = sem("centered")
        squared = sem("squared")
        var_ready = sem("var_ready")
        std_ready = sem("std_ready")
        h_ready = sem("h_ready")
        part0 = sem("part0")
        rest1 = sem("rest1")
        part1 = sem("part1")
        parts_ready = sem("parts_ready")
        table_out = sem2("table_out")
        edges_f = sem("edges_f")
        edgesT = sem("edgesT")
        edge_cols = sem("edge_cols")
        acc_zero = sem("acc_zero")
        counted = sem("counted")
        totals = sem("totals")
        offsets = sem("offsets")
        info_ready = sem("info_ready")
        info_out = sem("info_out")
        info_in = sem("info_in")
        infoT = sem("infoT")
        b1T = sem("b1T")
        idx_ready = sem("idx_ready")
        fix_idx_ready = sem("fix_idx_ready")
        idx_staged = [sem2(f"idx_staged{n}_") for n in range(3)]
        idx_first = [sem2(f"idx_first{n}_") for n in range(3)]
        rows_in = [sem2(f"rows_in{n}_") for n in range(2)]
        onehot_ready = [sem2(f"onehot_ready{n}_") for n in range(2)]
        summed = [sem2(f"summed{n}_") for n in range(2)]
        added = [sem2(f"added{n}_") for n in range(2)]
        sums_ready = sem2("sums_ready")
        far_free = sem2("far_free")
        far_staged = sem2("far_staged")
        far_rows = sem2("far_rows")
        far_key_ready = sem2("far_key_ready")
        far_onehot = sem2("far_onehot")
        far_summed = sem2("far_summed")
        far_added = sem2("far_added")
        oh_ready = sem("oh_ready")
        pre_done = sem("pre_done")
        hiT_done = sem("hiT_done")
        hiT_ready = sem("hiT_ready")
        before_ready = sem("before_ready")
        eq_done = sem("eq_done")
        same_ready = sem("same_ready")
        rank_done = sem("rank_done")
        picked_ready = sem("picked_ready")
        rank_ready = sem("rank_ready")
        b_oh_ready = sem("b_oh_ready")
        b_hiT_done = sem("b_hiT_done")
        b_hiT_ready = sem("b_hiT_ready")
        base_done = sem("base_done")
        b_picked = sem("b_picked")
        b_pos_f = sem("b_pos_f")
        pos_ready = sem("pos_ready")
        attr_in = sem2("attr_in")
        scattered = sem2("scattered")
        flags_out = sem("flags_out")
        flags_in = sem("flags_in")
        sorted_in = sem2("sorted_in")
        run_step = sem("run_step")
        run_done = sem2("run_done")
        run_out = sem2("run_out")
        gate_ready = sem("gate_ready")
        tails_ready = sem("tails_ready")
        tailsT = sem("tailsT")
        carry_ready = sem("carry_ready")
        carry_back = sem("carry_back")
        fix_in = sem("fix_in")
        fixed_ready = sem("fixed_ready")
        fix_out = sem("fix_out")
        agg_in = sem("agg_in")
        z_h = sem2("z_h")
        z_T = sem2("z_T")
        z_Tc = sem2("z_Tc")
        z_m = sem("z_m")
        z_mm = sem2("z_mm")
        z_sum = sem("z_sum")
        z_out = sem2("z_out")
        f_ready = sem("f_ready")
        f_T = sem("f_T")
        f_Tc = sem("f_Tc")
        f_hid = sem("f_hid")
        f_part = sem("f_part")
        f_out = sem2("f_out")
        t_m = sem("t_m")
        t_z = sem("t_z")
        t_step = sem("t_step")
        t_xc = sem("t_xc")
        t_sq = sem("t_sq")
        t_var = sem("t_var")
        t_std = sem("t_std")
        t_h = sem("t_h")
        t_hT = sem("t_hT")
        t_hTc = sem("t_hTc")
        hid_got = sem2("hid_got")
        t_hid = sem("t_hid")
        t_added = sem("t_added")
        t_relu = sem("t_relu")
        t_y = sem("t_y")
        y_ready = sem("y_ready")
        y_out = sem("y_out")

        block = ctx.enter_context(nc.Block())

        sorted_v = sorted_rows.rearrange("(p t) f -> p t f", p=P)
        running_v = running[0:E_PAD, :].rearrange("(p t) f -> p t f", p=P)
        attr_v = attr[0:EP * P, :].rearrange("(p t) f -> p t f", p=P)
        PARTS = [(0, 13), (13, NJ)]

        def node_view(a, j0, j1):
            return a[j0 * P:j1 * P, :].rearrange("(j p) f -> p j f", p=P)

        def split(g):
            return g // 2, g % 2

        @block.sync
        def _(sp):
            sp.wait_ge(memsets, 4)
            a1 = PARTS[0][1]
            sp.dma_start(x_sb[:, 0:a1, :], node_view(x, 0, a1)).then_inc(x_in[0], 16)
            sp.dma_start(x_sb[:, a1:NJ - 1, :], node_view(x, a1, NJ - 1)).then_inc(x_in[1], 16)
            sp.dma_start(x_sb[0:N_LAST, NJ - 1, :], x[(NJ - 1) * P:N_NODES, :]).then_inc(x_in[1], 16)
            full = (NG - 1) * GE
            for t, a in ((dst_g, dst), (src_g, src)):
                sp.dma_start(t[0:NG - 1, :], a[0:full].rearrange("(g e) -> g e", e=GE)).then_inc(e_in, 16)
                sp.dma_start(t[NG - 1:NG, 0:N_EDGES - full], a[full:N_EDGES].rearrange("(o e) -> o e", o=1)).then_inc(e_in, 16)
            sp.dma_start(src_p[:, 0:EP], src[0:EP * P].rearrange("(p t) -> p t", p=P)).then_inc(e_in, 16)
            sp.dma_start(src_p[0:E_TAIL, EP:EP + 1], src[EP * P:N_EDGES].rearrange("(p o) -> p o", o=1)).then_inc(e_in, 16)
            sp.wait_ge(consts, 1)
            sp.dma_start(flags.rearrange("(p c) o -> p (c o)", p=P), zeros[:, 0:424]).then_inc(zero_out, 16)
            sp.dma_start(sorted_rows[N_EDGES:E_PAD, :].rearrange("r f -> (r f)").rearrange("(p c) -> p c", p=P),
                         zeros[:, 0:E_PAD - N_EDGES]).then_inc(zero_out, 16)
            sp.dma_start(running[R_DUMP:R_ZERO + 1, :].rearrange("r f -> (r f)").rearrange("(p c) -> p c", p=P),
                         zeros[:, 0:258]).then_inc(zero_out, 16)

            def load_attr(i, s, first, last):
                g = i * 2 + s
                if not first:
                    sp.wait_ge(scattered[s], i * (16 * K))
                if not last:
                    sp.dma_start(attr_sb[s], attr_v[:, ds(g * K, K), :]).then_inc(attr_in[s], 16)
                else:
                    sp.dma_start(attr_sb[s][:, 0:K - 2, :], attr_v[:, EP - K + 2:EP, :]).then_inc(attr_in[s], 16)
                    sp.dma_start(attr_sb[s][0:E_TAIL, K - 2, :], attr[EP * P:N_EDGES, :]).then_inc(attr_in[s], 16)

            sp.wait_ge(edge_cols, 1)
            over_chunks(sp, load_attr, 0, 1, False)
            sp.wait_ge(info_ready, 1)
            sp.dma_start(node_scr.rearrange("k (h l) -> h k l", l=NH), info[:, :, :]).then_inc(info_out, 16)
            sp.wait_ge(info_out, 16)
            sp.dma_start(info_r[:, :, :], node_scr.rearrange("k (j p) -> j k p", p=P)).then_inc(info_in, 16)
            over_chunks(sp, load_attr, 1, HALF, True)
            sp.wait_ge(flags_out, 16 * NJ)
            sp.dma_start(is_start[:, :], flags[0:E_PAD, :].rearrange("(p t) o -> p (t o)", p=P)).then_inc(flags_in, 16)
            sp.wait_ge(scattered[0], 16 * K * (HALF + 1) - 16)
            sp.wait_ge(scattered[1], 16 * K * HALF)
            sp.wait_ge(base_done, NG)

            def store_run(i, s):
                g = i * 2 + s
                sp.wait_ge(run_done[s], i + 1)
                sp.dma_start(running_v[:, ds(g * K, K), :], run_sb[s]).then_inc(run_out[s], 16)

            def load_sorted(i, s, first, last):
                g = i * 2 + s
                if not first:
                    sp.wait_ge(run_done[s], i)
                sp.dma_start(sorted_sb[s], sorted_v[:, ds(g * K, K), :]).then_inc(sorted_in[s], 16)
                if s == 1:
                    store_run(i, 0)
                elif not first:
                    store_run(i - 1, 1)

            over_chunks(sp, load_sorted)
            store_run(HALF, 0)

            sp.wait_ge(run_out[0], 16 * (HALF + 1))
            sp.wait_ge(run_out[1], 16 * HALF)
            sp.wait_ge(f_out[0], 16 * (NJ // 2 + 1))
            sp.wait_ge(f_out[1], 16 * (NJ // 2))
            hid_v = hid_scr.rearrange("j p f -> p j f")
            for q in range(NQ):
                if q >= 2:
                    sp.wait_ge(t_added, Q * (q - 1))
                sp.dma_start(hid_in[q % 2], hid_v[:, q * Q:(q + 1) * Q, :]).then_inc(hid_got[q % 2], 16)
                if q >= 2:
                    sp.wait_ge(y_ready, q - 1)
                    sp.dma_start(node_view(out, (q - 2) * Q, (q - 1) * Q), h_sb[:, (q - 2) * Q:(q - 1) * Q, :]).then_inc(y_out, 16)
            sp.wait_ge(y_ready, NQ - 1)
            sp.dma_start(node_view(out, (NQ - 2) * Q, (NQ - 1) * Q), h_sb[:, (NQ - 2) * Q:(NQ - 1) * Q, :]).then_inc(y_out, 16)
            sp.wait_ge(y_ready, NQ)
            sp.dma_start(node_view(out, (NQ - 1) * Q, NJ - 1), h_sb[:, (NQ - 1) * Q:NJ - 1, :]).then_inc(y_out, 16)
            sp.dma_start(out[(NJ - 1) * P:N_NODES, :], h_sb[0:N_LAST, NJ - 1, :]).then_inc(y_out, 16)
            sp.wait_ge(y_out, 16 * (NQ + 1))

        @block.gpsimd
        def _(pool):
            pool.memset(x_sb[:, NJ - 1, :], 0.0).then_inc(memsets, 1)
            pool.memset(src_g, 0).then_inc(memsets, 1)
            pool.memset(dst_g, PAD_DST).then_inc(memsets, 1)
            pool.memset(src_p[:, EP:TP], PAD_KEY).then_inc(memsets, 1)
            pool.memset(zeros[:, :], 0.0).then_inc(consts, 1)
            pool.memset(ones[:, :], 1.0).then_inc(consts_a, 1)
            pool.memset(ident[:, :], 0.0).then_inc(consts_a, 1)
            pool.memset(identb[:, :], 0.0).then_inc(consts_a, 1)
            pool.wait_ge(consts_a, 3)
            for m in (ident, identb):
                pool.affine_select(out=m[:, :], in_=m[:, :], compare_op=ALU.not_equal, fill=1.0, base=0,
                                   pattern=[[-1, P]], channel_multiplier=1).then_inc(consts, 1)
            pool.affine_select(out=tri[:, :], in_=ones[:, :], compare_op=ALU.is_gt, fill=0.0, base=0,
                               pattern=[[1, P]], channel_multiplier=-1).then_inc(consts, 1)
            pool.iota(iota_w[:, :], pattern=[[1, W]], base=0, channel_multiplier=0,
                      allow_small_or_imprecise_dtypes=True).then_inc(consts, 1)
            pool.iota(dump_f[:, :], pattern=[[P, 32]], base=E_PAD, channel_multiplier=1,
                      allow_small_or_imprecise_dtypes=True).then_inc(consts, 1)
            pool.iota(pdump[:, 0:1], pattern=[[0, 1]], base=R_DUMP, channel_multiplier=1,
                      allow_small_or_imprecise_dtypes=True).then_inc(consts, 1)
            pool.iota(pdump[:, 1:2], pattern=[[0, 1]], base=-1, channel_multiplier=TP,
                      allow_small_or_imprecise_dtypes=True).then_inc(consts, 1)
            pool.iota(tcol[:, :], pattern=[[1, TP]], base=0, channel_multiplier=0,
                      allow_small_or_imprecise_dtypes=True).then_inc(consts, 1)
            pool.memset(onesb[:, :], 1.0).then_inc(consts, 1)
            pool.memset(before[1][:, K, :], 0.0).then_inc(consts, 1)
            pool.memset(acc[:, :, :], 0.0).then_inc(acc_zero, 1)

            def stage(n, i, s, cols, first):
                g = i * 2 + s
                copied = pool.tensor_copy(idx[s][:, :], cols[:, ds(g * K, K)])
                if first:
                    copied.then_inc(idx_first[n][s], 1)
                    pool.wait_ge(idx_first[n][s], 1)
                else:
                    copied.then_inc(idx_staged[n][s], 1)
                    pool.wait_ge(consts, 11)
                    pool.wait_ge(idx_staged[n][s], i)

            src_cols = src_col[:, :, :].rearrange("p g k -> p (g k)")

            def gather(layer):
                def step(i, s, first, last):
                    if not first:
                        pool.wait_ge(acc_zero, 1)
                        pool.wait_ge(summed[layer][s], i)
                    stage(layer, i, s, src_cols, first)
                    for k in range(K):
                        pool.indirect_dma_start(rows[s][:, k, :], None, table[layer][:, :],
                                                bass.IndirectOffsetOnAxis(ap=idx[s][:, k:k + 1], axis=0)
                                                ).then_inc(rows_in[layer][s], 16)
                return step

            def gather_again(layer):
                pool.wait_ge(far_free[layer], 1)
                with pool.If(pool.value_load(any_far[0:1, 0:1]) > 0):
                    with pool.Fori(1, NG + 1) as g1:
                        pool.wait_ge(consts, 11)
                        pool.wait_ge(far_free[layer], g1)
                        pool.tensor_copy(idx[0][:, :], src_cols[:, ds((g1 - 1) * K, K)]).then_inc(far_staged[layer], 1)
                        pool.wait_ge(consts, 11)
                        pool.wait_ge(far_staged[layer], g1)
                        for k in range(K):
                            pool.indirect_dma_start(rows[0][:, k, :], None, table[layer][:, :],
                                                    bass.IndirectOffsetOnAxis(ap=idx[0][:, k:k + 1], axis=0)
                                                    ).then_inc(far_rows[layer], 16)
                    pool.wait_ge(far_rows[layer], NG * 16 * K)

            pool.wait_ge(edge_cols, 1)
            pool.wait_ge(table_out[0], 48)
            over_chunks(pool, gather(0))
            gather_again(0)
            pool.wait_ge(summed[0][0], HALF + 1)
            pool.wait_ge(summed[0][1], HALF)

            def scatter(i, s, first, last):
                if not first:
                    pool.wait_ge(acc_zero, 1)
                    pool.wait_ge(scattered[s], i * (16 * K))
                pool.wait_ge(pos_ready, i * 2 + s + 1)
                pool.wait_ge(attr_in[s], (i + 2 if last else i + 1) * 16)
                stage(2, i, s, pos, first)
                for k in range(K if not last else K - 1):
                    n = E_TAIL if last and k == K - 2 else P
                    pool.indirect_dma_start(sorted_rows[:, :], bass.IndirectOffsetOnAxis(ap=idx[s][0:n, k:k + 1], axis=0),
                                            attr_sb[s][0:n, k, :], None).then_inc(scattered[s], 16)

            over_chunks(pool, scatter)
            pool.wait_ge(zero_out, 48)
            pool.wait_ge(idx_ready, 2)
            for j in range(NJ):
                pool.indirect_dma_start(flags[:, :], bass.IndirectOffsetOnAxis(ap=start_idx[:, j:j + 1], axis=0),
                                        ones[:, 0:1], None).then_inc(flags_out, 16)
            pool.wait_ge(scattered[0], 16 * K * (HALF + 1) - 16)
            pool.wait_ge(scattered[1], 16 * K * HALF)
            pool.wait_ge(table_out[1], 48)
            over_chunks(pool, gather(1), 0, FIXED, False)
            pool.wait_ge(run_out[0], 16 * (HALF + 1))
            pool.wait_ge(run_out[1], 16 * HALF)
            pool.wait_ge(fix_idx_ready, 1)
            pool.indirect_dma_start(fix_rows[:, :], None, running[:, :],
                                    bass.IndirectOffsetOnAxis(ap=fix_idx[:, 0:1], axis=0)).then_inc(fix_in, 16)
            over_chunks(pool, gather(1), FIXED, FIXED + 1, False)
            pool.wait_ge(fixed_ready, 2)
            pool.indirect_dma_start(running[:, :], bass.IndirectOffsetOnAxis(ap=fix_idx[:, 0:1], axis=0),
                                    fixed[:, :], None).then_inc(fix_out, 16)
            pool.wait_ge(fix_out, 16)
            for j in range(NJ):
                pool.indirect_dma_start(agg[:, j, :], None, running[:, :],
                                        bass.IndirectOffsetOnAxis(ap=last_idx[:, j:j + 1], axis=0)).then_inc(agg_in, 16)
            over_chunks(pool, gather(1), FIXED + 1, HALF, True)
            gather_again(1)

        @block.scalar
        def _(act):
            for n, w in enumerate((w0a, w0b)):
                act.dma_start(w0[n][:, :, :], w.rearrange("(k p) n -> p k n", p=P)).then_inc(w_in, 16)
            for n, b in enumerate((b0a, b0b, b2)):
                act.dma_start(b_all[:, n, :], b.rearrange("(o n) -> o n", o=1).to_broadcast([P, D])).then_inc(w_in, 16)
            act.dma_start(w1_sb[:, :, :], w1[0:HID, :].rearrange("(k p) n -> p k n", p=P)).then_inc(w_in, 16)
            act.dma_start(w2_sb[:, :, :], w2.rearrange("(k p) n -> p k n", p=P)).then_inc(w_in, 16)
            act.dma_start(u_sb[:, :], u[0:1, :]).then_inc(w_in, 16)
            act.dma_start(w1u_b1[0:4, :], w1[HID, :].rearrange("(c p) -> c p", p=P)).then_inc(w_in, 16)
            act.dma_start(w1u_b1[4:8, :], b1.rearrange("(c p) -> c p", p=P)).then_inc(w_in, 16)

            for n, (j0, j1) in enumerate(PARTS):
                act.wait_ge(centered, n + 1)
                act.activation(tmp[:, j0:j1, :], h_sb[:, j0:j1, :], ACT.Square).then_inc(squared, 1)
            for n, (j0, j1) in enumerate(PARTS):
                act.wait_ge(var_ready, n + 1)
                act.activation(stat[:, 2, j0:j1], stat[:, 1, j0:j1], ACT.Sqrt).then_inc(std_ready, 1)

            def parts_and_table(layer):
                for n, (j0, j1) in enumerate(PARTS):
                    act.wait_ge(h_ready, 2 * layer + n + 1)
                    act.activation(parts[:, j0:j1, 0, :], h_sb[:, j0:j1, :], ACT.Copy).then_inc(part0, 1)
                for n, (j0, j1) in enumerate(PARTS):
                    act.wait_ge(rest1, 2 * layer + n + 1)
                    act.activation(parts[:, j0:j1, 1, :], tmp[:, j0:j1, :], ACT.Copy).then_inc(part1, 1)
                v = parts.rearrange("p j c f -> p j (c f)")
                a1 = PARTS[0][1]
                act.wait_ge(parts_ready, 2 * layer + 1)
                act.dma_start(node_view(table[layer], 0, a1), v[:, 0:a1, :]).then_inc(table_out[layer], 16)
                act.wait_ge(parts_ready, 2 * layer + 2)
                act.dma_start(node_view(table[layer], a1, NJ - 1), v[:, a1:NJ - 1, :]).then_inc(table_out[layer], 16)
                act.dma_start(table[layer][(NJ - 1) * P:N_NODES, :], v[0:N_LAST, NJ - 1, :]).then_inc(table_out[layer], 16)

            parts_and_table(0)

            def rank_copies(i, s, first, last):
                act.wait_ge(hiT_done, i * 2 + s + 1)
                if not first:
                    act.wait_ge(rank_done, i * 2 + s - 1)
                act.activation(hiT_f[s], p_hiT[0:NH, :], ACT.Copy).then_inc(hiT_ready, 1)
                act.activation(hiT_b[s], p_hiT[0:NH, :], ACT.Copy).then_inc(hiT_ready, 1)

            over_chunks(act, rank_copies)

            def base_copies(i, s, first, last):
                act.wait_ge(b_hiT_done, i * 2 + s + 1)
                if not first:
                    act.wait_ge(base_done, i * 2 + s - 1)
                act.activation(hiT_f[s], p_hiT[0:NH, :], ACT.Copy).then_inc(b_hiT_ready, 1)

            act.wait_ge(rank_done, NG)
            over_chunks(act, base_copies)

            def z_copies(n):
                def step(q, first):
                    if not first:
                        act.wait_ge(z_T[n], q)
                    act.activation(g_h[:, :, :], h_sb[:, ds(q * Q, Q), :], ACT.Copy).then_inc(z_h[n], 1)
                    act.wait_ge(z_T[n], q + 1)
                    if not first:
                        act.wait_ge(z_mm[n], q)
                    act.activation(g_hT[:, :, :].rearrange("p j n -> p (j n)"), p_eq[:, 0:Q * P], ACT.Copy).then_inc(z_Tc[n], 1)
                return step

            over_groups(act, z_copies(0))
            parts_and_table(1)
            act.wait_ge(z_mm[0], NQ)
            over_groups(act, z_copies(1))

            act.wait_ge(agg_in, 16 * NJ)
            act.wait_ge(idx_ready, 2)

            def hid_copies(i, s, first):
                j = i * 2 + s
                one = ds(j, 1)
                if s or not first:
                    act.wait_ge(f_T, j)
                for c, (f0, scale) in enumerate(((D, 1.0), (0, 1.0), (D, rcnt[:, one]))):
                    act.activation(feat[:, c, :], agg[:, one, f0:f0 + D].rearrange("p o f -> p (o f)"), ACT.Copy,
                                   scale=scale).then_inc(f_ready, 1)
                act.wait_ge(f_T, j + 1)
                if s or not first:
                    act.wait_ge(f_hid, j)
                act.activation(featT.rearrange("p k n -> p (k n)"), p_misc[:, 0:3 * P], ACT.Copy).then_inc(f_Tc, 1)
                act.wait_ge(f_hid, j + 1)
                if not first:
                    act.wait_ge(f_out[s], i * 16)
                for c in range(4):
                    act.activation(hid_part[s][:, c * P:(c + 1) * P], p_rank[:, c * P:(c + 1) * P], ACT.Identity,
                                   bias=bias1[:, c:c + 1]).then_inc(f_part, 1)
                act.wait_ge(f_part, j * 4 + 4)
                act.dma_start(hid_scr[ds(j, 1), :, :].rearrange("o p f -> p (o f)"), hid_part[s]).then_inc(f_out[s], 16)

            hid_copies(0, 0, True)
            hid_copies(0, 1, True)
            with act.Fori(1, NJ // 2) as i:
                hid_copies(i, 0, False)
                hid_copies(i, 1, False)
            hid_copies(NJ // 2, 0, False)

            def tail_norm(q):
                act.wait_ge(t_xc, q + 1)
                act.activation(tmp[:, q * Q:(q + 1) * Q, :], h_sb[:, q * Q:(q + 1) * Q, :], ACT.Square).then_inc(t_sq, 1)
                act.wait_ge(t_var, q + 1)
                act.activation(stat[:, 2, q * Q:(q + 1) * Q], stat[:, 1, q * Q:(q + 1) * Q], ACT.Sqrt).then_inc(t_std, 1)

            def tail_turn(q):
                act.wait_ge(t_hT, q + 1)
                if q:
                    act.wait_ge(t_hid, Q * q)
                act.activation(g_hT[:, :, :].rearrange("p j n -> p (j n)"), p_eq[:, 0:Q * P], ACT.Copy).then_inc(t_hTc, 1)

            def tail_relu(n):
                act.wait_ge(t_added, n + 1)
                act.activation(hidT[n % 2], hidT[n % 2], ACT.Relu).then_inc(t_relu, 1)

            tail_norm(0)
            for q in range(NQ):
                tail_turn(q)
                for t in range(Q):
                    tail_relu(q * Q + t)
                    if t == 1 and q + 1 < NQ:
                        tail_norm(q + 1)

        @block.tensor
        def _(pe):
            mm = nc.tensor.matmul
            pe.wait_ge(consts, 11)
            pe.wait_ge(edges_f, 3)
            for k in range(K):
                nc.tensor.transpose(p_misc[:, k * NG:(k + 1) * NG], dl_g[:, k * P:(k + 1) * P], ident[0:NG, 0:NG]).then_inc(edgesT, 1)
            for k in range(K):
                nc.tensor.transpose(p_rank[:, k * NG:(k + 1) * NG], srcf_g[:, k * P:(k + 1) * P], ident[0:NG, 0:NG]).then_inc(edgesT, 1)
            for k in range(K):
                nc.tensor.transpose(p_agg[0][:, k * NG:(k + 1) * NG], far_g[:, k * P:(k + 1) * P], ident[0:NG, 0:NG]).then_inc(edgesT, 1)
            nc.tensor.transpose(p_pre[0:1, 64:64 + NG], any_g[:, :], ident[0:NG, 0:NG]).then_inc(edgesT, 1)
            nc.tensor.transpose(p_pre[0:1, 0:NG], base_g[:, :], ident[0:NG, 0:NG]).then_inc(edgesT, 1)
            pe.wait_ge(w_in, 16 * 10)
            nc.tensor.transpose(p_eq[:, 0:8], w1u_b1[:, :], ident[0:8, 0:8])
            mm(p_eq[:, 8:9], ones[0:1, :], u_sb[:, :], start=True, stop=True).then_inc(b1T, 1)
            pe.wait_ge(edge_cols, 2)

            def sums(layer, s):
                for k in range(K):
                    for c in range(3):
                        n = mm(p_agg[s][:, 0:W], rows[s][:, k, c * D:(c + 1) * D], onehot[s][:, k, :],
                               start=(k == 0 and c == 0), stop=(k == K - 1 and c == 2))
                if layer == 0:
                    for k in range(K):
                        n = mm(p_agg[s][:, W:2 * W], onesb[:, :], onehot[s][:, k, :], start=(k == 0), stop=(k == K - 1))
                return n

            def sum_rows(layer):
                def step(i, s, first, last):
                    pe.wait_ge(rows_in[layer][s], (i + 1) * (16 * K))
                    pe.wait_ge(onehot_ready[layer][s], i + 1)
                    if not first:
                        pe.wait_ge(added[layer][s], i)
                    sums(layer, s).then_inc(summed[layer][s], 1)
                return step

            def sum_far(layer):
                pe.wait_ge(far_free[layer], 1)
                with pe.If(pe.value_load(any_far[0:1, 0:1]) > 0):
                    with pe.Fori(1, NG + 1) as g1:
                        with pe.Fori(1, NJ + 1) as c1:
                            pe.wait_ge(consts, 11)
                            pe.wait_ge(far_rows[layer], g1 * (16 * K))
                            pe.wait_ge(far_onehot[layer], (g1 - 1) * NJ + c1)
                            sums(layer, 0).then_inc(far_summed[layer], 1)

            def rank_open(i, s, first, last):
                pe.wait_ge(oh_ready, i * 2 + s + 1)
                if s or not first:
                    pe.wait_ge(before_ready, i * 4 + 2 * s)
                for k in range(K):
                    n = mm(p_pre[0:NH, k * NH:K * NH].rearrange("p (t l) -> p t l", l=NH), oh_hi[s][:, k, :],
                           oh_lo[s][:, k:k + 1, :].to_broadcast([P, K - k, NH]), start=(k == 0), stop=(k == K - 1))
                n.then_inc(pre_done, 1)
                if s or not first:
                    pe.wait_ge(consts, 11)
                    pe.wait_ge(hiT_ready, i * 4 + 2 * s)
                for k in range(K):
                    n = nc.tensor.transpose(p_hiT[0:NH, k * P:(k + 1) * P], oh_hi[s][:, k, :], identb[:, :])
                n.then_inc(hiT_done, 1)

            def rank_same(i, s, first, last):
                pe.wait_ge(hiT_ready, i * 4 + 2 * s + 2)
                if s or not first:
                    pe.wait_ge(same_ready, i * 2 + s)
                for k in range(K):
                    n = mm(p_eq[:, k * P:(k + 1) * P], hiT_b[s][:, k * P:(k + 1) * P], hiT_b[s][:, k * P:(k + 1) * P],
                           start=True, stop=True)
                n.then_inc(eq_done, 1)

            def rank_close(i, s, first):
                pe.wait_ge(same_ready, i * 2 + s + 1)
                pe.wait_ge(before_ready, i * 4 + 2 * s + 2)
                if s or not first:
                    pe.wait_ge(picked_ready, i * 2 + s)
                for k in range(K):
                    mm(p_rank[:, k * NH:(k + 1) * NH], hiT_f[s][:, k * P:(k + 1) * P], before[s][:, k, :], start=True, stop=False)
                    n = mm(p_rank[:, k * NH:(k + 1) * NH], same[:, k, :], oh_lo[s][:, k, :], start=False, stop=True)
                n.then_inc(rank_done, 1)

            agg0 = sum_rows(0)

            def both(i, s, first, last):
                rank_open(i, s, first, last)
                if s:
                    rank_close(i, 0, first)
                elif not first:
                    rank_close(i - 1, 1, False)
                rank_same(i, s, first, last)
                agg0(i, s, first, last)

            over_chunks(pe, both)
            rank_close(HALF, 0, False)
            sum_far(0)
            pe.wait_ge(totals, 1)
            mm(p_pre[0:NH, 0:1], tri[0:NH, 0:NH], incl[:, NH - 1:NH], start=True, stop=True).then_inc(offsets, 1)
            pe.wait_ge(info_ready, 1)

            def base_look(i, s, first):
                pe.wait_ge(b_hiT_ready, i * 2 + s + 1)
                if s or not first:
                    pe.wait_ge(b_picked, i * 2 + s)
                for k in range(K):
                    n = mm(p_rank[:, k * NH:(k + 1) * NH], hiT_f[s][:, k * P:(k + 1) * P], info[:, 0, :], start=True, stop=True)
                n.then_inc(base_done, 1)

            def base(i, s, first, last):
                pe.wait_ge(b_oh_ready, i * 2 + s + 1)
                if s:
                    base_look(i, 0, first)
                elif not first:
                    base_look(i - 1, 1, False)
                for k in range(K):
                    n = nc.tensor.transpose(p_hiT[0:NH, k * P:(k + 1) * P], oh_hi[s][:, k, :], identb[:, :])
                n.then_inc(b_hiT_done, 1)

            over_chunks(pe, base)
            base_look(HALF, 0, False)
            pe.wait_ge(info_in, 16)
            for k in range(3):
                nc.tensor.transpose(p_misc[:, 32 * k:32 * k + 32], info_r[:, k, :], ident[0:32, 0:32]).then_inc(infoT, 1)

            def z_mms(n):
                def step(q, first):
                    pe.wait_ge(z_h[n], q + 1)
                    if not first:
                        pe.wait_ge(z_Tc[n], q)
                    for t in range(Q):
                        last = nc.tensor.transpose(p_eq[:, t * P:(t + 1) * P], g_h[:, t, :], ident[:, :])
                    last.then_inc(z_T[n], 1)
                    pe.wait_ge(z_Tc[n], q + 1)
                    if n == 0:
                        pe.wait_ge(z_m, q + 1)
                    if not first:
                        pe.wait_ge(z_out[n], q)
                    for t in range(Q):
                        last = mm(p_aggs[:, t * P:(t + 1) * P], g_hT[:, t, :], w0[n][:, 0, :], start=True, stop=(n == 1))
                        if n == 0:
                            last = mm(p_aggs[:, t * P:(t + 1) * P], g_m[:, t, :], w0[n][:, 1, :], start=False, stop=True)
                    last.then_inc(z_mm[n], 1)
                return step

            over_groups(pe, z_mms(0))
            pe.wait_ge(z_out[0], NQ)
            over_groups(pe, z_mms(1))
            pe.wait_ge(z_out[1], NQ)
            over_chunks(pe, sum_rows(1), 0, FIXED, False)
            pe.wait_ge(tails_ready, 1)
            mm(p_misc[:, 0:P], ones[:, :], diag[:, :], start=True, stop=True)
            for c in range(2):
                n = nc.tensor.transpose(p_misc[:, (c + 1) * P:(c + 2) * P], tail[:, c * D:(c + 1) * D], ident[:, :])
            n.then_inc(tailsT, 1)
            pe.wait_ge(carry_ready, 4)
            for c in range(2):
                n = nc.tensor.transpose(p_eq[:, c * P:(c + 1) * P], carry[:, c, 0:P], ident[:, :])
            n.then_inc(carry_back, 1)
            over_chunks(pe, sum_rows(1), FIXED, FIXED + 1, False)

            def hid_edges(j, first):
                pe.wait_ge(f_ready, j * 3 + 3)
                if not first:
                    pe.wait_ge(f_Tc, j)
                for c in range(3):
                    n = nc.tensor.transpose(p_misc[:, c * P:(c + 1) * P], feat[:, c, :], ident[:, :])
                n.then_inc(f_T, 1)
                pe.wait_ge(f_Tc, j + 1)
                if not first:
                    pe.wait_ge(f_part, j * 4)
                for c in range(4):
                    for k in range(3):
                        n = mm(p_rank[:, c * P:(c + 1) * P], w1_sb[:, k + 1, c * P:(c + 1) * P], featT[:, k, :],
                               start=(k == 0), stop=(k == 2))
                n.then_inc(f_hid, 1)

            agg1 = sum_rows(1)
            FIRST = FIXED + 1
            agg1(FIRST, 0, False, False)
            hid_edges(0, True)
            agg1(FIRST, 1, False, False)
            hid_edges(1, False)
            with pe.Fori(FIRST + 1, HALF) as i:
                for s in range(2):
                    agg1(i, s, False, False)
                    hid_edges((i - FIRST) * 2 + s, False)
            agg1(HALF, 0, False, True)
            sum_far(1)
            with pe.Fori((HALF - FIRST) * 2, NJ) as j:
                hid_edges(j, False)

            def tail_z(q):
                pe.wait_ge(t_m, q + 1)
                for t in range(Q):
                    n = mm(p_aggs[:, t * P:(t + 1) * P], g_m[:, t, :], w0[1][:, 1, :], start=True, stop=True)
                n.then_inc(t_z, 1)

            def tail_turn(q):
                pe.wait_ge(t_h, q + 1)
                for t in range(Q):
                    n = nc.tensor.transpose(p_eq[:, t * P:(t + 1) * P], g_h[:, t, :], ident[:, :])
                n.then_inc(t_hT, 1)

            hid_bank = [p_rank, p_hT]
            out_bank = [p_pre, p_misc]

            def tail_hid(n):
                if n % Q == 0:
                    pe.wait_ge(t_hTc, n // Q + 1)
                if n >= 2:
                    pe.wait_ge(t_added, n - 1)
                for c in range(4):
                    last = mm(hid_bank[n % 2][:, c * P:(c + 1) * P], w1_sb[:, 0, c * P:(c + 1) * P], g_hT[:, n % Q, :],
                              start=True, stop=True)
                last.then_inc(t_hid, 1)

            def tail_out(n):
                pe.wait_ge(t_relu, n + 1)
                q, t = divmod(n, Q)
                if q and t == 0:
                    pe.wait_ge(y_ready, q)
                o = p_pre[:, t * P:(t + 1) * P] if t < 4 else p_misc[:, 0:P]
                for c in range(4):
                    last = mm(o, hidT[n % 2][:, c * P:(c + 1) * P], w2_sb[:, c, :], start=(c == 0), stop=(c == 3))
                last.then_inc(t_y, 1)

            tail_z(0)
            tail_turn(0)
            for n in range(NJ):
                q, t = divmod(n, Q)
                if t == 0 and q + 1 < NQ:
                    tail_z(q + 1)
                tail_hid(n)
                if n:
                    tail_out(n - 1)
                if t == Q - 1 and q + 1 < NQ:
                    tail_turn(q + 1)
            tail_out(NJ - 1)

        @block.vector
        def _(v):
            tt, tsc, stt, copy = nc.vector.tensor_tensor, nc.vector.tensor_scalar, nc.vector.scalar_tensor_tensor, nc.vector.tensor_copy
            reduce = nc.vector.tensor_reduce
            link = counted_links(v, dve)

            def bc(a, n):
                return a.unsqueeze(2).to_broadcast([a.shape[0], a.shape[1], n])

            for n, (j0, j1) in enumerate(PARTS):
                J = slice(j0, j1)
                v.wait_ge(x_in[n], 16 * (n + 1))
                link(reduce(stat[:, 0, J], x_sb[:, J, :], axis=AX.X, op=ALU.add))
                link(tsc(stat[:, 0, J], stat[:, 0, J], 1.0 / D, None, ALU.mult))
                tt(h_sb[:, J, :], x_sb[:, J, :], bc(stat[:, 0, J], D), ALU.subtract).then_inc(centered, 1)
            for n, (j0, j1) in enumerate(PARTS):
                J = slice(j0, j1)
                v.wait_ge(squared, n + 1)
                link(reduce(stat[:, 1, J], tmp[:, J, :], axis=AX.X, op=ALU.add))
                tsc(stat[:, 1, J], stat[:, 1, J], 1.0 / D, EPS, ALU.mult, ALU.add).then_inc(var_ready, 1)
            for n, (j0, j1) in enumerate(PARTS):
                J = slice(j0, j1)
                v.wait_ge(std_ready, n + 1)
                link(nc.vector.reciprocal(stat[:, 3, J], stat[:, 2, J]))
                stt(h_sb[:, J, :], h_sb[:, J, :], 0.0, bc(stat[:, 3, J], D), ALU.max, ALU.mult).then_inc(h_ready, 1)

            def split_parts(layer):
                for n, (j0, j1) in enumerate(PARTS):
                    v.wait_ge(part0, 2 * layer + n + 1)
                    tt(tmp[:, j0:j1, :], h_sb[:, j0:j1, :], parts[:, j0:j1, 0, :], ALU.subtract).then_inc(rest1, 1)
                for n, (j0, j1) in enumerate(PARTS):
                    v.wait_ge(part1, 2 * layer + n + 1)
                    tt(parts[:, j0:j1, 2, :], tmp[:, j0:j1, :], parts[:, j0:j1, 1, :], ALU.subtract).then_inc(parts_ready, 1)

            split_parts(0)
            v.wait_ge(e_in, 16 * 6)
            link(copy(dl_g, dst_g))
            link(reduce(base_g[:, :], dl_g, axis=AX.X, op=ALU.min))
            copy(srcf_g, src_g).then_inc(edges_f, 1)
            link(tsc(far_g, dl_g, base_g[:, 0:1], float(W), ALU.subtract, ALU.is_lt))
            link(stt(far_g, far_g, float(PAD_DST), dl_g, ALU.mult, ALU.add))
            link(reduce(any_g[:, :], far_g, axis=AX.X, op=ALU.min))
            link(tsc(any_g[:, :], any_g[:, :], float(NPAD), None, ALU.is_lt))
            tsc(dl_g, dl_g, base_g[:, 0:1], None, ALU.subtract).then_inc(edges_f, 2)
            link(tsc(ki[:, :], src_p[:, :], 6, None, ALU.arith_shift_right))
            link(copy(s_hi[:, :], ki[:, :]))
            link(tsc(ki[:, :], src_p[:, :], NH - 1, None, ALU.bitwise_and))
            link(copy(s_lo[:, :], ki[:, :]))
            v.wait_ge(edgesT, 3 * K + 2)
            copy(src_col[:, :, :], p_rank[:, 0:TP].rearrange("p (k g) -> p g k", g=NG)).then_inc(edge_cols, 1)
            link(copy(dl_col[:, :, :], p_misc[:, 0:TP].rearrange("p (k g) -> p g k", g=NG)))
            link(copy(base_row[:, :], p_pre[0:1, 0:NG]))
            link(copy(far_col[:, :, :], p_agg[0][:, 0:TP].rearrange("p (k g) -> p g k", g=NG)))
            link(reduce(any_row[:, 0:1], p_pre[0:1, 64:64 + NG], axis=AX.X, op=ALU.max))
            link(copy(any_far[:, :], any_row[:, 0:1]))
            v.wait_ge(b1T, 1)
            link(copy(u_col[:, :], p_eq[:, 8:9]))
            link(copy(w1u_b1T[:, :], p_eq[:, 0:8]))
            stt(bias1[:, :], w1u_b1T[:, 0:4], u_col[:, 0:1], w1u_b1T[:, 4:8], ALU.mult, ALU.add).then_inc(edge_cols, 1)
            v.wait_ge(consts, 11)

            def which(dst_t, keys, g, n):
                return tt(dst_t[:, :, :], bc(keys[:, ds(g * K, K)], n),
                          iota_w[:, 0:n].unsqueeze(1).to_broadcast([P, K, n]), ALU.is_equal)

            dl_cols = dl_col[:, :, :].rearrange("p g k -> p (g k)")

            def make_onehot(layer, i, s, first):
                if not first:
                    v.wait_ge(summed[layer][s], i)
                which(onehot[s], dl_cols, i * 2 + s, W).then_inc(onehot_ready[layer][s], 1)

            def add_window(layer, at, bank):
                n = 2 if layer == 0 else 1
                a = acc[:, 0:n, ds(at, W)]
                return tt(a, a, bank[:, 0:n * W].rearrange("p (n w) -> p n w", n=n), ALU.add)

            def add_sum(layer, i, s, very_first=False):
                v.wait_ge(summed[layer][s], i + 1)
                if s == 1:
                    v.wait_ge(added[layer][0], i + 1)
                elif not very_first:
                    v.wait_ge(added[layer][1], i)
                at = v.value_load(base_row[0:1, ds(i * 2 + s, 1)], min_val=0, max_val=NPAD)
                add_window(layer, at, p_agg[s]).then_inc(added[layer][s], 1)

            def add_before(layer, i, s, first):
                if s == 1:
                    add_sum(layer, i, 0, first)
                elif not first:
                    add_sum(layer, i - 1, 1)

            def add_far(layer):
                v.wait_ge(added[layer][0], HALF + 1)
                nc.vector.memset(far_key[:, :], 0.0).then_inc(far_free[layer], 1)
                v.wait_ge(far_free[layer], 1)
                with v.If(v.value_load(any_far[0:1, 0:1]) > 0):
                    with v.Fori(1, NG + 1) as g1:
                        v.wait_ge(far_free[layer], g1)
                        copy(far_key[:, :], far_col[:, :, :].rearrange("p g k -> p (g k)")[:, ds((g1 - 1) * K, K)]
                             ).then_inc(far_key_ready[layer], 1)
                        with v.Fori(1, NJ + 1) as c1:
                            n = (g1 - 1) * NJ + c1
                            v.wait_ge(far_key_ready[layer], n + g1 - 1)
                            tt(onehot[0][:, :, :], bc(far_key[:, :], W), iota_w[:, :].unsqueeze(1).to_broadcast([P, K, W]),
                               ALU.is_equal).then_inc(far_onehot[layer], 1)
                            v.wait_ge(far_onehot[layer], n)
                            tsc(far_key[:, :], far_key[:, :], -float(W), None, ALU.add).then_inc(far_key_ready[layer], 1)
                            v.wait_ge(far_summed[layer], n)
                            add_window(layer, (c1 - 1) * W, p_agg[0]).then_inc(far_added[layer], 1)
                            v.wait_ge(far_added[layer], n)
                        v.wait_ge(far_key_ready[layer], g1 * (NJ + 1))
                        nc.vector.memset(any_row[:, 1:2], 0.0).then_inc(far_free[layer], 1)
                nc.vector.memset(any_row[:, 2:3], 0.0).then_inc(sums_ready[layer], 1)

            def source_onehots(g, s, signal):
                which(oh_hi[s], s_hi, g, NH)
                which(oh_lo[s], s_lo, g, NH).then_inc(signal, 1)

            def rank_pick(i, s, first):
                v.wait_ge(rank_done, i * 2 + s + 1)
                tt(picked[:, :, :], p_rank[:, :].rearrange("p (k l) -> p k l", l=NH), oh_lo[s][:, :, :],
                   ALU.mult).then_inc(picked_ready, 1)
                v.wait_ge(picked_ready, i * 2 + s + 1)
                reduce(rank_f[:, ds((i * 2 + s) * K, K)], picked[:, :, :], axis=AX.X, op=ALU.add).then_inc(rank_ready, 1)

            def both(i, s, first, last):
                g = i * 2 + s
                v.wait_ge(pre_done, g + 1)
                if s or not first:
                    v.wait_ge(before_ready, i * 4 + 2 * s)
                carried = before[1 - s][:, K:K + 1, :]
                copy(before[s][:, 0:1, :], carried).then_inc(before_ready, 1)
                tt(before[s][:, 1:K + 1, :], p_pre[0:NH, :].rearrange("p (t l) -> p t l", l=NH),
                   carried.to_broadcast([NH, K, NH]), ALU.add).then_inc(before_ready, 1)
                if s:
                    rank_pick(i, 0, first)
                elif not first:
                    rank_pick(i - 1, 1, False)
                if not last:
                    source_onehots(g + 1, 1 - s, oh_ready)
                v.wait_ge(eq_done, g + 1)
                if s or not first:
                    v.wait_ge(rank_done, g)
                tt(same[:, :, :], p_eq[:, :].rearrange("p (k e) -> p k e", e=P),
                   tri[:, :].unsqueeze(1).to_broadcast([P, K, P]), ALU.mult).then_inc(same_ready, 1)
                if not last:
                    if s == 0:
                        make_onehot(0, i, 1, first)
                    else:
                        make_onehot(0, i + 1, 0, False)
                add_before(0, i, s, first)

            source_onehots(0, 0, oh_ready)
            make_onehot(0, 0, 0, True)
            v.wait_ge(acc_zero, 1)
            over_chunks(v, both)
            rank_pick(HALF, 0, False)
            add_sum(0, HALF, 0)
            add_far(0)

            v.wait_ge(before_ready, 2 * NG)
            link(copy(info[:, 1, :], before[0][:, K, :]))
            nc.vector.tensor_tensor_scan(incl[:, :], ones[0:NH, 0:NH], info[:, 1, :], 0.0, ALU.mult, ALU.add).then_inc(totals, 1)
            v.wait_ge(offsets, 1)
            link(copy(off[:, :], p_pre[0:NH, 0:1]))
            link(tsc(incl[:, :], incl[:, :], off[:, 0:1], None, ALU.add))
            link(tsc(info[:, 2, :], incl[:, :], -1.0, None, ALU.add))
            tt(info[:, 0, :], incl[:, :], info[:, 1, :], ALU.subtract).then_inc(info_ready, 1)

            def place(i, s, first):
                g = i * 2 + s
                v.wait_ge(base_done, g + 1)
                tt(picked[:, :, :], p_rank[:, :].rearrange("p (k l) -> p k l", l=NH), oh_lo[s][:, :, :],
                   ALU.mult).then_inc(b_picked, 1)
                v.wait_ge(b_picked, g + 1)
                reduce(pos_f[:, :], picked[:, :, :], axis=AX.X, op=ALU.add).then_inc(b_pos_f, 1)
                v.wait_ge(b_pos_f, g + 1)
                v.wait_ge(rank_ready, NG)
                tt(pos[:, ds(g * K, K)], pos_f[:, :], rank_f[:, ds(g * K, K)], ALU.add).then_inc(pos_ready, 1)

            def bases(i, s, first, last):
                if s:
                    place(i, 0, first)
                elif not first:
                    place(i - 1, 1, False)
                if not last:
                    source_onehots(i * 2 + s + 1, 1 - s, b_oh_ready)

            source_onehots(0, 0, b_oh_ready)
            over_chunks(v, bases)
            place(HALF, 0, False)
            v.wait_ge(infoT, 3)
            link(copy(info_n[:, :, :], p_misc[:, 0:3 * 32].rearrange("p (k j) -> p k j", j=32)))
            link(tsc(has[:, :], info_n[:, 1, :], 0.0, None, ALU.is_gt))
            link(tt(nt1[:, :], info_n[:, 0, :], dump_f[:, :], ALU.subtract))
            link(tt(nt1[:, :], nt1[:, :], has[:, :], ALU.mult))
            tt(start_idx[:, :], nt1[:, :], dump_f[:, :], ALU.add).then_inc(idx_ready, 1)
            v.wait_ge(idx_ready, 1)
            link(stt(nt1[:, :], info_n[:, 2, :], -float(R_ZERO), has[:, :], ALU.add, ALU.mult))
            link(tsc(last_idx[:, :], nt1[:, :], float(R_ZERO), None, ALU.add))
            link(tsc(nt1[:, :], info_n[:, 1, :], 1.0, None, ALU.max))
            nc.vector.reciprocal(rcnt[:, :], nt1[:, :]).then_inc(idx_ready, 1)

            v.wait_ge(sums_ready[0], 1)
            link(tsc(acc[:, 1, :], acc[:, 1, :], 1.0, None, ALU.max))
            link(nc.vector.reciprocal(acc[:, 1, :], acc[:, 1, :]))

            def mean(q):
                return tt(g_m[:, :, :].rearrange("p j n -> p (j n)"), acc[:, 0, ds(q * (Q * P), Q * P)],
                          acc[:, 1, ds(q * (Q * P), Q * P)], ALU.mult)

            def z0(q, first):
                if not first:
                    v.wait_ge(z_mm[0], q)
                mean(q).then_inc(z_m, 1)
                v.wait_ge(z_mm[0], q + 1)
                tt(tmp[:, ds(q * Q, Q), :], p_aggs[:, 0:Q * D].rearrange("p (j f) -> p j f", j=Q),
                   b_all[:, 0:1, :].to_broadcast([P, Q, D]), ALU.add).then_inc(z_sum, 1)
                v.wait_ge(z_sum, q + 1)
                v.wait_ge(z_T[0], q + 1)
                tsc(h_sb[:, ds(q * Q, Q), :], tmp[:, ds(q * Q, Q), :], 0.0, None, ALU.max).then_inc(z_out[0], 1)

            over_groups(v, z0)
            v.wait_ge(z_out[0], NQ)
            v.wait_ge(table_out[0], 48)
            nc.vector.memset(acc[:, 0, :], 0.0).then_inc(h_ready, 2)
            split_parts(1)

            def z1(q, first):
                v.wait_ge(z_mm[1], q + 1)
                tt(h_sb[:, ds(q * Q, Q), :], p_aggs[:, 0:Q * D].rearrange("p (j f) -> p j f", j=Q),
                   b_all[:, 1:2, :].to_broadcast([P, Q, D]), ALU.add).then_inc(z_out[1], 1)

            over_groups(v, z1)

            v.wait_ge(flags_in, 16)
            link(tsc(keep[:, 0, :], is_start[:, :], -2.0, 1.0, ALU.mult, ALU.add))
            link(tsc(keep[:, 0, :], keep[:, 0, :], FMAX, None, ALU.mult))
            link(tsc(keep[:, 1, :], is_start[:, :], -1.0, 1.0, ALU.mult, ALU.add))
            link(tsc(seg_t[:, :], tcol[:, :], -float(TP), None, ALU.add))
            link(tt(seg_t[:, :], seg_t[:, :], is_start[:, :], ALU.mult))
            link(reduce(first_t[:, :], seg_t[:, :], axis=AX.X, op=ALU.min))
            link(tsc(first_t[:, :], first_t[:, :], float(TP), None, ALU.add))
            link(tsc(whole[:, :], first_t[:, :], float(TP), None, ALU.is_equal))
            link(tsc(diag[:, :], ident[:, :], whole[:, 0:1], None, ALU.mult))
            link(tsc(fix_f[:, 0:1], first_t[:, :], 0.0, None, ALU.is_gt))
            link(tt(fix_f[:, 1:2], first_t[:, :], pdump[:, 1:2], ALU.add))
            link(tt(fix_f[:, 2:3], fix_f[:, 1:2], pdump[:, 0:1], ALU.subtract))
            link(tt(fix_f[:, 3:4], fix_f[:, 2:3], fix_f[:, 0:1], ALU.mult))
            tt(fix_idx[:, :], fix_f[:, 3:4], pdump[:, 0:1], ALU.add).then_inc(fix_idx_ready, 1)
            link(nc.vector.memset(run_sb[1][:, K - 1, 0:D], -FMAX))
            link(nc.vector.memset(run_sb[1][:, K - 1, D:2 * D], 0.0))

            per = 2 * K

            def run(g, s, first):
                c0 = g * 2 + s
                for c in range(2):
                    copy(gate[s][:, c, :], keep[:, c, ds(c0 * K, K)]).then_inc(gate_ready, 1)
                v.wait_ge(sorted_in[s], (g + 1) * 16)
                if not first:
                    v.wait_ge(run_out[s], g * 16)
                v.wait_ge(gate_ready, c0 * 2 + 2)
                for k in range(K):
                    old = run_sb[s][:, k - 1, :] if k else run_sb[1 - s][:, K - 1, :]
                    for c, (o0, o1) in enumerate(((ALU.min, ALU.max), (ALU.mult, ALU.add))):
                        if k or s or not first:
                            v.wait_ge(run_step, c0 * per + 2 * k + c - 1)
                        n = stt(run_sb[s][:, k, c * D:(c + 1) * D], old[:, c * D:(c + 1) * D],
                                gate[s][:, c, k:k + 1], sorted_sb[s][:, k, :], o0, o1).then_inc(run_step, 1)
                v.wait_ge(run_step, c0 * per + per)
                copy(gate[s][:, 0, 0:1], gate[s][:, 0, 1:2]).then_inc(run_done[s], 1)

            def scan_too(i, s, first, last):
                g = i * 2 + s
                make_onehot(1, i, s, first)
                run(g, 0, first and s == 0)
                run(g, 1, first and s == 0)
                add_before(1, i, s, first)

            def sums_only(i, s, first, last):
                make_onehot(1, i, s, first)
                add_before(1, i, s, first)

            over_chunks(v, scan_too, 0, SCANNED, False)
            make_onehot(1, SCANNED, 0, False)
            run(HALF, 0, False)
            copy(tail[:, :], run_sb[0][:, K - 1, :]).then_inc(tails_ready, 1)
            add_before(1, SCANNED, 0, False)
            sums_only(SCANNED, 1, False, False)
            over_chunks(v, sums_only, SCANNED + 1, FIXED, False)
            v.wait_ge(tailsT, 1)
            link(tsc(whole_row[:, 0, :], p_misc[:, 0:P], 2.0, -1.0, ALU.mult, ALU.add))
            link(tsc(whole_row[:, 0, :], whole_row[:, 0, :], FMAX, None, ALU.mult))
            link(copy(whole_row[:, 1, :], p_misc[:, 0:P]))
            nc.vector.memset(carry[:, 0, 0:1], -FMAX).then_inc(carry_ready, 1)
            nc.vector.memset(carry[:, 1, 0:1], 0.0).then_inc(carry_ready, 1)
            nc.vector.tensor_tensor_scan(carry[:, 0, 1:P + 1], whole_row[:, 0, :], p_misc[:, P:2 * P], -FMAX, ALU.min, ALU.max).then_inc(carry_ready, 1)
            nc.vector.tensor_tensor_scan(carry[:, 1, 1:P + 1], whole_row[:, 1, :], p_misc[:, 2 * P:3 * P], 0.0, ALU.mult, ALU.add).then_inc(carry_ready, 1)
            v.wait_ge(fix_in, 16)
            v.wait_ge(carry_back, 1)
            tt(fixed[:, 0:D], fix_rows[:, 0:D], p_eq[:, 0:D], ALU.max).then_inc(fixed_ready, 1)
            tt(fixed[:, D:2 * D], fix_rows[:, D:2 * D], p_eq[:, D:2 * D], ALU.add).then_inc(fixed_ready, 1)
            over_chunks(v, sums_only, FIXED, HALF, True)
            add_sum(1, HALF, 0)
            add_far(1)
            v.wait_ge(sums_ready[1], 1)

            tlink = counted_links(v, t_step)

            def tail_mean(q):
                if q:
                    v.wait_ge(t_z, q)
                mean(q).then_inc(t_m, 1)

            def tail_norm_1(q):
                J = slice(q * Q, (q + 1) * Q)
                v.wait_ge(t_z, q + 1)
                tlink(tt(tmp[:, J, :], p_aggs[:, 0:Q * D].rearrange("p (j f) -> p j f", j=Q), h_sb[:, J, :], ALU.add))
                tlink(stt(x_sb[:, J, :], tmp[:, J, :], 0.0, x_sb[:, J, :], ALU.max, ALU.add))
                tlink(reduce(stat[:, 0, J], x_sb[:, J, :], axis=AX.X, op=ALU.add))
                tlink(tsc(stat[:, 0, J], stat[:, 0, J], 1.0 / D, None, ALU.mult))
                tt(h_sb[:, J, :], x_sb[:, J, :], bc(stat[:, 0, J], D), ALU.subtract).then_inc(t_xc, 1)
                if q + 1 < NQ:
                    tail_mean(q + 1)
                tlink(tt(x_sb[:, J, :], x_sb[:, J, :], b_all[:, 2:3, :].to_broadcast([P, Q, D]), ALU.add))

            def tail_norm_2(q):
                J = slice(q * Q, (q + 1) * Q)
                v.wait_ge(t_sq, q + 1)
                tlink(reduce(stat[:, 1, J], tmp[:, J, :], axis=AX.X, op=ALU.add))
                tsc(stat[:, 1, J], stat[:, 1, J], 1.0 / D, EPS, ALU.mult, ALU.add).then_inc(t_var, 1)
                v.wait_ge(t_std, q + 1)
                tlink(nc.vector.reciprocal(stat[:, 3, J], stat[:, 2, J]))
                if q:
                    v.wait_ge(t_hT, q)
                v.wait_ge(t_xc, q + 1)
                stt(g_h[:, :, :], h_sb[:, J, :], 0.0, bc(stat[:, 3, J], D), ALU.max, ALU.mult).then_inc(t_h, 1)
                v.wait_ge(t_h, q + 1)
                tlink(tt(x_sb[:, J, :], x_sb[:, J, :], g_h[:, :, :], ALU.add))

            hid_bank = [p_rank, p_hT]

            def tail_add(n):
                q, t = divmod(n, Q)
                if t == 0:
                    v.wait_ge(hid_got[q % 2], 16 * (q // 2 + 1))
                v.wait_ge(t_hid, n + 1)
                if n >= 2:
                    v.wait_ge(t_y, n - 1)
                tt(hidT[n % 2], hid_bank[n % 2][:, :], hid_in[q % 2][:, t, :], ALU.add).then_inc(t_added, 1)

            def tail_out(q):
                v.wait_ge(t_y, Q * (q + 1))
                tlink(tt(h_sb[:, q * Q:q * Q + 4, :], p_pre[:, 0:4 * D].rearrange("p (j f) -> p j f", j=4),
                         x_sb[:, q * Q:q * Q + 4, :], ALU.add))
                tt(h_sb[:, q * Q + 4, :], p_misc[:, 0:D], x_sb[:, q * Q + 4, :], ALU.add).then_inc(y_ready, 1)

            tail_mean(0)
            tail_norm_1(0)
            tail_norm_2(0)
            for q in range(NQ):
                for t in range(Q):
                    tail_add(q * Q + t)
                    if t == 0 and q:
                        tail_out(q - 1)
                    if t == 0 and q + 1 < NQ:
                        tail_norm_1(q + 1)
                    if t == 1 and q + 1 < NQ:
                        tail_norm_2(q + 1)
            tail_out(NQ - 1)


_INS = ["x", "src", "dst", "edge_attr_128", "L0_gnn_W1", "L0_gnn_b1", "L0_gnn_W2", "L0_gnn_b2",
        "L1_gnn_u", "L1_gnn_W1", "L1_gnn_b1", "L1_gnn_W2", "L1_gnn_b2"]


def kernel(**inputs):
    import numpy as np
    import concourse.bacc as bacc
    from concourse import mybir as mb
    from concourse.bass_utils import run_bass_kernel_spmd

    nc = bacc.Bacc("TRN2", target_bir_lowering=False, num_devices=1)
    arrays, args = {}, []
    for name in _INS:
        a = np.ascontiguousarray(inputs[name])
        arrays[f"in_{name}"] = a
        args.append(nc.dram_tensor(f"in_{name}", a.shape, mb.dt.from_np(a.dtype), kind="ExternalInput").ap())
    args.append(nc.dram_tensor("out_x", (N_NODES, D), mb.dt.float32, kind="ExternalOutput").ap())
    f32, b16 = mb.dt.float32, mb.dt.bfloat16
    table = [nc.dram_tensor(f"table{n}", (N_NODES, 3 * D), b16).ap() for n in range(2)]
    sorted_rows = nc.dram_tensor("sorted_rows", (E_PAD, D), f32).ap()
    flags = nc.dram_tensor("flags", (E_PAD + 4096, 1), f32).ap()
    running = nc.dram_tensor("running", (R_ZERO + 1, 2 * D), f32).ap()
    node_scr = nc.dram_tensor("node_scr", (3, NH * NH), f32).ap()
    hid_scr = nc.dram_tensor("hid_scr", (NJ, P, HID), f32).ap()
    gnn(nc, *args, table, sorted_rows, flags, running, node_scr, hid_scr)
    r = run_bass_kernel_spmd(nc, [arrays], core_ids=[0])
    return r.results[0]["out_x"]
```

```python
import concourse.bass as bass
from concourse import mybir
from contextlib import ExitStack

P = 128
N_NODES = 3125
D = 128
HID = 512
N_EDGES = 50000
K = 8
GE = K * P
NG = -(-N_EDGES // GE)
TP = NG * K
E_PAD = TP * P
NJ = -(-N_NODES // P)
N_LAST = N_NODES - (NJ - 1) * P
NPAD = NJ * P
W = 128
EP = N_EDGES // P
E_TAIL = N_EDGES - EP * P
NH = 64
PAD_KEY = NH * NH - 1
PAD_DST = 1 << 20
FMAX = 3.4028234663852886e38
EPS = 1e-5
R_DUMP = E_PAD
R_ZERO = E_PAD + 2 * P
assert NG % 2 == 1 and EP * P + E_TAIL == N_EDGES and TP - EP == 2
HALF = NG // 2
SCANNED = HALF * 2 // 3
assert SCANNED % 2 == 0 and 3 * SCANNED == 2 * HALF
FIXED = SCANNED + 1
assert NJ == 4 * (HALF - FIXED - 1) + 1
NQ = 5
Q = NJ // NQ
KH = K // 2
TH = TP // 2


def over_chunks(eng, step, i0=0, i1=HALF, last=True):
    if i0 == 0:
        step(0, 0, True, False)
        step(0, 1, True, False)
    i0 = max(i0, 1)
    if i0 + 1 == i1:
        step(i0, 0, False, False)
        step(i0, 1, False, False)
    elif i0 < i1:
        with eng.Fori(i0, i1) as i:
            step(i, 0, False, False)
            step(i, 1, False, False)
    if last:
        step(HALF, 0, False, True)


def over_groups(eng, step, n=NQ):
    step(0, True)
    with eng.Fori(1, n) as q:
        step(q, False)


def counted_links(eng, done):
    count = [0]

    def link(ins):
        count[0] += 1
        ins.then_inc(done, 1)
        eng.wait_ge(done, count[0])

    return link


def gnn(nc, x, src, dst, attr, w0a, b0a, w0b, b0b, u, w1, b1, w2, b2, out, table, sorted_rows, running, node_scr, hid_scr):
    fp32, bf16, i32 = mybir.dt.float32, mybir.dt.bfloat16, mybir.dt.int32
    ALU = mybir.AluOpType
    ACT = mybir.ActivationFunctionType
    AX = mybir.AxisListType
    ds = bass.ds

    ctx = ExitStack()
    with ctx:
        def sb(name, shape, dt):
            return ctx.enter_context(nc.sbuf_tensor(name, shape, dt))

        def pb(name, shape, dt):
            return ctx.enter_context(nc.psum_tensor(name, shape, dt))

        def sem(name):
            return ctx.enter_context(nc.semaphore(name))

        def sem2(name):
            return [sem(f"{name}{s}") for s in range(2)]

        x_sb = sb("x_sb", [P, NJ, D], fp32)
        h_sb = sb("h_sb", [P, NJ, D], fp32)
        tmp = sb("tmp", [P, NJ, D], fp32)
        acc = sb("acc", [P, 2, NPAD + W], fp32)
        agg_mem = sb("agg_mem", [P, NJ * 2 * D], fp32)
        agg = agg_mem[:, :].rearrange("p (j f) -> p j f", j=NJ)
        parts = agg_mem[:, 0:NJ * 3 * D // 2].bitcast(bf16).rearrange("p (j c f) -> p j c f", j=NJ, c=3)
        stat = sb("stat", [P, 4, NJ], fp32)
        iota_w = sb("iota_w", [P, W], fp32)
        tri = sb("tri", [P, P], fp32)
        ident = sb("ident", [P, P], fp32)
        identb = sb("identb", [P, P], bf16)
        ones = sb("ones", [P, P], fp32)
        onesb = sb("onesb", [P, P], bf16)
        zeros = sb("zeros", [P, 2 * D], fp32)
        bounds = sb("bounds", [P, P + 1], fp32)
        iota_t = sb("iota_t", [P, TP], fp32)
        dump_f = sb("dump_f", [P, 32], fp32)
        pdump = sb("pdump", [P, 4], fp32)
        tcol = sb("tcol", [P, TH], fp32)
        ring = sb("ring", [P, 8 * K * D], fp32)

        def ring_at(n, m, dt=fp32, parts_=P):
            v = ring[0:parts_, n * K * D // 2:(n + m) * K * D // 2]
            return v if dt == fp32 else v.bitcast(dt)

        attr_sb = [ring_at(2 * s, 2).rearrange("p (k f) -> p k f", k=K) for s in range(2)]
        sorted_sb = [ring_at(4 + 2 * s, 2).rearrange("p (h k f) -> p h k f", h=2, k=KH) for s in range(2)]
        run_sb = [ring_at(8 + 4 * s, 4).rearrange("p (h k f) -> p h k f", h=2, k=KH) for s in range(2)]
        hid_in = [ring_at(8 * s, 5).rearrange("p (j f) -> p j f", j=Q) for s in range(2)]
        src_g, dst_g = [ring_at(2 * s, 2, i32, NG) for s in range(2)]
        srcf_g, dl_g, far_g = [ring_at(4 + 2 * s, 2, fp32, NG) for s in range(3)]
        base_g = sb("base_g", [NG, 1], fp32)
        any_g = sb("any_g", [NG, 1], fp32)
        base_row = sb("base_row", [1, NG], i32)
        any_row = sb("any_row", [1, 4], fp32)
        any_far = sb("any_far", [1, 1], i32)
        far_key = sb("far_key", [P, K], fp32)
        src_col = sb("src_col", [P, NG, K], i32)
        dl_col = sb("dl_col", [P, NG, K], fp32)
        far_col = sb("far_col", [P, NG, K], fp32)
        src_p = sb("src_p", [P, TP], i32)
        ki = sb("ki", [P, TP], i32)
        s_hi = sb("s_hi", [P, TP], fp32)
        s_lo = sb("s_lo", [P, TP], fp32)
        rank_f = sb("rank_f", [P, TP], fp32)
        pos = sb("pos", [P, TP], i32)
        w0 = [sb(f"w0_{n}", [P, 2, D], fp32) for n in range(2)]
        w1_sb = sb("w1_sb", [P, 4, HID], fp32)
        w2_sb = sb("w2_sb", [P, 4, D], fp32)
        b_all = sb("b_all", [P, 3, D], fp32)
        w1u_b1 = sb("w1u_b1", [8, P], fp32)
        w1u_b1T = sb("w1u_b1T", [P, 8], fp32)
        u_sb = sb("u_sb", [1, 1], fp32)
        u_col = sb("u_col", [P, 1], fp32)
        bias1 = sb("bias1", [P, 4], fp32)
        idx = [[sb(f"idx{n}_{s}", [P, K], i32) for s in range(2)] for n in range(3)]
        neg_dl = [sb(f"neg_dl{s}", [P, K], fp32) for s in range(2)]
        chunk_mem = [sb(f"chunk_mem{s}", [P, K * 2 * D], fp32) for s in range(2)]
        rows_parts = [m[:, 0:K * 3 * D // 2].bitcast(bf16).rearrange("p (k f) -> p k f", k=K) for m in chunk_mem]
        rows = [rows_parts, [m[:, 0:K * D].rearrange("p (k f) -> p k f", k=K) for m in chunk_mem]]
        onehot = [[m[:, K * 3 * D // 2:K * 2 * D].bitcast(bf16).rearrange("p (k w) -> p k w", k=K) for m in chunk_mem],
                  [m[:, K * D:K * 2 * D].rearrange("p (k w) -> p k w", k=K) for m in chunk_mem]]
        oh_hi = [sb(f"oh_hi{s}", [P, K, NH], bf16) for s in range(2)]
        oh_lo = [sb(f"oh_lo{s}", [P, K, NH], bf16) for s in range(2)]
        hiT_f = [ring_at(10 + 2 * s, 2, fp32, NH) for s in range(2)]
        hiT_b = [ring_at(14 + s, 1, bf16, NH) for s in range(2)]
        same = sb("same", [P, K, P], bf16)
        before = [sb(f"before{s}", [NH, K + 1, NH], fp32) for s in range(2)]
        picked = sb("picked", [P, K, NH], fp32)
        pos_f = sb("pos_f", [P, K], fp32)
        gate = [sb(f"gate{s}", [P, 2, K], fp32) for s in range(2)]
        info = sb("info", [NH, 3, NH], fp32)
        incl = sb("incl", [NH, NH], fp32)
        off = sb("off", [NH, 1], fp32)
        info_r = sb("info_r", [32, 3, P], fp32)
        info_n = sb("info_n", [P, 3, 32], fp32)
        has = sb("has", [P, 32], fp32)
        nt1 = sb("nt1", [P, 32], fp32)
        start_f = sb("start_f", [P, 32], fp32)
        last_idx = sb("last_idx", [P, 32], i32)
        rcnt = sb("rcnt", [P, 32], fp32)
        g_h = sb("g_h", [P, Q, D], fp32)
        g_hT = sb("g_hT", [P, Q, P], fp32)
        g_m = sb("g_m", [P, Q, P], fp32)
        fix_mem = sb("fix_mem", [P, 4 * D], fp32)
        turned = [g_hT[:, :, :].rearrange("p j n -> p (j n)"), ring_at(6, 2)[:, 0:Q * P]]
        start_mem = [m[:, 0:K * D].bitcast(bf16) for m in chunk_mem]
        begun = start_mem[0][:, 0:Q * (P + 1)].rearrange("p (j c) -> p j c", j=Q)
        start_p = start_mem[0][:, Q * (P + 1) + Q:Q * (2 * P + 2)].rearrange("p (j c) -> p j c", j=Q)
        start_t = start_mem[1][:, 0:Q * TP].rearrange("p (j c) -> p j c", j=Q)
        start_in = sb("start_in", [P, 2, Q], fp32)
        is_start = sb("is_start", [P, TP], fp32)
        keep = sb("keep", [P, 2, TP], fp32)
        seg_t = sb("seg_t", [P, TP], fp32)
        first_t = sb("first_t", [P, 2], fp32)
        whole = sb("whole", [P, 2], fp32)
        fix_f = sb("fix_f", [P, 4, 2], fp32)
        fix_idx = sb("fix_idx", [P, 2], i32)
        diag = g_hT[:, 0:2, :]
        tail = g_h[:, 0:4, :].rearrange("p (h c) f -> p h (c f)", h=2)
        whole_row = tmp[:, 0:4, :].rearrange("p (c j) f -> p c (j f)", c=2)
        tail_row = tmp[:, 4:8, :].rearrange("p (c j) f -> p c (j f)", c=2)
        carry = tmp[:, 8:NJ, :].rearrange("p j f -> p (j f)")[:, 0:2 * (2 * P + 2)].rearrange("p (c v) -> p c v", c=2)
        fix_rows = g_m[:, 0:4, :].rearrange("p (h c) f -> p h (c f)", h=2)
        fixed = fix_mem[:, :].rearrange("p (h f) -> p h f", h=2)
        feat = [g_h[:, 0:3, :], fix_mem[:, 0:3 * D].rearrange("p (k f) -> p k f", k=3)]
        featT = [g_hT[:, 0:3, :], g_m[:, 0:3, :]]
        hid_part = [picked[:, :, :].rearrange("p k l -> p (k l)"),
                    same[:, :, :].rearrange("p k e -> p (k e)").bitcast(fp32)]
        hidT = hid_part

        p_aggs = pb("p_aggs", [P, 1024], fp32)
        p_agg = [p_aggs[:, 512 * s:512 * s + 512] for s in range(2)]
        p_pre = pb("p_pre", [P, 512], fp32)
        p_hT = pb("p_hT", [P, 512], fp32)
        p_hiT = p_hT[:, :].bitcast(bf16)
        p_eq = pb("p_eq", [P, 1024], fp32)
        p_rank = pb("p_rank", [P, 512], fp32)
        p_misc = pb("p_misc", [P, 512], fp32)
        p_featT = [p_misc, p_pre]
        p_hid = [p_rank, p_hT]

        consts_a = sem("consts_a")
        consts = sem("consts")
        memsets = sem("memsets")
        x_in = sem2("x_in")
        e_in = sem("e_in")
        w_in = sem("w_in")
        zero_out = sem("zero_out")
        dve = sem("dve_step")
        centered = sem("centered")
        squared = sem("squared")
        var_ready = sem("var_ready")
        std_ready = sem("std_ready")
        h_ready = sem("h_ready")
        part0 = sem("part0")
        rest1 = sem("rest1")
        part1 = sem("part1")
        parts_ready = sem("parts_ready")
        table_out = sem2("table_out")
        src_f = sem("src_f")
        edges_f = sem("edges_f")
        edgesT = sem("edgesT")
        edge_cols = sem("edge_cols")
        acc_zero = sem("acc_zero")
        totals = sem("totals")
        offsets = sem("offsets")
        info_ready = sem("info_ready")
        info_moved = sem("info_moved")
        residual = sem("residual")
        infoT = sem("infoT")
        b1T = sem("b1T")
        idx_ready = sem("idx_ready")
        fix_idx_ready = sem("fix_idx_ready")
        idx_staged = [sem2(f"idx_staged{n}_") for n in range(3)]
        idx_first = [sem2(f"idx_first{n}_") for n in range(3)]
        rows_in = [sem2(f"rows_in{n}_") for n in range(2)]
        onehot_ready = [sem2(f"onehot_ready{n}_") for n in range(2)]
        summed = [sem2(f"summed{n}_") for n in range(2)]
        added = [sem2(f"added{n}_") for n in range(2)]
        sums_ready = sem2("sums_ready")
        far_free = sem2("far_free")
        far_staged = sem2("far_staged")
        far_rows = sem2("far_rows")
        far_key_ready = sem2("far_key_ready")
        far_onehot = sem2("far_onehot")
        far_summed = sem2("far_summed")
        far_added = sem2("far_added")
        oh_ready = sem("oh_ready")
        pre_done = sem("pre_done")
        hiT_done = sem("hiT_done")
        hiT_ready = sem("hiT_ready")
        before_ready = sem("before_ready")
        eq_done = sem("eq_done")
        same_ready = sem("same_ready")
        rank_done = sem("rank_done")
        picked_ready = sem("picked_ready")
        rank_ready = sem("rank_ready")
        b_oh_ready = sem("b_oh_ready")
        b_hiT_done = sem("b_hiT_done")
        b_hiT_ready = sem("b_hiT_ready")
        base_done = sem("base_done")
        b_picked = sem("b_picked")
        b_pos_f = sem("b_pos_f")
        pos_ready = sem("pos_ready")
        attr_in = sem2("attr_in")
        scattered = sem2("scattered")
        start_step = sem("start_step")
        start_onehots = sem("start_onehots")
        starts_found = sem("starts_found")
        sorted_in = sem2("sorted_in")
        run_step = sem("run_step")
        run_done = sem2("run_done")
        run_out = sem2("run_out")
        gate_ready = sem("gate_ready")
        tails_ready = sem("tails_ready")
        tailsT = sem("tailsT")
        carry_ready = sem("carry_ready")
        carry_back = sem("carry_back")
        fix_in = sem("fix_in")
        fixed_ready = sem("fixed_ready")
        fix_out = sem("fix_out")
        agg_in = sem("agg_in")
        z_h = sem2("z_h")
        z_T = sem2("z_T")
        z_Tc = sem2("z_Tc")
        z_m = sem("z_m")
        z_mm = sem2("z_mm")
        z_sum = sem("z_sum")
        z_out = sem2("z_out")
        oh_neg = sem("oh_neg")
        oh_abs = sem("oh_abs")
        f_ready = sem("f_ready")
        f_T = sem("f_T")
        f_Tc = sem("f_Tc")
        f_hid = sem("f_hid")
        f_part = sem("f_part")
        f_out = sem2("f_out")
        t_m = sem("t_m")
        t_z = sem("t_z")
        t_step = sem("t_step")
        t_xc = sem("t_xc")
        t_sq = sem("t_sq")
        t_var = sem("t_var")
        t_std = sem("t_std")
        t_h = sem("t_h")
        t_hT = sem("t_hT")
        t_hTc = sem("t_hTc")
        hid_got = sem2("hid_got")
        t_hid = sem("t_hid")
        t_added = sem("t_added")
        t_relu = sem("t_relu")
        t_y = sem("t_y")
        y_ready = sem("y_ready")
        y_out = sem("y_out")

        block = ctx.enter_context(nc.Block())

        sorted_v = sorted_rows.rearrange("(p h t) f -> p h t f", p=P, h=2)
        running_v = running[0:E_PAD, :].rearrange("(p h t) f -> p h t f", p=P, h=2)
        attr_v = attr[0:EP * P, :].rearrange("(p t) f -> p t f", p=P)
        PARTS = [(0, 13), (13, NJ)]

        def node_view(a, j0, j1):
            return a[j0 * P:j1 * P, :].rearrange("(j p) f -> p j f", p=P)

        def split(g):
            return g // 2, g % 2

        @block.sync
        def _(sp):
            a1 = PARTS[0][1]
            sp.dma_start(x_sb[:, 0:a1, :], node_view(x, 0, a1)).then_inc(x_in[0], 16)
            sp.dma_start(x_sb[:, a1:NJ - 1, :], node_view(x, a1, NJ - 1)).then_inc(x_in[1], 16)
            sp.wait_ge(memsets, 4)
            sp.dma_start(x_sb[0:N_LAST, NJ - 1, :], x[(NJ - 1) * P:N_NODES, :]).then_inc(x_in[1], 16)
            full = (NG - 1) * GE
            for t, a in ((dst_g, dst), (src_g, src)):
                sp.dma_start(t[0:NG - 1, :], a[0:full].rearrange("(g e) -> g e", e=GE)).then_inc(e_in, 16)
                sp.dma_start(t[NG - 1:NG, 0:N_EDGES - full], a[full:N_EDGES].rearrange("(o e) -> o e", o=1)).then_inc(e_in, 16)
            sp.dma_start(src_p[:, 0:EP], src[0:EP * P].rearrange("(p t) -> p t", p=P)).then_inc(e_in, 16)
            sp.dma_start(src_p[0:E_TAIL, EP:EP + 1], src[EP * P:N_EDGES].rearrange("(p o) -> p o", o=1)).then_inc(e_in, 16)
            sp.wait_ge(consts, 1)
            sp.dma_start(sorted_rows[N_EDGES:E_PAD, :].rearrange("r f -> (r f)").rearrange("(p c) -> p c", p=P),
                         zeros[:, 0:E_PAD - N_EDGES]).then_inc(zero_out, 16)
            sp.dma_start(running[R_DUMP:R_ZERO, :].rearrange("(h p) f -> p h f", p=P),
                         zeros[:, 0:2 * D].unsqueeze(1).to_broadcast([P, 2, 2 * D])).then_inc(zero_out, 16)
            sp.dma_start(running[R_ZERO:R_ZERO + 1, :].rearrange("o (p c) -> (o p) c", p=P),
                         zeros[:, 0:2]).then_inc(zero_out, 16)

            def load_attr(i, s, first, last):
                g = i * 2 + s
                if not first:
                    sp.wait_ge(scattered[s], i * (16 * K))
                if not last:
                    sp.dma_start(attr_sb[s], attr_v[:, ds(g * K, K), :]).then_inc(attr_in[s], 16)
                else:
                    sp.dma_start(attr_sb[s][:, 0:K - 2, :], attr_v[:, EP - K + 2:EP, :]).then_inc(attr_in[s], 16)
                    sp.dma_start(attr_sb[s][0:E_TAIL, K - 2, :], attr[EP * P:N_EDGES, :]).then_inc(attr_in[s], 16)

            sp.wait_ge(edge_cols, 1)
            sp.wait_ge(src_f, 1)
            over_chunks(sp, load_attr, 0, 1, False)
            sp.wait_ge(info_ready, 1)
            sp.dma_start(node_scr.rearrange("k (h l) -> h k l", l=NH), info[:, :, :]).then_inc(info_moved, 16)
            sp.wait_ge(info_moved, 16)
            sp.dma_start(info_r[:, :, :], node_scr.rearrange("k (j p) -> j k p", p=P)).then_inc(info_moved, 16)
            over_chunks(sp, load_attr, 1)
            sp.wait_ge(zero_out, 48)
            sp.wait_ge(scattered[0], 16 * K * (HALF + 1) - 16)
            sp.wait_ge(scattered[1], 16 * K * HALF)
            sp.wait_ge(base_done, NG)

            def store_run(i, s):
                g = i * 2 + s
                sp.wait_ge(run_done[s], i + 1)
                sp.dma_start(running_v[:, :, ds(g * KH, KH), :], run_sb[s]).then_inc(run_out[s], 16)

            def load_sorted(i, s, first, last):
                g = i * 2 + s
                if not first:
                    sp.wait_ge(run_done[s], i)
                sp.dma_start(sorted_sb[s], sorted_v[:, :, ds(g * KH, KH), :]).then_inc(sorted_in[s], 16)
                if s == 1:
                    store_run(i, 0)
                elif not first:
                    store_run(i - 1, 1)

            over_chunks(sp, load_sorted)
            store_run(HALF, 0)

            sp.wait_ge(run_out[0], 16 * (HALF + 1))
            sp.wait_ge(run_out[1], 16 * HALF)
            sp.wait_ge(f_out[0], 16 * (NJ // 2 + 1))
            sp.wait_ge(f_out[1], 16 * (NJ // 2))
            hid_v = hid_scr.rearrange("j p f -> p j f")
            for q in range(NQ):
                if q >= 2:
                    sp.wait_ge(t_added, Q * (q - 1))
                sp.dma_start(hid_in[q % 2], hid_v[:, q * Q:(q + 1) * Q, :]).then_inc(hid_got[q % 2], 16)
                if q >= 2:
                    sp.wait_ge(y_ready, q - 1)
                    sp.dma_start(node_view(out, (q - 2) * Q, (q - 1) * Q), h_sb[:, (q - 2) * Q:(q - 1) * Q, :]).then_inc(y_out, 16)
            sp.wait_ge(y_ready, NQ - 1)
            sp.dma_start(node_view(out, (NQ - 2) * Q, (NQ - 1) * Q), h_sb[:, (NQ - 2) * Q:(NQ - 1) * Q, :]).then_inc(y_out, 16)
            sp.wait_ge(y_ready, NQ)
            sp.dma_start(node_view(out, (NQ - 1) * Q, NJ - 1), h_sb[:, (NQ - 1) * Q:NJ - 1, :]).then_inc(y_out, 16)
            sp.dma_start(out[(NJ - 1) * P:N_NODES, :], h_sb[0:N_LAST, NJ - 1, :]).then_inc(y_out, 16)
            sp.wait_ge(y_out, 16 * (NQ + 1))

        @block.gpsimd
        def _(pool):
            pool.memset(x_sb[:, NJ - 1, :], 0.0).then_inc(memsets, 1)
            in_last = N_EDGES - (NG - 1) * GE
            pool.memset(src_g[:, in_last:GE], 0).then_inc(memsets, 1)
            pool.memset(dst_g[:, in_last:GE], PAD_DST).then_inc(memsets, 1)
            pool.memset(src_p[:, EP:TP], PAD_KEY).then_inc(memsets, 1)
            pool.memset(zeros[:, :], 0.0).then_inc(consts, 1)
            pool.memset(ones[:, :], 1.0).then_inc(consts_a, 1)
            pool.memset(ident[:, :], 0.0).then_inc(consts_a, 1)
            pool.memset(identb[:, :], 0.0).then_inc(consts_a, 1)
            pool.wait_ge(consts_a, 3)
            for m in (ident, identb):
                pool.affine_select(out=m[:, :], in_=m[:, :], compare_op=ALU.not_equal, fill=1.0, base=0,
                                   pattern=[[-1, P]], channel_multiplier=1).then_inc(consts, 1)
            pool.affine_select(out=tri[:, :], in_=ones[:, :], compare_op=ALU.is_gt, fill=0.0, base=0,
                               pattern=[[1, P]], channel_multiplier=-1).then_inc(consts, 1)
            pool.iota(iota_w[:, :], pattern=[[1, W]], base=0, channel_multiplier=0,
                      allow_small_or_imprecise_dtypes=True).then_inc(consts, 1)
            pool.iota(dump_f[:, :], pattern=[[P, 32]], base=E_PAD, channel_multiplier=1,
                      allow_small_or_imprecise_dtypes=True).then_inc(consts, 1)
            pool.iota(pdump[:, 0:2], pattern=[[P, 2]], base=R_DUMP, channel_multiplier=1,
                      allow_small_or_imprecise_dtypes=True).then_inc(consts, 1)
            pool.iota(pdump[:, 2:4], pattern=[[TH, 2]], base=-1, channel_multiplier=TP,
                      allow_small_or_imprecise_dtypes=True).then_inc(consts, 1)
            pool.iota(tcol[:, :], pattern=[[1, TH]], base=0, channel_multiplier=0,
                      allow_small_or_imprecise_dtypes=True).then_inc(consts, 1)
            pool.iota(bounds[:, :], pattern=[[TP, P + 1]], base=0, channel_multiplier=0,
                      allow_small_or_imprecise_dtypes=True).then_inc(consts, 1)
            pool.iota(iota_t[:, :], pattern=[[1, TP]], base=0, channel_multiplier=0,
                      allow_small_or_imprecise_dtypes=True).then_inc(consts, 1)
            pool.memset(onesb[:, :], 1.0).then_inc(consts, 1)
            pool.memset(before[1][:, K, :], 0.0).then_inc(consts, 1)
            pool.wait_ge(e_in, 16 * 6)
            pool.wait_ge(memsets, 4)
            pool.tensor_copy(srcf_g, src_g).then_inc(src_f, 1)
            pool.memset(acc[:, :, :], 0.0).then_inc(acc_zero, 1)
            pool.wait_ge(src_f, 2)

            def stage(n, i, s, cols, first):
                g = i * 2 + s
                copied = pool.tensor_copy(idx[n][s][:, :], cols[:, ds(g * K, K)])
                if first:
                    copied.then_inc(idx_first[n][s], 1)
                    pool.wait_ge(idx_first[n][s], 1)
                else:
                    copied.then_inc(idx_staged[n][s], 1)
                    pool.wait_ge(consts, 13)
                    pool.wait_ge(idx_staged[n][s], i)

            src_cols = src_col[:, :, :].rearrange("p g k -> p (g k)")

            def gather(layer, staged=True):
                def step(i, s, first, last):
                    if first or not staged:
                        if not first:
                            pool.wait_ge(acc_zero, 1)
                            pool.wait_ge(summed[layer][s], i)
                        stage(layer, i, s, src_cols, first)
                    else:
                        pool.wait_ge(consts, 13)
                        pool.wait_ge(idx_staged[layer][s], i)
                        pool.wait_ge(summed[layer][s], i)
                    for k in range(K):
                        pool.indirect_dma_start(rows[layer][s][:, k, :], None, table[layer][:, :],
                                                bass.IndirectOffsetOnAxis(ap=idx[layer][s][:, k:k + 1], axis=0)
                                                ).then_inc(rows_in[layer][s], 16)
                return step

            def gather_again(layer):
                with pool.If(pool.value_load(any_far[0:1, 0:1]) > 0):
                    with pool.Fori(1, NG + 1) as g1:
                        pool.wait_ge(consts, 13)
                        pool.wait_ge(far_free[layer], g1)
                        pool.tensor_copy(idx[layer][0][:, :], src_cols[:, ds((g1 - 1) * K, K)]).then_inc(far_staged[layer], 1)
                        pool.wait_ge(consts, 13)
                        pool.wait_ge(far_staged[layer], g1)
                        for k in range(K):
                            pool.indirect_dma_start(rows[layer][0][:, k, :], None, table[layer][:, :],
                                                    bass.IndirectOffsetOnAxis(ap=idx[layer][0][:, k:k + 1], axis=0)
                                                    ).then_inc(far_rows[layer], 16)
                    pool.wait_ge(far_rows[layer], NG * 16 * K)

            pool.wait_ge(table_out[0], 48)
            over_chunks(pool, gather(0))
            pool.wait_ge(edge_cols, 1)
            gather_again(0)

            def scatter(i, s, first, last):
                if not first:
                    pool.wait_ge(acc_zero, 1)
                    pool.wait_ge(scattered[s], i * (16 * K))
                pool.wait_ge(pos_ready, i * 2 + s + 1)
                pool.wait_ge(attr_in[s], (i + 2 if last else i + 1) * 16)
                stage(2, i, s, pos, first)
                for k in range(K if not last else K - 1):
                    n = E_TAIL if last and k == K - 2 else P
                    pool.indirect_dma_start(sorted_rows[:, :], bass.IndirectOffsetOnAxis(ap=idx[2][s][0:n, k:k + 1], axis=0),
                                            attr_sb[s][0:n, k, :], None).then_inc(scattered[s], 16)

            over_chunks(pool, scatter)
            pool.wait_ge(zero_out, 48)
            pool.wait_ge(idx_ready, 2)
            pool.wait_ge(sums_ready[0], 1)
            pool.wait_ge(starts_found, NQ)
            pool.wait_ge(table_out[1], 32)
            over_chunks(pool, gather(1), 0, SCANNED, False)
            over_chunks(pool, gather(1, False), SCANNED, FIXED, False)
            pool.wait_ge(run_out[0], 16 * (HALF + 1))
            pool.wait_ge(run_out[1], 16 * HALF)
            pool.wait_ge(fix_idx_ready, 1)
            for h in range(2):
                pool.indirect_dma_start(fix_rows[:, h, :], None, running[:, :],
                                        bass.IndirectOffsetOnAxis(ap=fix_idx[:, h:h + 1], axis=0)).then_inc(fix_in, 16)
            over_chunks(pool, gather(1, False), FIXED, FIXED + 1, False)
            pool.wait_ge(fixed_ready, 4)
            for h in range(2):
                pool.indirect_dma_start(running[:, :], bass.IndirectOffsetOnAxis(ap=fix_idx[:, h:h + 1], axis=0),
                                        fixed[:, h, :], None).then_inc(fix_out, 16)
            pool.wait_ge(fix_out, 32)
            for j in range(NJ):
                pool.indirect_dma_start(agg[:, j, :], None, running[:, :],
                                        bass.IndirectOffsetOnAxis(ap=last_idx[:, j:j + 1], axis=0)).then_inc(agg_in, 16)
            over_chunks(pool, gather(1, False), FIXED + 1, HALF, True)
            gather_again(1)

            pool.wait_ge(sums_ready[1], 1)
            for q in range(NQ):
                J = slice(q * Q, (q + 1) * Q)
                if q + 1 < NQ:
                    pool.wait_ge(t_z, q + 1)
                    n0 = (q + 1) * Q * P
                    pool.tensor_tensor(g_m[:, :, :].rearrange("p j n -> p (j n)"), acc[:, 0, n0:n0 + Q * P],
                                       acc[:, 1, n0:n0 + Q * P], ALU.mult).then_inc(t_m, 1)
                pool.wait_ge(t_xc, q + 1)
                pool.tensor_tensor(x_sb[:, J, :], x_sb[:, J, :], b_all[:, 2:3, :].to_broadcast([P, Q, D]), ALU.add).then_inc(residual, 1)
                pool.wait_ge(t_h, q + 1)
                pool.wait_ge(residual, 2 * q + 1)
                pool.tensor_tensor(x_sb[:, J, :], x_sb[:, J, :], g_h[:, :, :], ALU.add).then_inc(residual, 1)

        @block.scalar
        def _(act):
            for n, w in enumerate((w0a, w0b)):
                act.dma_start(w0[n][:, :, :], w.rearrange("(k p) n -> p k n", p=P)).then_inc(w_in, 16)
            for n, b in enumerate((b0a, b0b, b2)):
                act.dma_start(b_all[:, n, :], b.rearrange("(o n) -> o n", o=1).to_broadcast([P, D])).then_inc(w_in, 16)
            act.dma_start(w1_sb[:, :, :], w1[0:HID, :].rearrange("(k p) n -> p k n", p=P)).then_inc(w_in, 16)
            act.dma_start(w2_sb[:, :, :], w2.rearrange("(k p) n -> p k n", p=P)).then_inc(w_in, 16)
            act.dma_start(u_sb[:, :], u[0:1, :]).then_inc(w_in, 16)
            act.dma_start(w1u_b1[0:4, :], w1[HID, :].rearrange("(c p) -> c p", p=P)).then_inc(w_in, 16)
            act.dma_start(w1u_b1[4:8, :], b1.rearrange("(c p) -> c p", p=P)).then_inc(w_in, 16)

            for n, (j0, j1) in enumerate(PARTS):
                act.wait_ge(centered, n + 1)
                act.activation(tmp[:, j0:j1, :], h_sb[:, j0:j1, :], ACT.Square).then_inc(squared, 1)
            for n, (j0, j1) in enumerate(PARTS):
                act.wait_ge(var_ready, n + 1)
                act.activation(stat[:, 2, j0:j1], stat[:, 1, j0:j1], ACT.Sqrt).then_inc(std_ready, 1)

            a1 = PARTS[0][1]
            for n, (j0, j1) in enumerate(PARTS):
                act.wait_ge(h_ready, n + 1)
                act.activation(parts[:, j0:j1, 0, :], h_sb[:, j0:j1, :], ACT.Copy).then_inc(part0, 1)
            for n, (j0, j1) in enumerate(PARTS):
                act.wait_ge(rest1, n + 1)
                act.activation(parts[:, j0:j1, 1, :], tmp[:, j0:j1, :], ACT.Copy).then_inc(part1, 1)
            parts_v = parts.rearrange("p j c f -> p j (c f)")
            act.wait_ge(parts_ready, 1)
            act.dma_start(node_view(table[0], 0, a1), parts_v[:, 0:a1, :]).then_inc(table_out[0], 16)
            act.wait_ge(parts_ready, 2)
            act.dma_start(node_view(table[0], a1, NJ - 1), parts_v[:, a1:NJ - 1, :]).then_inc(table_out[0], 16)
            act.dma_start(table[0][(NJ - 1) * P:N_NODES, :], parts_v[0:N_LAST, NJ - 1, :]).then_inc(table_out[0], 16)

            def rank_copies(i, s, first, last):
                act.wait_ge(hiT_done, i * 2 + s + 1)
                if not first:
                    act.wait_ge(rank_done, i * 2 + s - 1)
                act.activation(hiT_f[s], p_hiT[0:NH, :], ACT.Copy).then_inc(hiT_ready, 1)
                act.activation(hiT_b[s], p_hiT[0:NH, :], ACT.Copy).then_inc(hiT_ready, 1)

            src_cols = src_col[:, :, :].rearrange("p g k -> p (g k)")

            def stage_idx(layer, i, s):
                act.wait_ge(rows_in[layer][s], i * (16 * K))
                act.activation(idx[layer][s][:, :], src_cols[:, ds((i * 2 + s) * K, K)], ACT.Copy).then_inc(idx_staged[layer][s], 1)

            def copies_and_idx(i, s, first, last):
                rank_copies(i, s, first, last)
                stage_idx(0, i, s)

            for s in range(2):
                rank_copies(0, s, True, False)
                stage_idx(0, 1, s)
            for s in range(2):
                rank_copies(1, s, False, False)
            over_chunks(act, copies_and_idx, 2)

            def base_copies(i, s, first, last):
                act.wait_ge(b_hiT_done, i * 2 + s + 1)
                if not first:
                    act.wait_ge(base_done, i * 2 + s - 1)
                act.activation(hiT_f[s], p_hiT[0:NH, :], ACT.Copy).then_inc(b_hiT_ready, 1)

            act.wait_ge(rank_done, NG)
            over_chunks(act, base_copies)

            def z_copies(n):
                def step(q, first):
                    if not first:
                        act.wait_ge(z_T[n], q)
                    act.activation(g_h[:, :, :], h_sb[:, ds(q * Q, Q), :], ACT.Copy).then_inc(z_h[n], 1)
                    act.wait_ge(z_T[n], q + 1)
                    if not first:
                        act.wait_ge(z_mm[n], q)
                    act.activation(g_hT[:, :, :].rearrange("p j n -> p (j n)"), p_eq[:, 0:Q * P], ACT.Copy).then_inc(z_Tc[n], 1)
                return step

            over_groups(act, z_copies(0))
            act.wait_ge(z_out[0], NQ)
            act.dma_start(node_view(table[1], 0, NJ - 1), h_sb[:, 0:NJ - 1, :]).then_inc(table_out[1], 16)
            act.dma_start(table[1][(NJ - 1) * P:N_NODES, :], h_sb[0:N_LAST, NJ - 1, :]).then_inc(table_out[1], 16)
            act.wait_ge(z_mm[0], NQ)
            over_groups(act, z_copies(1))

            def near_onehots(i, s, first, last, idx_too=True):
                g = i * 2 + s
                act.activation(neg_dl[s][:, :], dl_cols[:, ds(g * K, K)], ACT.Copy, scale=-1.0).then_inc(oh_neg, 1)
                act.wait_ge(oh_neg, g + 1)
                for k in range(K):
                    act.activation(same[:, k, :], iota_w[:, :], ACT.Abs, bias=neg_dl[s][:, k:k + 1]).then_inc(oh_abs, 1)
                if not first and idx_too:
                    stage_idx(1, i, s)
                act.wait_ge(oh_abs, g * K + K)
                if not first:
                    act.wait_ge(summed[1][s], i)
                act.activation(onehot[1][s][:, :, :], same[:, :, :], ACT.Relu, bias=ones[:, 0:1], scale=-1.0).then_inc(onehot_ready[1][s], 1)

            dl_cols = dl_col[:, :, :].rearrange("p g k -> p (g k)")
            act.wait_ge(edge_cols, 1)
            act.wait_ge(sums_ready[0], 1)
            over_chunks(act, near_onehots, 0, SCANNED, False)
            near_onehots(SCANNED, 0, False, False, idx_too=False)

            act.wait_ge(agg_in, 16 * NJ)
            act.wait_ge(idx_ready, 2)

            def edge_values(j, s):
                one = ds(j, 1)
                for c, (f0, scale) in enumerate(((D, 1.0), (0, 1.0), (D, rcnt[:, one]))):
                    act.activation(feat[s][:, c, :], agg[:, one, f0:f0 + D].rearrange("p o f -> p (o f)"), ACT.Copy,
                                   scale=scale).then_inc(f_ready, 1)

            def turned_copy(j, s):
                act.wait_ge(f_T, j + 1)
                act.activation(featT[s].rearrange("p k n -> p (k n)"), p_featT[s][:, 0:3 * P], ACT.Copy).then_inc(f_Tc, 1)

            def hid_step(i, s, first, left=2):
                j = i * 2 + s
                if left >= 1:
                    if s or not first:
                        act.wait_ge(f_hid, j)
                    turned_copy(j + 1, 1 - s)
                if left >= 2:
                    edge_values(j + 2, s)
                act.wait_ge(f_hid, j + 1)
                if not first:
                    act.wait_ge(f_out[s], i * 16)
                for c in range(4):
                    act.activation(hid_part[s][:, c * P:(c + 1) * P], p_hid[s][:, c * P:(c + 1) * P], ACT.Identity,
                                   bias=bias1[:, c:c + 1]).then_inc(f_part, 1)
                act.wait_ge(f_part, j * 4 + 4)
                act.dma_start(hid_scr[ds(j, 1), :, :].rearrange("o p f -> p (o f)"), hid_part[s]).then_inc(f_out[s], 16)

            edge_values(0, 0)
            edge_values(1, 1)
            turned_copy(0, 0)
            hid_step(0, 0, True)
            hid_step(0, 1, True)
            with act.Fori(1, NJ // 2 - 1) as i:
                hid_step(i, 0, False)
                hid_step(i, 1, False)
            hid_step(NJ // 2 - 1, 0, False)
            hid_step(NJ // 2 - 1, 1, False, 1)
            hid_step(NJ // 2, 0, False, 0)

            def tail_norm(q):
                act.wait_ge(t_xc, q + 1)
                act.activation(tmp[:, q * Q:(q + 1) * Q, :], h_sb[:, q * Q:(q + 1) * Q, :], ACT.Square).then_inc(t_sq, 1)
                act.wait_ge(t_var, q + 1)
                act.activation(stat[:, 2, q * Q:(q + 1) * Q], stat[:, 1, q * Q:(q + 1) * Q], ACT.Sqrt).then_inc(t_std, 1)

            def tail_turn(q):
                act.wait_ge(t_hT, q + 1)
                if q >= 2:
                    act.wait_ge(t_hid, Q * (q - 1))
                act.activation(turned[q % 2], p_eq[:, 0:Q * P], ACT.Copy).then_inc(t_hTc, 1)

            def tail_relu(n):
                act.wait_ge(t_added, n + 1)
                act.activation(hidT[n % 2], hidT[n % 2], ACT.Relu).then_inc(t_relu, 1)

            tail_norm(0)
            tail_turn(0)
            for q in range(NQ):
                for t in range(Q):
                    tail_relu(q * Q + t)
                    if t == 2 and q + 1 < NQ:
                        tail_norm(q + 1)
                    if t == 3 and q + 1 < NQ:
                        tail_turn(q + 1)

        @block.tensor
        def _(pe):
            mm = nc.tensor.matmul
            pe.wait_ge(consts, 13)
            pe.wait_ge(src_f, 1)
            for k in range(K):
                nc.tensor.transpose(p_rank[:, k * NG:(k + 1) * NG], srcf_g[:, k * P:(k + 1) * P], ident[0:NG, 0:NG]).then_inc(edgesT, 1)
            pe.wait_ge(edges_f, 1)
            for k in range(K):
                nc.tensor.transpose(p_misc[:, k * NG:(k + 1) * NG], dl_g[:, k * P:(k + 1) * P], ident[0:NG, 0:NG]).then_inc(edgesT, 1)
            for k in range(K):
                nc.tensor.transpose(p_agg[0][:, k * NG:(k + 1) * NG], far_g[:, k * P:(k + 1) * P], ident[0:NG, 0:NG]).then_inc(edgesT, 1)
            nc.tensor.transpose(p_pre[0:1, 64:64 + NG], any_g[:, :], ident[0:NG, 0:NG]).then_inc(edgesT, 1)
            nc.tensor.transpose(p_pre[0:1, 0:NG], base_g[:, :], ident[0:NG, 0:NG]).then_inc(edgesT, 1)
            pe.wait_ge(w_in, 16 * 10)
            nc.tensor.transpose(p_eq[:, 0:8], w1u_b1[:, :], ident[0:8, 0:8])
            mm(p_eq[:, 8:9], ones[0:1, :], u_sb[:, :], start=True, stop=True).then_inc(b1T, 1)
            pe.wait_ge(edge_cols, 1)

            def degrees(s):
                for k in range(K):
                    mm(p_agg[s][:, W:2 * W], onesb[:, :], onehot[0][s][:, k, :], start=(k == 0), stop=(k == K - 1))

            def sums(layer, s):
                parts_ = 3 if layer == 0 else 1
                for k in range(K):
                    for c in range(parts_):
                        n = mm(p_agg[s][:, 0:W], rows[layer][s][:, k, c * D:(c + 1) * D], onehot[layer][s][:, k, :],
                               start=(k == 0 and c == 0), stop=(k == K - 1 and c == parts_ - 1))
                return n

            def sum_rows(layer):
                def step(i, s, first, last):
                    pe.wait_ge(onehot_ready[layer][s], i + 1)
                    if not first:
                        pe.wait_ge(added[layer][s], i)
                    if layer == 0:
                        degrees(s)
                    pe.wait_ge(rows_in[layer][s], (i + 1) * (16 * K))
                    sums(layer, s).then_inc(summed[layer][s], 1)
                return step

            def sum_far(layer):
                with pe.If(pe.value_load(any_far[0:1, 0:1]) > 0):
                    with pe.Fori(1, NG + 1) as g1:
                        with pe.Fori(1, NJ + 1) as c1:
                            pe.wait_ge(consts, 13)
                            pe.wait_ge(far_rows[layer], g1 * (16 * K))
                            pe.wait_ge(far_onehot[layer], (g1 - 1) * NJ + c1)
                            if layer == 0:
                                degrees(0)
                            sums(layer, 0).then_inc(far_summed[layer], 1)

            def rank_open(i, s, first, last):
                pe.wait_ge(oh_ready, i * 2 + s + 1)
                if s or not first:
                    pe.wait_ge(before_ready, i * 4 + 2 * s)
                for k in range(K):
                    n = mm(p_pre[0:NH, k * NH:K * NH].rearrange("p (t l) -> p t l", l=NH), oh_hi[s][:, k, :],
                           oh_lo[s][:, k:k + 1, :].to_broadcast([P, K - k, NH]), start=(k == 0), stop=(k == K - 1))
                n.then_inc(pre_done, 1)
                if s or not first:
                    pe.wait_ge(consts, 13)
                    pe.wait_ge(hiT_ready, i * 4 + 2 * s)
                for k in range(K):
                    n = nc.tensor.transpose(p_hiT[0:NH, k * P:(k + 1) * P], oh_hi[s][:, k, :], identb[:, :])
                n.then_inc(hiT_done, 1)

            def rank_same(i, s, first, last):
                pe.wait_ge(hiT_ready, i * 4 + 2 * s + 2)
                if s or not first:
                    pe.wait_ge(same_ready, i * 2 + s)
                for k in range(K):
                    n = mm(p_eq[:, k * P:(k + 1) * P], hiT_b[s][:, k * P:(k + 1) * P], hiT_b[s][:, k * P:(k + 1) * P],
                           start=True, stop=True)
                n.then_inc(eq_done, 1)

            def rank_close(i, s, first):
                pe.wait_ge(same_ready, i * 2 + s + 1)
                pe.wait_ge(before_ready, i * 4 + 2 * s + 2)
                if s or not first:
                    pe.wait_ge(picked_ready, i * 2 + s)
                for k in range(K):
                    mm(p_rank[:, k * NH:(k + 1) * NH], hiT_f[s][:, k * P:(k + 1) * P], before[s][:, k, :], start=True, stop=False)
                    n = mm(p_rank[:, k * NH:(k + 1) * NH], same[:, k, :], oh_lo[s][:, k, :], start=False, stop=True)
                n.then_inc(rank_done, 1)

            agg0 = sum_rows(0)

            def both(i, s, first, last, second=False):
                rank_open(i, s, first, last)
                if s:
                    rank_close(i, 0, first)
                elif not first:
                    rank_close(i - 1, 1, False)
                rank_same(i, s, first, last)
                if last:
                    rank_close(i, 0, False)
                if first:
                    agg0(0, s, True, False)
                elif not second:
                    agg0(i - 1, s, False, False)

            over_chunks(pe, both, 0, 1, False)
            for s in range(2):
                both(1, s, False, False, second=True)
            over_chunks(pe, both, 2)
            pe.wait_ge(totals, 1)
            mm(p_pre[0:NH, 0:1], tri[0:NH, 0:NH], incl[:, NH - 1:NH], start=True, stop=True).then_inc(offsets, 1)
            pe.wait_ge(info_ready, 1)

            def base_look(i, s, first):
                pe.wait_ge(b_hiT_ready, i * 2 + s + 1)
                if s or not first:
                    pe.wait_ge(b_picked, i * 2 + s)
                for k in range(K):
                    n = mm(p_rank[:, k * NH:(k + 1) * NH], hiT_f[s][:, k * P:(k + 1) * P], info[:, 0, :], start=True, stop=True)
                n.then_inc(base_done, 1)

            def base(i, s, first, last):
                pe.wait_ge(b_oh_ready, i * 2 + s + 1)
                if s:
                    base_look(i, 0, first)
                elif not first:
                    base_look(i - 1, 1, False)
                for k in range(K):
                    n = nc.tensor.transpose(p_hiT[0:NH, k * P:(k + 1) * P], oh_hi[s][:, k, :], identb[:, :])
                n.then_inc(b_hiT_done, 1)

            over_chunks(pe, base, 0, 1, False)
            agg0(HALF - 1, 1, False, False)
            agg0(HALF, 0, False, True)
            sum_far(0)
            over_chunks(pe, base, 1, 3, False)
            pe.wait_ge(info_moved, 32)
            for k in range(3):
                nc.tensor.transpose(p_misc[:, 32 * k:32 * k + 32], info_r[:, k, :], ident[0:32, 0:32]).then_inc(infoT, 1)
            over_chunks(pe, base, 3, HALF, True)
            base_look(HALF, 0, False)

            def z_mms(n):
                def step(q, first):
                    pe.wait_ge(z_h[n], q + 1)
                    if not first:
                        pe.wait_ge(z_Tc[n], q)
                    for t in range(Q):
                        last = nc.tensor.transpose(p_eq[:, t * P:(t + 1) * P], g_h[:, t, :], ident[:, :])
                    last.then_inc(z_T[n], 1)
                    pe.wait_ge(z_Tc[n], q + 1)
                    if n == 0:
                        pe.wait_ge(z_m, q + 1)
                    if not first:
                        pe.wait_ge(z_out[n], q)
                    for t in range(Q):
                        last = mm(p_aggs[:, t * P:(t + 1) * P], g_hT[:, t, :], w0[n][:, 0, :], start=True, stop=(n == 1))
                        if n == 0:
                            last = mm(p_aggs[:, t * P:(t + 1) * P], g_m[:, t, :], w0[n][:, 1, :], start=False, stop=True)
                    last.then_inc(z_mm[n], 1)
                return step

            over_groups(pe, z_mms(0))
            pe.wait_ge(z_out[0], NQ)
            over_groups(pe, z_mms(1))
            pe.wait_ge(z_out[1], NQ)

            def find_starts(q, first):
                pe.wait_ge(start_onehots, q * 2 + 2)
                if not first:
                    pe.wait_ge(start_step, q * 6)
                for t in range(Q):
                    n = mm(p_rank[:, 0:TP], start_p[:, t, :], start_t[:, t, :], start=(t == 0), stop=(t == Q - 1))
                n.then_inc(starts_found, 1)

            over_groups(pe, find_starts)
            over_chunks(pe, sum_rows(1), 0, FIXED, False)
            pe.wait_ge(tails_ready, 2)
            for h in range(2):
                mm(p_misc[:, h * P:(h + 1) * P], ones[:, :], diag[:, h, :], start=True, stop=True)
            for h in range(2):
                for c in range(2):
                    n = nc.tensor.transpose(p_eq[:, (2 * c + h) * P:(2 * c + h + 1) * P], tail[:, h, c * D:(c + 1) * D], ident[:, :])
            n.then_inc(tailsT, 1)
            pe.wait_ge(carry_ready, 4)
            for h in range(2):
                for c in range(2):
                    n = nc.tensor.transpose(p_rank[:, (2 * h + c) * P:(2 * h + c + 1) * P], carry[:, c, h:h + 2 * P:2], ident[:, :])
            n.then_inc(carry_back, 1)
            over_chunks(pe, sum_rows(1), FIXED, FIXED + 1, False)

            def hid_turn(j, s, first=False):
                pe.wait_ge(f_ready, j * 3 + 3)
                if not first:
                    pe.wait_ge(f_Tc, j - 1)
                for c in range(3):
                    n = nc.tensor.transpose(p_featT[s][:, c * P:(c + 1) * P], feat[s][:, c, :], ident[:, :])
                n.then_inc(f_T, 1)

            def hid_edges(j, s, first=False, last=False):
                if not last:
                    hid_turn(j + 1, 1 - s, first and s == 0)
                pe.wait_ge(f_Tc, j + 1)
                if not first:
                    pe.wait_ge(f_part, (j - 1) * 4)
                for c in range(4):
                    for k in range(3):
                        n = mm(p_hid[s][:, c * P:(c + 1) * P], w1_sb[:, k + 1, c * P:(c + 1) * P], featT[s][:, k, :],
                               start=(k == 0), stop=(k == 2))
                n.then_inc(f_hid, 1)

            agg1 = sum_rows(1)
            FIRST = FIXED + 1
            agg1(FIRST, 0, False, False)
            hid_turn(0, 0, True)
            hid_edges(0, 0, True)
            hid_edges(1, 1, True)
            agg1(FIRST, 1, False, False)
            hid_edges(2, 0)
            hid_edges(3, 1)
            with pe.Fori(FIRST + 1, HALF) as i:
                for s in range(2):
                    agg1(i, s, False, False)
                    for n in range(2):
                        hid_edges((i - FIRST) * 4 + 2 * s + n, n)
            agg1(HALF, 0, False, True)
            sum_far(1)
            hid_edges(NJ - 1, 0, last=True)

            def tail_z(q):
                pe.wait_ge(t_m, q + 1)
                for t in range(Q):
                    n = mm(p_aggs[:, t * P:(t + 1) * P], g_m[:, t, :], w0[1][:, 1, :], start=True, stop=True)
                n.then_inc(t_z, 1)

            def tail_turn(q):
                pe.wait_ge(t_h, q + 1)
                for t in range(Q):
                    n = nc.tensor.transpose(p_eq[:, t * P:(t + 1) * P], g_h[:, t, :], ident[:, :])
                n.then_inc(t_hT, 1)

            hid_bank = [p_rank, p_hT]
            out_bank = [p_pre, p_misc]

            def tail_hid(n):
                if n % Q == 0:
                    pe.wait_ge(t_hTc, n // Q + 1)
                if n >= 2:
                    pe.wait_ge(t_added, n - 1)
                for c in range(4):
                    last = mm(hid_bank[n % 2][:, c * P:(c + 1) * P], w1_sb[:, 0, c * P:(c + 1) * P], turned[n // Q % 2][:, n % Q * P:(n % Q + 1) * P],
                              start=True, stop=True)
                last.then_inc(t_hid, 1)

            def tail_out(n):
                pe.wait_ge(t_relu, n + 1)
                q, t = divmod(n, Q)
                if q and t == 0:
                    pe.wait_ge(y_ready, q)
                o = p_pre[:, t * P:(t + 1) * P] if t < 4 else p_misc[:, 0:P]
                for c in range(4):
                    last = mm(o, hidT[n % 2][:, c * P:(c + 1) * P], w2_sb[:, c, :], start=(c == 0), stop=(c == 3))
                last.then_inc(t_y, 1)

            tail_z(0)
            tail_turn(0)
            for n in range(NJ):
                q, t = divmod(n, Q)
                if t == 0 and q + 1 < NQ:
                    tail_z(q + 1)
                if t == Q - 1 and q + 1 < NQ:
                    tail_turn(q + 1)
                tail_hid(n)
                if n:
                    tail_out(n - 1)
            tail_out(NJ - 1)

        @block.vector
        def _(v):
            tt, tsc, stt, copy = nc.vector.tensor_tensor, nc.vector.tensor_scalar, nc.vector.scalar_tensor_tensor, nc.vector.tensor_copy
            reduce = nc.vector.tensor_reduce
            link = counted_links(v, dve)

            def bc(a, n):
                return a.unsqueeze(2).to_broadcast([a.shape[0], a.shape[1], n])

            for n, (j0, j1) in enumerate(PARTS):
                J = slice(j0, j1)
                v.wait_ge(x_in[n], 16 * (n + 1))
                link(reduce(stat[:, 0, J], x_sb[:, J, :], axis=AX.X, op=ALU.add))
                link(tsc(stat[:, 0, J], stat[:, 0, J], 1.0 / D, None, ALU.mult))
                tt(h_sb[:, J, :], x_sb[:, J, :], bc(stat[:, 0, J], D), ALU.subtract).then_inc(centered, 1)
            for n, (j0, j1) in enumerate(PARTS):
                J = slice(j0, j1)
                v.wait_ge(squared, n + 1)
                link(reduce(stat[:, 1, J], tmp[:, J, :], axis=AX.X, op=ALU.add))
                tsc(stat[:, 1, J], stat[:, 1, J], 1.0 / D, EPS, ALU.mult, ALU.add).then_inc(var_ready, 1)
            for n, (j0, j1) in enumerate(PARTS):
                J = slice(j0, j1)
                v.wait_ge(std_ready, n + 1)
                link(nc.vector.reciprocal(stat[:, 3, J], stat[:, 2, J]))
                stt(h_sb[:, J, :], h_sb[:, J, :], 0.0, bc(stat[:, 3, J], D), ALU.max, ALU.mult).then_inc(h_ready, 1)

            v.wait_ge(edgesT, K)
            copy(src_col[:, :, :], p_rank[:, 0:TP].rearrange("p (k g) -> p g k", g=NG)).then_inc(src_f, 1)
            for n, (j0, j1) in enumerate(PARTS):
                v.wait_ge(part0, n + 1)
                tt(tmp[:, j0:j1, :], h_sb[:, j0:j1, :], parts[:, j0:j1, 0, :], ALU.subtract).then_inc(rest1, 1)
            for n, (j0, j1) in enumerate(PARTS):
                v.wait_ge(part1, n + 1)
                tt(parts[:, j0:j1, 2, :], tmp[:, j0:j1, :], parts[:, j0:j1, 1, :], ALU.subtract).then_inc(parts_ready, 1)
            v.wait_ge(e_in, 16 * 6)
            link(copy(dl_g, dst_g))
            link(reduce(base_g[:, :], dl_g, axis=AX.X, op=ALU.min))
            link(tsc(far_g, dl_g, base_g[:, 0:1], float(W), ALU.subtract, ALU.is_lt))
            link(stt(far_g, far_g, float(PAD_DST), dl_g, ALU.mult, ALU.add))
            link(reduce(any_g[:, :], far_g, axis=AX.X, op=ALU.min))
            link(tsc(any_g[:, :], any_g[:, :], float(NPAD), None, ALU.is_lt))
            tsc(dl_g, dl_g, base_g[:, 0:1], None, ALU.subtract).then_inc(edges_f, 1)
            link(tsc(ki[:, :], src_p[:, :], 6, None, ALU.arith_shift_right))
            link(copy(s_hi[:, :], ki[:, :]))
            link(tsc(ki[:, :], src_p[:, :], NH - 1, None, ALU.bitwise_and))
            link(copy(s_lo[:, :], ki[:, :]))
            v.wait_ge(edgesT, 3 * K + 2)
            link(copy(dl_col[:, :, :], p_misc[:, 0:TP].rearrange("p (k g) -> p g k", g=NG)))
            link(copy(base_row[:, :], p_pre[0:1, 0:NG]))
            link(copy(far_col[:, :, :], p_agg[0][:, 0:TP].rearrange("p (k g) -> p g k", g=NG)))
            link(reduce(any_row[:, 0:1], p_pre[0:1, 64:64 + NG], axis=AX.X, op=ALU.max))
            link(copy(any_far[:, :], any_row[:, 0:1]))
            v.wait_ge(b1T, 1)
            link(copy(u_col[:, :], p_eq[:, 8:9]))
            link(copy(w1u_b1T[:, :], p_eq[:, 0:8]))
            stt(bias1[:, :], w1u_b1T[:, 0:4], u_col[:, 0:1], w1u_b1T[:, 4:8], ALU.mult, ALU.add).then_inc(edge_cols, 1)
            v.wait_ge(consts, 13)

            def which(dst_t, keys, g, n):
                return tt(dst_t[:, :, :], bc(keys[:, ds(g * K, K)], n),
                          iota_w[:, 0:n].unsqueeze(1).to_broadcast([P, K, n]), ALU.is_equal)

            dl_cols = dl_col[:, :, :].rearrange("p g k -> p (g k)")

            def make_onehot(layer, i, s, first):
                if not first:
                    v.wait_ge(summed[layer][s], i)
                which(onehot[layer][s], dl_cols, i * 2 + s, W).then_inc(onehot_ready[layer][s], 1)

            def add_window(layer, at, bank):
                n = 2 if layer == 0 else 1
                a = acc[:, 0:n, ds(at, W)]
                return tt(a, a, bank[:, 0:n * W].rearrange("p (n w) -> p n w", n=n), ALU.add)

            def add_sum(layer, i, s, very_first=False):
                v.wait_ge(summed[layer][s], i + 1)
                if s == 1:
                    v.wait_ge(added[layer][0], i + 1)
                elif not very_first:
                    v.wait_ge(added[layer][1], i)
                at = v.value_load(base_row[0:1, ds(i * 2 + s, 1)], min_val=0, max_val=NPAD)
                add_window(layer, at, p_agg[s]).then_inc(added[layer][s], 1)

            def add_before(layer, i, s, first):
                if s == 1:
                    add_sum(layer, i, 0, first)
                elif not first:
                    add_sum(layer, i - 1, 1)

            def add_far(layer):
                v.wait_ge(added[layer][0], HALF + 1)
                nc.vector.memset(far_key[:, :], 0.0).then_inc(far_free[layer], 1)
                v.wait_ge(far_free[layer], 1)
                with v.If(v.value_load(any_far[0:1, 0:1]) > 0):
                    with v.Fori(1, NG + 1) as g1:
                        v.wait_ge(far_free[layer], g1)
                        copy(far_key[:, :], far_col[:, :, :].rearrange("p g k -> p (g k)")[:, ds((g1 - 1) * K, K)]
                             ).then_inc(far_key_ready[layer], 1)
                        with v.Fori(1, NJ + 1) as c1:
                            n = (g1 - 1) * NJ + c1
                            v.wait_ge(far_key_ready[layer], n + g1 - 1)
                            tt(onehot[layer][0][:, :, :], bc(far_key[:, :], W), iota_w[:, :].unsqueeze(1).to_broadcast([P, K, W]),
                               ALU.is_equal).then_inc(far_onehot[layer], 1)
                            v.wait_ge(far_onehot[layer], n)
                            tsc(far_key[:, :], far_key[:, :], -float(W), None, ALU.add).then_inc(far_key_ready[layer], 1)
                            v.wait_ge(far_summed[layer], n)
                            add_window(layer, (c1 - 1) * W, p_agg[0]).then_inc(far_added[layer], 1)
                            v.wait_ge(far_added[layer], n)
                        v.wait_ge(far_key_ready[layer], g1 * (NJ + 1))
                        nc.vector.memset(any_row[:, 1:2], 0.0).then_inc(far_free[layer], 1)
                nc.vector.memset(any_row[:, 2:3], 0.0).then_inc(sums_ready[layer], 1)

            def source_onehots(g, s, signal):
                which(oh_hi[s], s_hi, g, NH)
                which(oh_lo[s], s_lo, g, NH).then_inc(signal, 1)

            def rank_pick(i, s, first):
                v.wait_ge(rank_done, i * 2 + s + 1)
                tt(picked[:, :, :], p_rank[:, :].rearrange("p (k l) -> p k l", l=NH), oh_lo[s][:, :, :],
                   ALU.mult).then_inc(picked_ready, 1)
                v.wait_ge(picked_ready, i * 2 + s + 1)
                reduce(rank_f[:, ds((i * 2 + s) * K, K)], picked[:, :, :], axis=AX.X, op=ALU.add).then_inc(rank_ready, 1)

            def both(i, s, first, last, second=False):
                g = i * 2 + s
                v.wait_ge(pre_done, g + 1)
                if s or not first:
                    v.wait_ge(before_ready, i * 4 + 2 * s)
                carried = before[1 - s][:, K:K + 1, :]
                copy(before[s][:, 0:1, :], carried).then_inc(before_ready, 1)
                tt(before[s][:, 1:K + 1, :], p_pre[0:NH, :].rearrange("p (t l) -> p t l", l=NH),
                   carried.to_broadcast([NH, K, NH]), ALU.add).then_inc(before_ready, 1)
                if s:
                    rank_pick(i, 0, first)
                elif not first:
                    rank_pick(i - 1, 1, False)
                if not last:
                    source_onehots(g + 1, 1 - s, oh_ready)
                v.wait_ge(eq_done, g + 1)
                if s or not first:
                    v.wait_ge(rank_done, g)
                tt(same[:, :, :], p_eq[:, :].rearrange("p (k e) -> p k e", e=P),
                   tri[:, :].unsqueeze(1).to_broadcast([P, K, P]), ALU.mult).then_inc(same_ready, 1)
                if first:
                    if s == 0:
                        make_onehot(0, 0, 1, True)
                elif s:
                    make_onehot(0, i, 0, False)
                    add_sum(0, i - 1, 0, second)
                elif not second:
                    make_onehot(0, i - 1, 1, False)
                    add_sum(0, i - 2, 1)

            source_onehots(0, 0, oh_ready)
            make_onehot(0, 0, 0, True)
            v.wait_ge(acc_zero, 1)
            over_chunks(v, both, 0, 1, False)
            for s in range(2):
                both(1, s, False, False, second=True)
            over_chunks(v, both, 2)
            rank_pick(HALF, 0, False)

            v.wait_ge(before_ready, 2 * NG)
            link(copy(info[:, 1, :], before[0][:, K, :]))
            nc.vector.tensor_tensor_scan(incl[:, :], ones[0:NH, 0:NH], info[:, 1, :], 0.0, ALU.mult, ALU.add).then_inc(totals, 1)
            v.wait_ge(offsets, 1)
            link(copy(off[:, :], p_pre[0:NH, 0:1]))
            link(tsc(incl[:, :], incl[:, :], off[:, 0:1], None, ALU.add))
            link(tsc(info[:, 2, :], incl[:, :], -1.0, None, ALU.add))
            tt(info[:, 0, :], incl[:, :], info[:, 1, :], ALU.subtract).then_inc(info_ready, 1)

            def place(i, s, nxt):
                g = i * 2 + s
                v.wait_ge(base_done, g + 1)
                tt(picked[:, :, :], p_rank[:, :].rearrange("p (k l) -> p k l", l=NH), oh_lo[s][:, :, :],
                   ALU.mult).then_inc(b_picked, 1)
                v.wait_ge(b_picked, g + 1)
                if nxt is not None:
                    source_onehots(nxt, s, b_oh_ready)
                reduce(pos_f[:, :], picked[:, :, :], axis=AX.X, op=ALU.add).then_inc(b_pos_f, 1)
                v.wait_ge(b_pos_f, g + 1)
                tt(pos[:, ds(g * K, K)], pos_f[:, :], rank_f[:, ds(g * K, K)], ALU.add).then_inc(pos_ready, 1)

            def bases(i, s, first, last):
                nxt = None if last else i * 2 + s + 1
                if s:
                    place(i, 0, nxt)
                elif not first:
                    place(i - 1, 1, nxt)
                else:
                    source_onehots(1, 1, b_oh_ready)

            v.wait_ge(rank_ready, NG)
            source_onehots(0, 0, b_oh_ready)
            over_chunks(v, bases, 0, 1, False)
            make_onehot(0, HALF, 0, False)
            add_sum(0, HALF - 1, 0)
            add_sum(0, HALF - 1, 1)
            add_sum(0, HALF, 0)
            add_far(0)
            over_chunks(v, bases, 1, 3, False)
            v.wait_ge(infoT, 3)
            link(copy(info_n[:, :, :], p_misc[:, 0:3 * 32].rearrange("p (k j) -> p k j", j=32)))
            link(tsc(has[:, :], info_n[:, 1, :], 0.0, None, ALU.is_gt))
            link(tt(nt1[:, :], info_n[:, 0, :], dump_f[:, :], ALU.subtract))
            link(tt(nt1[:, :], nt1[:, :], has[:, :], ALU.mult))
            tt(start_f[:, :], nt1[:, :], dump_f[:, :], ALU.add).then_inc(idx_ready, 1)
            v.wait_ge(idx_ready, 1)
            link(stt(nt1[:, :], info_n[:, 2, :], -float(R_ZERO), has[:, :], ALU.add, ALU.mult))
            link(tsc(last_idx[:, :], nt1[:, :], float(R_ZERO), None, ALU.add))
            link(tsc(nt1[:, :], info_n[:, 1, :], 1.0, None, ALU.max))
            nc.vector.reciprocal(rcnt[:, :], nt1[:, :]).then_inc(idx_ready, 1)
            over_chunks(v, bases, 3, HALF, True)
            place(HALF, 0, None)
            v.wait_ge(sums_ready[0], 1)
            link(tsc(acc[:, 1, :], acc[:, 1, :], 1.0, None, ALU.max))
            link(nc.vector.reciprocal(acc[:, 1, :], acc[:, 1, :]))

            def mean(q):
                return tt(g_m[:, :, :].rearrange("p j n -> p (j n)"), acc[:, 0, ds(q * (Q * P), Q * P)],
                          acc[:, 1, ds(q * (Q * P), Q * P)], ALU.mult)

            def z0(q, first):
                if not first:
                    v.wait_ge(z_mm[0], q)
                mean(q).then_inc(z_m, 1)
                v.wait_ge(z_mm[0], q + 1)
                tt(tmp[:, ds(q * Q, Q), :], p_aggs[:, 0:Q * D].rearrange("p (j f) -> p j f", j=Q),
                   b_all[:, 0:1, :].to_broadcast([P, Q, D]), ALU.add).then_inc(z_sum, 1)
                v.wait_ge(z_sum, q + 1)
                v.wait_ge(z_T[0], q + 1)
                tsc(h_sb[:, ds(q * Q, Q), :], tmp[:, ds(q * Q, Q), :], 0.0, None, ALU.max).then_inc(z_out[0], 1)

            over_groups(v, z0)
            nc.vector.memset(acc[:, 0, :], 0.0).then_inc(h_ready, 1)
            v.wait_ge(table_out[1], 32)

            def z1(q, first):
                v.wait_ge(z_mm[1], q + 1)
                tt(h_sb[:, ds(q * Q, Q), :], p_aggs[:, 0:Q * D].rearrange("p (j f) -> p j f", j=Q),
                   b_all[:, 1:2, :].to_broadcast([P, Q, D]), ALU.add).then_inc(z_out[1], 1)

            over_groups(v, z1)

            v.wait_ge(idx_ready, 2)
            v.wait_ge(summed[0][1], HALF)
            v.wait_ge(summed[0][0], HALF + 1)
            v.wait_ge(sums_ready[0], 1)

            def starts(q, first):
                n0 = q * 6

                def slink(n, ins):
                    ins.then_inc(start_step, 1)
                    v.wait_ge(start_step, n0 + n)

                if not first:
                    v.wait_ge(starts_found, q)
                    v.wait_ge(start_step, n0)
                at = start_f[:, ds(q * Q, Q)]
                slink(1, tt(begun, bc(at, P + 1), bounds[:, :].unsqueeze(1).to_broadcast([P, Q, P + 1]), ALU.is_ge))
                tt(start_p, begun[:, :, 0:P], begun[:, :, 1:P + 1], ALU.subtract).then_inc(start_onehots, 1)
                slink(2, reduce(start_in[:, 0, :], begun, axis=AX.X, op=ALU.add))
                slink(3, tsc(start_in[:, 0, :], start_in[:, 0, :], -1.0, float(TP), ALU.add, ALU.mult))
                slink(4, tt(start_in[:, 1, :], at, start_in[:, 0, :], ALU.subtract))
                tt(start_t, bc(start_in[:, 1, :], TP), iota_t[:, :].unsqueeze(1).to_broadcast([P, Q, TP]),
                   ALU.is_equal).then_inc(start_onehots, 1)
                v.wait_ge(starts_found, q + 1)
                if first:
                    copy(is_start[:, :], p_rank[:, 0:TP]).then_inc(start_step, 2)
                else:
                    tt(is_start[:, :], is_start[:, :], p_rank[:, 0:TP], ALU.add).then_inc(start_step, 2)

            over_groups(v, starts)
            v.wait_ge(start_step, NQ * 6)
            link(tsc(keep[:, 0, :], is_start[:, :], -2.0, 1.0, ALU.mult, ALU.add))
            link(tsc(keep[:, 0, :], keep[:, 0, :], FMAX, None, ALU.mult))
            link(tsc(keep[:, 1, :], is_start[:, :], -1.0, 1.0, ALU.mult, ALU.add))
            starts = is_start[:, :].rearrange("p (h t) -> p h t", h=2)
            offs = seg_t[:, :].rearrange("p (h t) -> p h t", h=2)
            link(tsc(tcol[:, :], tcol[:, :], -float(TH), None, ALU.add))
            link(tt(offs, tcol[:, :].unsqueeze(1).to_broadcast([P, 2, TH]), starts, ALU.mult))
            link(reduce(first_t[:, :], offs, axis=AX.X, op=ALU.min))
            link(tsc(first_t[:, :], first_t[:, :], float(TH), None, ALU.add))
            link(tsc(whole[:, :], first_t[:, :], float(TH), None, ALU.is_equal))
            link(tsc(fix_f[:, 0, :], first_t[:, :], 0.0, None, ALU.is_gt))
            link(tt(fix_f[:, 1, :], first_t[:, :], pdump[:, 2:4], ALU.add))
            link(tt(fix_f[:, 2, :], fix_f[:, 1, :], pdump[:, 0:2], ALU.subtract))
            link(tt(fix_f[:, 3, :], fix_f[:, 2, :], fix_f[:, 0, :], ALU.mult))
            tt(fix_idx[:, :], fix_f[:, 3, :], pdump[:, 0:2], ALU.add).then_inc(fix_idx_ready, 1)
            v.wait_ge(base_done, NG)
            link(nc.vector.memset(run_sb[1][:, :, KH - 1, 0:D], -FMAX))
            link(nc.vector.memset(run_sb[1][:, :, KH - 1, D:2 * D], 0.0))

            per = 2 * K
            keep_h = keep[:, :, :].rearrange("p c (h t) -> p c h t", h=2)

            def run(g, s, first):
                c0 = g * 2 + s
                for c in range(2):
                    copy(gate[s][:, c, :].rearrange("p (h k) -> p h k", h=2), keep_h[:, c, :, ds(c0 * KH, KH)]).then_inc(gate_ready, 1)
                v.wait_ge(sorted_in[s], (g + 1) * 16)
                if not first:
                    v.wait_ge(run_out[s], g * 16)
                v.wait_ge(gate_ready, c0 * 2 + 2)
                for k in range(KH):
                    old = run_sb[s][:, :, k - 1, :] if k else run_sb[1 - s][:, :, KH - 1, :]
                    for n in range(4):
                        c, h = divmod(n, 2)
                        o0, o1 = ((ALU.min, ALU.max), (ALU.mult, ALU.add))[c]
                        if n % 2 == 0 and (k or s or not first):
                            v.wait_ge(run_step, c0 * per + 4 * k + n - 2)
                        stt(run_sb[s][:, h, k, c * D:(c + 1) * D], old[:, h, c * D:(c + 1) * D],
                            gate[s][:, c, h * KH + k:h * KH + k + 1], sorted_sb[s][:, h, k, :], o0, o1).then_inc(run_step, 1)
                v.wait_ge(run_step, c0 * per + per)
                copy(gate[s][:, 0, 0:1], gate[s][:, 0, 1:2]).then_inc(run_done[s], 1)

            def scan_too(m, first):
                g, i = m * 3, m * 2
                run(g, 0, first)
                run(g, 1, first)
                add_before(1, i, 0, first)
                run(g + 1, 0, False)
                add_before(1, i, 1, first)
                run(g + 1, 1, False)
                run(g + 2, 0, False)
                add_before(1, i + 1, 0, False)
                run(g + 2, 1, False)
                add_before(1, i + 1, 1, False)

            def sums_only(i, s, first, last):
                make_onehot(1, i, s, first)
                add_before(1, i, s, first)

            over_groups(v, scan_too, SCANNED // 2)
            run(HALF, 0, False)
            tt(diag, ident[:, :].unsqueeze(1).to_broadcast([P, 2, P]), bc(whole[:, :], P), ALU.mult).then_inc(tails_ready, 1)
            copy(tail, run_sb[0][:, :, KH - 1, :]).then_inc(tails_ready, 1)
            add_before(1, SCANNED, 0, False)
            sums_only(SCANNED, 1, False, False)
            over_chunks(v, sums_only, SCANNED + 1, FIXED, False)
            v.wait_ge(tailsT, 1)
            whole_v = p_misc[:, 0:2 * P].rearrange("p (h n) -> p n h", h=2)
            link(tsc(whole_row[:, 0, :].rearrange("p (n h) -> p n h", h=2), whole_v, 2.0, -1.0, ALU.mult, ALU.add))
            link(tsc(whole_row[:, 0, :], whole_row[:, 0, :], FMAX, None, ALU.mult))
            link(copy(whole_row[:, 1, :].rearrange("p (n h) -> p n h", h=2), whole_v))
            for c in range(2):
                link(copy(tail_row[:, c, :].rearrange("p (n h) -> p n h", h=2),
                          p_eq[:, 2 * c * P:2 * (c + 1) * P].rearrange("p (h n) -> p n h", h=2)))
            nc.vector.memset(carry[:, 0, 0:1], -FMAX).then_inc(carry_ready, 1)
            nc.vector.memset(carry[:, 1, 0:1], 0.0).then_inc(carry_ready, 1)
            nc.vector.tensor_tensor_scan(carry[:, 0, 1:2 * P + 1], whole_row[:, 0, :], tail_row[:, 0, :], -FMAX, ALU.min, ALU.max).then_inc(carry_ready, 1)
            nc.vector.tensor_tensor_scan(carry[:, 1, 1:2 * P + 1], whole_row[:, 1, :], tail_row[:, 1, :], 0.0, ALU.mult, ALU.add).then_inc(carry_ready, 1)
            v.wait_ge(fix_in, 32)
            v.wait_ge(carry_back, 1)
            for h in range(2):
                tt(fixed[:, h, 0:D], fix_rows[:, h, 0:D], p_rank[:, 2 * h * P:(2 * h + 1) * P], ALU.max).then_inc(fixed_ready, 1)
                tt(fixed[:, h, D:2 * D], fix_rows[:, h, D:2 * D], p_rank[:, (2 * h + 1) * P:(2 * h + 2) * P], ALU.add).then_inc(fixed_ready, 1)
            over_chunks(v, sums_only, FIXED, HALF, True)
            add_sum(1, HALF, 0)
            add_far(1)
            v.wait_ge(sums_ready[1], 1)

            tlink = counted_links(v, t_step)

            def tail_norm_1(q, part):
                J = slice(q * Q, (q + 1) * Q)
                if part == 0:
                    v.wait_ge(t_z, q + 1)
                    tlink(tt(tmp[:, J, :], p_aggs[:, 0:Q * D].rearrange("p (j f) -> p j f", j=Q), h_sb[:, J, :], ALU.add))
                elif part == 1:
                    tlink(stt(x_sb[:, J, :], tmp[:, J, :], 0.0, x_sb[:, J, :], ALU.max, ALU.add))
                    tlink(reduce(stat[:, 0, J], x_sb[:, J, :], axis=AX.X, op=ALU.add))
                    tlink(tsc(stat[:, 0, J], stat[:, 0, J], 1.0 / D, None, ALU.mult))
                else:
                    tt(h_sb[:, J, :], x_sb[:, J, :], bc(stat[:, 0, J], D), ALU.subtract).then_inc(t_xc, 1)

            def tail_norm_2(q):
                J = slice(q * Q, (q + 1) * Q)
                v.wait_ge(t_sq, q + 1)
                tlink(reduce(stat[:, 1, J], tmp[:, J, :], axis=AX.X, op=ALU.add))
                tsc(stat[:, 1, J], stat[:, 1, J], 1.0 / D, EPS, ALU.mult, ALU.add).then_inc(t_var, 1)
                v.wait_ge(t_std, q + 1)
                tlink(nc.vector.reciprocal(stat[:, 3, J], stat[:, 2, J]))
                if q:
                    v.wait_ge(t_hT, q)
                    v.wait_ge(residual, 2 * q)
                v.wait_ge(t_xc, q + 1)
                stt(g_h[:, :, :], h_sb[:, J, :], 0.0, bc(stat[:, 3, J], D), ALU.max, ALU.mult).then_inc(t_h, 1)

            hid_bank = [p_rank, p_hT]

            def tail_add(n):
                q, t = divmod(n, Q)
                if t == 0:
                    v.wait_ge(hid_got[q % 2], 16 * (q // 2 + 1))
                v.wait_ge(t_hid, n + 1)
                if n >= 2:
                    v.wait_ge(t_y, n - 1)
                tt(hidT[n % 2], hid_bank[n % 2][:, :], hid_in[q % 2][:, t, :], ALU.add).then_inc(t_added, 1)

            def tail_out(q):
                v.wait_ge(t_y, Q * (q + 1))
                v.wait_ge(residual, 2 * q + 2)
                tlink(tt(h_sb[:, q * Q:q * Q + 4, :], p_pre[:, 0:4 * D].rearrange("p (j f) -> p j f", j=4),
                         x_sb[:, q * Q:q * Q + 4, :], ALU.add))
                tt(h_sb[:, q * Q + 4, :], p_misc[:, 0:D], x_sb[:, q * Q + 4, :], ALU.add).then_inc(y_ready, 1)

            mean(0).then_inc(t_m, 1)
            for part in range(3):
                tail_norm_1(0, part)
            tail_norm_2(0)
            for q in range(NQ):
                for t in range(Q):
                    tail_add(q * Q + t)
                    if t == 0 and q:
                        tail_out(q - 1)
                    if t < 3 and q + 1 < NQ:
                        tail_norm_1(q + 1, t)
                    if t == 3 and q + 1 < NQ:
                        tail_norm_2(q + 1)
            tail_out(NQ - 1)


_INS = ["x", "src", "dst", "edge_attr_128", "L0_gnn_W1", "L0_gnn_b1", "L0_gnn_W2", "L0_gnn_b2",
        "L1_gnn_u", "L1_gnn_W1", "L1_gnn_b1", "L1_gnn_W2", "L1_gnn_b2"]


def kernel(**inputs):
    import numpy as np
    import concourse.bacc as bacc
    from concourse import mybir as mb
    from concourse.bass_utils import run_bass_kernel_spmd

    nc = bacc.Bacc("TRN2", target_bir_lowering=False, num_devices=1)
    arrays, args = {}, []
    for name in _INS:
        a = np.ascontiguousarray(inputs[name])
        arrays[f"in_{name}"] = a
        args.append(nc.dram_tensor(f"in_{name}", a.shape, mb.dt.from_np(a.dtype), kind="ExternalInput").ap())
    args.append(nc.dram_tensor("out_x", (N_NODES, D), mb.dt.float32, kind="ExternalOutput").ap())
    f32, b16 = mb.dt.float32, mb.dt.bfloat16
    table = [nc.dram_tensor("table0", (N_NODES, 3 * D), b16).ap(), nc.dram_tensor("table1", (N_NODES, D), f32).ap()]
    sorted_rows = nc.dram_tensor("sorted_rows", (E_PAD, D), f32).ap()
    running = nc.dram_tensor("running", (R_ZERO + 1, 2 * D), f32).ap()
    node_scr = nc.dram_tensor("node_scr", (3, NH * NH), f32).ap()
    hid_scr = nc.dram_tensor("hid_scr", (NJ, P, HID), f32).ap()
    gnn(nc, *args, table, sorted_rows, running, node_scr, hid_scr)
    r = run_bass_kernel_spmd(nc, [arrays], core_ids=[0])
    return r.results[0]["out_x"]
```
